# Optimizing a Trainium2 kernel written in Bass

```python
import numpy as np
import jax
import jax.numpy as jnp

def _softmax(x, axis=-1):
    return jax.nn.softmax(x, axis=axis)

def _gelu(x):
    return jax.nn.gelu(x, approximate=True)

def _silu(x):
    return jax.nn.silu(x)

def _sigmoid(x):
    return jax.nn.sigmoid(x)

def _layernorm(x, axis=-1, eps=1e-05):
    m = jnp.mean(x, axis=axis, keepdims=True)
    v = jnp.var(x, axis=axis, keepdims=True)
    return (x - m) / jnp.sqrt(v + eps)

def _scatter_add(tgt, idx, src, axis=0):
    return tgt.at[idx].add(src)

def _segment_sum(src, seg, n):
    return jax.ops.segment_sum(src, seg, n)
kernel_name = 'mk_hybrid_d1_jaxref_r4_432eb4'

def setup_inputs(seed: int=0):
    np.random.seed(seed)
    _w = jnp.asarray

    def _L0_attn_a_setup():
        import jax, jax.numpy as jnp
        import numpy as np
        B, T, D = (4, 1024, 256)
        F = 4 * D
        EPS_INIT = -1e+30

        def layer_norm(x, w, b, eps=1e-05):
            mu = jnp.mean(x, axis=-1, keepdims=True)
            var = jnp.var(x, axis=-1, keepdims=True)
            return (x - mu) * jax.lax.rsqrt(var + eps) * w + b

        def time_shift(x):
            return jnp.concatenate([jnp.zeros_like(x[:, :1]), x[:, :-1]], axis=1)

        def wkv(w, u, k, v):
            bsz, _, dim = k.shape
            alpha0 = jnp.zeros((bsz, dim), k.dtype)
            beta0 = jnp.zeros((bsz, dim), k.dtype)
            eps0 = jnp.full((bsz, dim), EPS_INIT, k.dtype)

            def step(carry, kv_t):
                alpha, beta, eps = carry
                kt, vt = kv_t
                ukt = u + kt
                tau = jnp.maximum(ukt, eps)
                e1 = jnp.exp(eps - tau)
                e2 = jnp.exp(ukt - tau)
                out = (e1 * alpha + e2 * vt) / (e1 * beta + e2)
                weps = eps - w
                tau2 = jnp.maximum(weps, kt)
                d1 = jnp.exp(weps - tau2)
                d2 = jnp.exp(kt - tau2)
                return ((d1 * alpha + d2 * vt, d1 * beta + d2, tau2), out)
            kT = jnp.swapaxes(k, 0, 1)
            vT = jnp.swapaxes(v, 0, 1)
            _, outT = jax.lax.scan(step, (alpha0, beta0, eps0), (kT, vT))
            return jnp.swapaxes(outT, 0, 1)
        key = jax.random.key(seed)
        ks = jax.random.split(key, 20)
        n = lambda k, shape, s: jax.random.normal(k, shape, jnp.float32) * s
        u = lambda k, shape: jax.random.uniform(k, shape, jnp.float32)
        s = 0.02
        return {'x': jax.random.normal(ks[0], (B, T, D), jnp.float32), 'ln1_w': jnp.ones((D,), jnp.float32), 'ln1_b': jnp.zeros((D,), jnp.float32), 'ln2_w': jnp.ones((D,), jnp.float32), 'ln2_b': jnp.zeros((D,), jnp.float32), 'time_decay': n(ks[1], (D,), 0.5), 'time_first': n(ks[2], (D,), 0.5), 'time_mix_k': u(ks[3], (1, 1, D)), 'time_mix_v': u(ks[4], (1, 1, D)), 'time_mix_r': u(ks[5], (1, 1, D)), 'w_key': n(ks[6], (D, D), s), 'w_value': n(ks[7], (D, D), s), 'w_recept': n(ks[8], (D, D), s), 'w_output': n(ks[9], (D, D), s), 'f_time_mix_k': u(ks[10], (1, 1, D)), 'f_time_mix_r': u(ks[11], (1, 1, D)), 'f_w_key': n(ks[12], (D, F), s), 'f_w_recept': n(ks[13], (D, D), s), 'f_w_value': n(ks[14], (F, D), s)}
    _L0_attn_a_in = _L0_attn_a_setup()

    def _L0_attn_b_setup():
        import jax, jax.numpy as jnp
        import numpy as np
        EPS = 1e-06

        def _causal_depthwise_conv(x, conv_w, conv_b):
            B, L, d = x.shape
            lhs = jnp.transpose(x, (0, 2, 1))
            out = jax.lax.conv_general_dilated(lhs, conv_w, window_strides=(1,), padding=[(3, 0)], feature_group_count=d, dimension_numbers=('NCH', 'OIH', 'NCH'))
            out = out + conv_b[None, :, None]
            return jnp.transpose(out, (0, 2, 1))
        key = jax.random.key(seed)
        ks = jax.random.split(key, 8)
        B, L, d = (4, 1024, 256)
        x = jax.random.normal(ks[0], (B, L, d), dtype=jnp.float32)
        conv_w = jax.random.normal(ks[1], (d, 1, 4), dtype=jnp.float32) * 0.02
        conv_b = jnp.zeros((d,), dtype=jnp.float32)
        lim = 1.0 / np.sqrt(d)
        W_r = jax.random.uniform(ks[2], (d, d), jnp.float32, -lim, lim)
        b_r = jax.random.uniform(ks[3], (d,), jnp.float32, -lim, lim)
        W_i = jax.random.uniform(ks[4], (d, d), jnp.float32, -lim, lim)
        b_i = jax.random.uniform(ks[5], (d,), jnp.float32, -lim, lim)
        log_a = jnp.full((d,), 7.5, dtype=jnp.float32)
        W_out = jax.random.uniform(ks[6], (d, d), jnp.float32, -lim, lim)
        gamma = jnp.ones((d,), dtype=jnp.float32)
        return {'x': x, 'conv_w': conv_w, 'conv_b': conv_b, 'W_r': W_r, 'b_r': b_r, 'W_i': W_i, 'b_i': b_i, 'log_a': log_a, 'W_out': W_out, 'gamma': gamma}
    _L0_attn_b_in = _L0_attn_b_setup()

    def _L0_ffn_setup():
        import jax, jax.numpy as jnp
        import numpy as np
        SL, BS, HS, FF, E, TOPK = (512, 2, 256, 1024, 8, 2)
        key = jax.random.key(seed)
        ks = jax.random.split(key, 6)
        T = SL * BS
        x = jax.random.normal(ks[0], (SL, BS, HS), jnp.float32)
        scores = jax.random.uniform(ks[1], (T, E), jnp.float32)
        expert_weights = jax.random.uniform(ks[2], (T, TOPK), jnp.float32)
        expert_indices = jax.random.randint(ks[3], (T, TOPK), 0, E, jnp.int32)
        w1 = jax.random.normal(ks[4], (E, HS, FF), jnp.float32) * (1.0 / np.sqrt(HS))
        w2 = jax.random.normal(ks[5], (E, FF, HS), jnp.float32) * (1.0 / np.sqrt(FF))
        bias = jnp.zeros((HS,), jnp.float32)
        return dict(x=x, scores=scores, expert_weights=expert_weights, expert_indices=expert_indices, w1=w1, w2=w2, bias=bias)
    _L0_ffn_in = _L0_ffn_setup()
    _d = {'L0_attn_a_x': _L0_attn_a_in['x'], 'L0_attn_a_ln1_w': _L0_attn_a_in['ln1_w'], 'L0_attn_a_ln1_b': _L0_attn_a_in['ln1_b'], 'L0_attn_a_ln2_w': _L0_attn_a_in['ln2_w'], 'L0_attn_a_ln2_b': _L0_attn_a_in['ln2_b'], 'L0_attn_a_time_decay': _L0_attn_a_in['time_decay'], 'L0_attn_a_time_first': _L0_attn_a_in['time_first'], 'L0_attn_a_time_mix_k': _L0_attn_a_in['time_mix_k'], 'L0_attn_a_time_mix_v': _L0_attn_a_in['time_mix_v'], 'L0_attn_a_time_mix_r': _L0_attn_a_in['time_mix_r'], 'L0_attn_a_w_key': _L0_attn_a_in['w_key'], 'L0_attn_a_w_value': _L0_attn_a_in['w_value'], 'L0_attn_a_w_recept': _L0_attn_a_in['w_recept'], 'L0_attn_a_w_output': _L0_attn_a_in['w_output'], 'L0_attn_a_f_time_mix_k': _L0_attn_a_in['f_time_mix_k'], 'L0_attn_a_f_time_mix_r': _L0_attn_a_in['f_time_mix_r'], 'L0_attn_a_f_w_key': _L0_attn_a_in['f_w_key'], 'L0_attn_a_f_w_recept': _L0_attn_a_in['f_w_recept'], 'L0_attn_a_f_w_value': _L0_attn_a_in['f_w_value'], 'L0_attn_b_conv_w': _L0_attn_b_in['conv_w'], 'L0_attn_b_conv_b': _L0_attn_b_in['conv_b'], 'L0_attn_b_W_r': _L0_attn_b_in['W_r'], 'L0_attn_b_b_r': _L0_attn_b_in['b_r'], 'L0_attn_b_W_i': _L0_attn_b_in['W_i'], 'L0_attn_b_b_i': _L0_attn_b_in['b_i'], 'L0_attn_b_log_a': _L0_attn_b_in['log_a'], 'L0_attn_b_W_out': _L0_attn_b_in['W_out'], 'L0_attn_b_gamma': _L0_attn_b_in['gamma'], 'L0_ffn_scores': _L0_ffn_in['scores'], 'L0_ffn_expert_weights': _L0_ffn_in['expert_weights'], 'L0_ffn_expert_indices': _L0_ffn_in['expert_indices'], 'L0_ffn_w1': _L0_ffn_in['w1'], 'L0_ffn_w2': _L0_ffn_in['w2'], 'L0_ffn_bias': _L0_ffn_in['bias']}
    _x0 = _d['L0_attn_a_x']
    _d['L0_attn_a_x'] = jax.random.normal(jax.random.fold_in(jax.random.key(seed), 1), (16, 512, 256), dtype=_x0.dtype)
    del _x0
    return _d

def reference(L0_attn_a_x, L0_attn_a_ln1_w, L0_attn_a_ln1_b, L0_attn_a_ln2_w, L0_attn_a_ln2_b, L0_attn_a_time_decay, L0_attn_a_time_first, L0_attn_a_time_mix_k, L0_attn_a_time_mix_v, L0_attn_a_time_mix_r, L0_attn_a_w_key, L0_attn_a_w_value, L0_attn_a_w_recept, L0_attn_a_w_output, L0_attn_a_f_time_mix_k, L0_attn_a_f_time_mix_r, L0_attn_a_f_w_key, L0_attn_a_f_w_recept, L0_attn_a_f_w_value, L0_attn_b_conv_w, L0_attn_b_conv_b, L0_attn_b_W_r, L0_attn_b_b_r, L0_attn_b_W_i, L0_attn_b_b_i, L0_attn_b_log_a, L0_attn_b_W_out, L0_attn_b_gamma, L0_ffn_scores, L0_ffn_expert_weights, L0_ffn_expert_indices, L0_ffn_w1, L0_ffn_w2, L0_ffn_bias):

    def _L0_attn_a_ref(x, ln1_w, ln1_b, ln2_w, ln2_b, time_decay, time_first, time_mix_k, time_mix_v, time_mix_r, w_key, w_value, w_recept, w_output, f_time_mix_k, f_time_mix_r, f_w_key, f_w_recept, f_w_value):
        import jax, jax.numpy as jnp
        import numpy as np
        B, T, D = (4, 1024, 256)
        F = 4 * D
        EPS_INIT = -1e+30

        def layer_norm(x, w, b, eps=1e-05):
            mu = jnp.mean(x, axis=-1, keepdims=True)
            var = jnp.var(x, axis=-1, keepdims=True)
            return (x - mu) * jax.lax.rsqrt(var + eps) * w + b

        def time_shift(x):
            return jnp.concatenate([jnp.zeros_like(x[:, :1]), x[:, :-1]], axis=1)

        def wkv(w, u, k, v):
            bsz, _, dim = k.shape
            alpha0 = jnp.zeros((bsz, dim), k.dtype)
            beta0 = jnp.zeros((bsz, dim), k.dtype)
            eps0 = jnp.full((bsz, dim), EPS_INIT, k.dtype)

            def step(carry, kv_t):
                alpha, beta, eps = carry
                kt, vt = kv_t
                ukt = u + kt
                tau = jnp.maximum(ukt, eps)
                e1 = jnp.exp(eps - tau)
                e2 = jnp.exp(ukt - tau)
                out = (e1 * alpha + e2 * vt) / (e1 * beta + e2)
                weps = eps - w
                tau2 = jnp.maximum(weps, kt)
                d1 = jnp.exp(weps - tau2)
                d2 = jnp.exp(kt - tau2)
                return ((d1 * alpha + d2 * vt, d1 * beta + d2, tau2), out)
            kT = jnp.swapaxes(k, 0, 1)
            vT = jnp.swapaxes(v, 0, 1)
            _, outT = jax.lax.scan(step, (alpha0, beta0, eps0), (kT, vT))
            return jnp.swapaxes(outT, 0, 1)
        xn = layer_norm(x, ln1_w, ln1_b)
        lx = time_shift(xn)
        k = (xn * time_mix_k + lx * (1.0 - time_mix_k)) @ w_key
        v = (xn * time_mix_v + lx * (1.0 - time_mix_v)) @ w_value
        r = (xn * time_mix_r + lx * (1.0 - time_mix_r)) @ w_recept
        sr = jax.nn.sigmoid(r)
        w = jnp.exp(time_decay)
        out = wkv(w, time_first, k, v)
        x = x + out * sr @ w_output
        xn2 = layer_norm(x, ln2_w, ln2_b)
        lx2 = time_shift(xn2)
        fk = (xn2 * f_time_mix_k + lx2 * (1.0 - f_time_mix_k)) @ f_w_key
        fr = (xn2 * f_time_mix_r + lx2 * (1.0 - f_time_mix_r)) @ f_w_recept
        vk = jnp.square(jax.nn.relu(fk)) @ f_w_value
        x = x + jax.nn.sigmoid(fr) * vk
        return x

    def _L0_attn_b_ref(x, conv_w, conv_b, W_r, b_r, W_i, b_i, log_a, W_out, gamma):
        import jax, jax.numpy as jnp
        import numpy as np
        EPS = 1e-06

        def _causal_depthwise_conv(x, conv_w, conv_b):
            B, L, d = x.shape
            lhs = jnp.transpose(x, (0, 2, 1))
            out = jax.lax.conv_general_dilated(lhs, conv_w, window_strides=(1,), padding=[(3, 0)], feature_group_count=d, dimension_numbers=('NCH', 'OIH', 'NCH'))
            out = out + conv_b[None, :, None]
            return jnp.transpose(out, (0, 2, 1))
        B, L, d = x.shape
        x_conv = _causal_depthwise_conv(x, conv_w, conv_b)
        r_t = jax.nn.sigmoid(x_conv @ W_r.T + b_r)
        i_t = jax.nn.sigmoid(x_conv @ W_i.T + b_i)
        a_base = jax.nn.sigmoid(log_a)
        a_t = a_base[None, None, :] ** (8.0 * r_t)
        inp = i_t * x_conv
        scale = jnp.sqrt(jnp.clip(1.0 - a_t * a_t, 0.0))

        def step(h, ab):
            a, b = ab
            h = a * h + b
            return (h, h)
        xs = (jnp.moveaxis(a_t, 1, 0), jnp.moveaxis(scale * inp, 1, 0))
        h0 = jnp.zeros((B, d), dtype=x.dtype)
        _, hs = jax.lax.scan(step, h0, xs)
        out = jnp.moveaxis(hs, 0, 1)
        out = out @ W_out.T
        rms = jax.lax.rsqrt(jnp.mean(out * out, axis=-1, keepdims=True) + EPS)
        return out * rms * gamma

    def _L0_ffn_ref(x, scores, expert_weights, expert_indices, w1, w2, bias):
        import jax, jax.numpy as jnp
        import numpy as np
        SL, BS, HS, FF, E, TOPK = (512, 2, 256, 1024, 8, 2)
        sl, bs, hs = x.shape
        n_exp = w1.shape[0]
        top_k = expert_indices.shape[-1]
        xf = x.reshape(-1, hs)
        flat_idx = expert_indices.reshape(-1)
        flat_w = expert_weights.reshape(-1)
        order = jnp.argsort(flat_idx)
        tok = order // top_k
        tokens_per_expert = jnp.bincount(flat_idx, length=n_exp).astype(jnp.int32)
        xs = xf[tok]
        h = jax.nn.gelu(jax.lax.ragged_dot(xs, w1, tokens_per_expert), approximate=False)
        ys = jax.lax.ragged_dot(h, w2, tokens_per_expert)
        ys = ys * flat_w[order][:, None]
        out = jnp.zeros_like(xf).at[tok].add(ys)
        return out.reshape(sl, bs, hs) + bias
    x = L0_attn_a_x
    x = x + _L0_attn_a_ref(_layernorm(x, axis=-1), L0_attn_a_ln1_w, L0_attn_a_ln1_b, L0_attn_a_ln2_w, L0_attn_a_ln2_b, L0_attn_a_time_decay, L0_attn_a_time_first, L0_attn_a_time_mix_k, L0_attn_a_time_mix_v, L0_attn_a_time_mix_r, L0_attn_a_w_key, L0_attn_a_w_value, L0_attn_a_w_recept, L0_attn_a_w_output, L0_attn_a_f_time_mix_k, L0_attn_a_f_time_mix_r, L0_attn_a_f_w_key, L0_attn_a_f_w_recept, L0_attn_a_f_w_value)
    x = x + _L0_ffn_ref(_layernorm(x, axis=-1), L0_ffn_scores, L0_ffn_expert_weights, L0_ffn_expert_indices, L0_ffn_w1, L0_ffn_w2, L0_ffn_bias)
    x = x + _L0_attn_b_ref(_layernorm(x, axis=-1), L0_attn_b_conv_w, L0_attn_b_conv_b, L0_attn_b_W_r, L0_attn_b_b_r, L0_attn_b_W_i, L0_attn_b_b_i, L0_attn_b_log_a, L0_attn_b_W_out, L0_attn_b_gamma)
    x = x + _L0_ffn_ref(_layernorm(x, axis=-1), L0_ffn_scores, L0_ffn_expert_weights, L0_ffn_expert_indices, L0_ffn_w1, L0_ffn_w2, L0_ffn_bias)
    return x

_drawn_inputs = setup_inputs


def setup_inputs(seed=0):
    import zlib

    import numpy as np

    out = dict(_drawn_inputs(seed))
    spreads = {'L0_attn_a_ln1_w': (1.0, 0.6),
     'L0_attn_a_ln1_b': (0.0, 0.8),
     'L0_attn_a_ln2_w': (1.0, 0.6),
     'L0_attn_a_ln2_b': (0.0, 0.8),
     'L0_attn_b_conv_b': (0.0, 0.8),
     'L0_attn_b_log_a': (7.5, 0.6),
     'L0_attn_b_gamma': (1.0, 0.6),
     'L0_ffn_bias': (0.0, 0.8)}
    factors = {'L0_attn_a_time_decay': 8.0,
     'L0_attn_a_time_first': 8.0,
     'L0_attn_a_time_mix_k': 8.0,
     'L0_attn_a_time_mix_v': 8.0,
     'L0_attn_a_time_mix_r': 8.0,
     'L0_attn_a_w_key': 8.0,
     'L0_attn_a_w_value': 4.358,
     'L0_attn_a_w_recept': 8.0,
     'L0_attn_a_w_output': 4.331,
     'L0_attn_a_f_time_mix_k': 7.747,
     'L0_attn_a_f_time_mix_r': 8.0,
     'L0_attn_a_f_w_key': 4.675,
     'L0_attn_a_f_w_recept': 8.0,
     'L0_attn_a_f_w_value': 4.218,
     'L0_attn_b_W_r': 64.0,
     'L0_attn_b_b_r': 64.0,
     'L0_attn_b_W_i': 37.104,
     'L0_attn_b_b_i': 51.928,
     'L0_attn_b_conv_w': 8.0,
     'L0_attn_b_W_out': 8.0,
     'L0_ffn_expert_weights': 8.0,
     'L0_ffn_w1': 8.0,
     'L0_ffn_w2': 8.0}
    for name, (base, spread) in spreads.items():
        noise = np.random.default_rng([zlib.crc32(name.encode()), seed]).standard_normal(out[name].shape)
        drawn = base * np.exp(spread * noise) if base else spread * noise
        out[name] = jnp.asarray(drawn.astype(out[name].dtype))
    for name, factor in factors.items():
        out[name] = (out[name] * factor).astype(out[name].dtype)
    return out
```

```python
import concourse.bass as bass
from concourse import mybir
from contextlib import ExitStack

F32 = mybir.dt.float32
I32 = mybir.dt.int32
ALU = mybir.AluOpType
ACT = mybir.ActivationFunctionType

B, T, D = 16, 512, 256
P = 128
DC = D // P
TC = T // P
FF = 1024
FC = FF // P
E, TOPK = 8, 2
NB = 2
NTOK = NB * T
NASG = NTOK * TOPK
NCH = NTOK // P
NT = NASG // P + E - 1
EPS = 1e-5
EPS_RMS = 1e-6
LOGIT_CAP = 40.0
TINY = 2.0 ** -60
FIRST, LAST = 5, 13

LOG_TERMS = range(15, 1, -2)
LOG_STEPS = 6 + len(LOG_TERMS) - 1 + 3

VECS = ["ln1_w", "ln1_b", "ln2_w", "ln2_b", "decay", "first", "mix_k", "mix_v", "mix_r", "fmix_k", "fmix_r",
        "conv_b", "b_r", "b_i", "log_a", "conv0", "conv1", "conv2", "conv3"]
COL = {name: DC * n for n, name in enumerate(VECS)}


class Steps:

    def __init__(self, sem, names, runs):
        self.sem, self.names, self.runs = sem, names, runs

    def count(self, run, name):
        return run * len(self.names) + self.names.index(name) + 1


def await_step(eng, steps, run, name):
    if isinstance(run, int):
        if run < 0:
            return
        run = min(run, steps.runs - 1)
    eng.wait_ge(steps.sem, steps.count(run, name))


def numbered(name, n):
    return [f"{name}{k}" for k in range(n)]


def hybrid_kernel(nc, x, vecs, bias_row, gamma_row, w_key, w_value, w_recept, w_output, f_w_key, f_w_recept,
                  f_w_value, w_r_t, w_i_t, w_out_t, expert_weights, expert_indices, w1, w2, out):
    ctx = ExitStack()
    with ctx:
        def sb(name, shape, dt=F32):
            return ctx.enter_context(nc.sbuf_tensor(name, shape, dt))

        def sem(name):
            return ctx.enter_context(nc.semaphore(name))

        def steps(name, names, runs):
            return Steps(sem(name), names, runs)

        ident = sb("ident", [P, P])
        zeros = sb("zeros", [P, D])
        half_neg = sb("half_neg", [P, 8])
        vec = sb("vec", [P, DC * len(VECS)])
        decay = sb("decay", [P, DC])
        log_a8 = sb("log_a8", [P, DC])
        euler = sb("euler", [P, DC])
        la = [sb(f"la{n}", [P, DC]) for n in range(4)]
        gamma = sb("gamma", [P, D])
        bias = sb("bias", [P, D])
        wk = sb("wk", [P, DC, D])
        wv = sb("wv", [P, DC, D])
        wr = sb("wr", [P, DC, D])
        wo = sb("wo", [P, DC, D])
        fwk = sb("fwk", [P, DC, FF])
        fwr = sb("fwr", [P, DC, D])
        fwv = sb("fwv", [P, FC, D])
        gwr = sb("gwr", [P, DC, D])
        gwi = sb("gwi", [P, DC, D])
        gwo = sb("gwo", [P, DC, D])

        x_in = sb("x_in", [P, TC, D])
        y = sb("y", [P, TC, D])
        xb = sb("xb", [P, TC, D])
        z = y
        xz = sb("xz", [P, TC, D])
        x2 = sb("x2", [P, TC, D])
        x2b = sb("x2b", [P, TC, D])
        xhat = [sb(f"xhat{n}", [P, TC, D]) for n in range(2)]
        xhat.append(xhat[0])
        stats = [sb(f"stats{n}", [P, 2 * TC, 6]) for n in range(3)]
        moments = [sb(f"moments{n}", [P, 2 * TC, 2]) for n in range(3)]
        negmean = [sb(f"negmean{n}", [P, 2 * TC]) for n in range(3)]
        varis = [sb(f"varis{n}", [P, 2 * TC]) for n in range(3)]
        rstd = [sb(f"rstd{n}", [P, 2 * TC]) for n in range(3)]

        xn1 = sb("xn1", [P, DC, T + 1])
        xn2 = sb("xn2", [P, DC, T + 1])
        xk = sb("xk", [P, DC, T])
        xv = sb("xv", [P, DC, T])
        xr = sb("xr", [P, DC, T])
        xfk = sb("xfk", [P, DC, T])
        xfr = sb("xfr", [P, DC, T])
        kc = sb("kc", [P, DC, T])
        vc = sb("vc", [P, DC, T])
        sr = sb("sr", [P, DC, T])
        top = sb("top", [P, DC, T + 1])
        dec = sb("dec", [P, 2, DC, T])
        diff = dec[:, 0]
        dv = dec[:, 1]
        num = dec[:, 0]
        g = sb("g", [P, DC, T])
        alpha = sb("alpha", [P, DC, T + 1])
        beta = sb("beta", [P, DC, T + 1])
        gv = sb("gv", [P, DC, T])
        den = kc
        mixed = sr
        hid = sb("hid", [P, FC, T])
        sf = sb("sf", [P, TC, D])

        space = sb("space", [P, DC * (T + 3) + 7 * DC * T])
        place = [0]

        def carve(*shape):
            n = shape[0] * shape[1]
            part = space[:, place[0]:place[0] + n].rearrange("p (a b) -> p a b", a=shape[0])
            place[0] += n
            return part

        xc = carve(DC, T + 3)
        cv = carve(DC, T)
        rg = carve(DC, T)
        ig = carve(DC, T)
        aa = carve(DC, T)
        om = carve(DC, T)
        hs = carve(DC, T)
        fo = carve(TC, D)
        SET = DC * FF + FC * D
        ew = space[:, 0:2 * SET].rearrange("p (s n) -> p s n", s=2)
        square = sb("square", [P, D])
        ssq = sb("ssq", [P, TC])
        msq = sb("msq", [P, TC])
        rms = sb("rms", [P, TC])

        xf = sb("xf", [P, NCH, D])
        choice_w = sb("choice_w", [P, NCH, TOPK])
        slot_i = sb("slot_i", [P, NCH * TOPK], I32)
        token_id = sb("token_id", [P, NCH], I32)
        token_of_slot = sb("token_of_slot", [P, NT], I32)
        token_idx = sb("token_idx", [P, 1], I32)
        slot_idx = sb("slot_idx", [P, 1], I32)
        table = sb("table", [1, NT + E], I32)
        xs = sb("xs", [P, D])
        xst = sb("xst", [P, DC, P])
        ys = sb("ys", [P, D])
        hb = dec[:, 1]
        hbt = dec[:, 0].rearrange("p a (b n) -> p (a b) n", n=P)
        xfn = hid[:, 0:4, :].rearrange("p a (b n) -> p (a b) n", n=D)
        picked = sb("picked", [P, TOPK, D])

        psum = ctx.enter_context(nc.psum_tensor("psum", [P, 8, T], F32))
        bank_t = psum[:, 0:DC, :]
        ring = [psum[:, 2 + n, :] for n in range(4)]
        ring_rows = psum[:, 4:6, :]
        rows_out = psum[:, 6:8, :]
        rows4 = psum[:, 6:8, :].rearrange("p a (b n) -> p (a b) n", n=D)
        fr4 = psum[:, 4:6, :].rearrange("p a (b n) -> p (a b) n", n=D)

        rank = hid[0:E, 0:4, :].rearrange("p a t -> p (a t)")
        onehot = hid[0:E, 4:8, :].rearrange("p a t -> p (a t)")
        asg_i = onehot.bitcast(I32)
        ones_e = sb("ones_e", [E, NT])
        before = sb("before", [E, E])
        upto = sb("upto", [E, E])
        expert_id = sb("expert_id", [E, 1])
        tile_no = sb("tile_no", [E, NT])
        past = sb("past", [E, NT])
        ntiles = sb("ntiles", [E, 1])
        ntiles_i = sb("ntiles_i", [E, 2], I32)
        ends = sb("ends", [E, 1])
        starts = sb("starts", [E, 1])

        token_table = nc.dram_tensor("token_table", (NT * P, 1), I32, kind="Internal").ap()
        xf_rows = nc.dram_tensor("xf_rows", (NTOK, D), F32, kind="Internal").ap()
        ys_rows = nc.dram_tensor("ys_rows", (NT * P, D), F32, kind="Internal").ap()

        x_loaded = sem("x_loaded")
        passed = sem("passed")
        consts_loaded = sem("consts_loaded")
        consts_made = sem("consts_made")
        cols_made = sem("cols_made")
        weights_loaded = sem("weights_loaded")
        vec_made = sem("vec_made")
        log_steps = sem("log_steps")
        exp_made = sem("exp_made")
        out_stored = sem("out_stored")
        tr_in = steps("tr_in", ["t"], B)
        tr_mid = steps("tr_mid", ["t"], B)
        tr_rec = steps("tr_rec", ["t"], B)
        ln1 = steps("ln1", numbered("st", TC) + numbered("ag", TC) + ["neg", "v0", "v1"], B)
        ln2 = steps("ln2", numbered("st", TC) + numbered("ag", TC) + ["neg", "v0"], B)
        ln3 = steps("ln3", numbered("st", TC) + numbered("ag", TC) + ["neg", "v0"], B)
        hat1 = steps("hat1", ["pow"] + numbered("h", TC), B)
        hat2 = steps("hat2", ["pow"] + numbered("h", TC), B)
        hat3 = steps("hat3", ["pow"] + numbered("h", TC), B)
        keep_y = steps("keep_y", numbered("y", TC) + ["xb"], B)
        keep_xz = steps("keep_xz", ["xz"], B)
        keep_x2 = steps("keep_x2", ["x2b"], B)
        ev1 = steps("ev1", numbered("e", DC), B)
        ev2 = steps("ev2", numbered("e", DC), B)
        ev3 = steps("ev3", numbered("x", DC) + numbered("c", DC), B)
        mix1 = steps("mix1", ["d"] + numbered("k", DC) + numbered("v", DC) + numbered("r", DC), B)
        mix2 = steps("mix2", ["d"] + numbered("k", DC) + numbered("r", DC), B)
        kvr = steps("kvr", numbered("k", DC) + numbered("v", DC) + numbered("r", DC), B)
        kvr_out = steps("kvr_out", numbered("k", DC) + numbered("v", DC) + numbered("r", DC), B)
        wkv = steps("wkv", ["m0", "m1", "q0", "q1", "cap", "z0", "z1", "in", "b0", "b1", "dv", "a0", "a1",
                            "num", "den", "gate", "out"], B)
        wkv_act = steps("wkv_act", ["g", "dec", "ln", "inv"], B)
        wkv_gv = steps("wkv_gv", ["gv"], B)
        proj = steps("proj", ["o"], B)
        zsum = steps("zsum", ["z"], B)
        fk = steps("fk", numbered("f", FC), B)
        relu = steps("relu", numbered("f", FC), B)
        sq = steps("sq", numbered("f", FC), B)
        fr = steps("fr", ["f"], B)
        fr_out = steps("fr_out", ["s"], B)
        fv = steps("fv", ["v"], B)
        comb = steps("comb", ["g", "x"], B)
        conv = steps("conv", [f"c{j}{c}" for j in (2, 1, 0) for c in range(DC)], B)
        gates = steps("gates", numbered("r", DC) + numbered("i", DC), B)
        gates_out = steps("gates_out", numbered("r", DC) + numbered("i", DC) + numbered("a", DC) + ["ln", "sc"], B)
        rec = steps("rec", ["na", "om", "in", "b", "h0", "h1"], B)
        rproj = steps("rproj", ["o"], B)
        sumsq = steps("sumsq", numbered("s", TC), B)
        fin = steps("fin", ["ms"] + numbered("f", TC) + ["o"], B)
        fin_pow = steps("fin_pow", ["p"], B)

        route = steps("route", ["idx", "one", "rank", "n", "nf", "ni", "start", "end", "tab0", "pos", "past", "tab1",
                                "slot"], 1)
        route_pe = steps("route_pe", ["ends", "slots", "experts"], 1)
        idx_loaded = sem("idx_loaded")
        table_zeroed = sem("table_zeroed")
        table_written = sem("table_written")
        table_loaded = sem("table_loaded")
        lnf = steps("lnf", numbered("st", NCH) + numbered("ag", NCH) + ["neg", "v0"], 2)
        hatf = steps("hatf", ["pow"] + numbered("h", NCH), 2)
        xf_stored = sem("xf_stored")
        expert_loaded = [sem(f"expert_loaded{n}") for n in range(2)]
        expert_ready = sem("expert_ready")
        gathered = sem("gathered")
        idx_copied = sem("idx_copied")
        xs_t = sem("xs_t")
        xst_ready = sem("xst_ready")
        up_done = sem("up_done")
        gelu_done = sem("gelu_done")
        hid_t = sem("hid_t")
        hidt_ready = sem("hidt_ready")
        tiles_done = sem("tiles_done")
        y_out = sem("y_out")
        y_stored = sem("y_stored")
        picks = [sem(f"picks{k}") for k in range(TOPK)]
        slot_copied = sem("slot_copied")
        merged = steps("merged", [f"{n}{c}" for c in range(NCH) for n in ("b", "p", "q")], 2)

        block = ctx.enter_context(nc.Block())

        def wide(ap, n):
            return ap[:].unsqueeze(1).to_broadcast([P, n, D])

        def col(name, c):
            return vec[:, COL[name] + c:COL[name] + c + 1]

        def seq(i):
            return i - NB

        def turns(eng, turn, experts):
            for i in range(-1, 3):
                turn(i)
            experts(0)
            for i in range(3, FIRST):
                turn(i)
            with eng.Fori(FIRST, LAST + 1) as i:
                turn(i)
            for i in range(LAST + 1, B + 4):
                turn(i)
            experts(1)

        def has(i, shift, low, high):
            return not isinstance(i, int) or low <= i + shift <= high

        def at(i, n):
            return isinstance(i, int) and i == n

        def await_apart(eng, semaphore, value):
            eng.wait_ge(semaphore, value)
            eng.sem_inc(passed, 1)

        @block.sync
        def _(sp):
            def load_x(b):
                await_step(sp, ln1, b - 1, "st3")
                await_step(sp, keep_y, b - 1, "xb")
                src = x[b] if isinstance(b, int) else x[bass.DynSlice(b, 1)].rearrange("a t d -> (a t) d")
                sp.dma_start(x_in[:], src.rearrange("(c p) d -> p c d", p=P)).then_inc(x_loaded, 16)

            sp.dma_start(vec[:], vecs).then_inc(consts_loaded, 16)
            load_x(0)
            sp.dma_start(asg_i[:], expert_indices.rearrange("n k -> (n k)").partition_broadcast(E)).then_inc(idx_loaded, 16)
            for dst, src in ((wk, w_key), (wv, w_value), (wr, w_recept), (wo, w_output), (fwk, f_w_key),
                             (fwr, f_w_recept), (fwv, f_w_value), (gwr, w_r_t), (gwi, w_i_t), (gwo, w_out_t)):
                sp.dma_start(dst[:], src.rearrange("(c p) n -> p c n", p=P)).then_inc(weights_loaded, 16)
            sp.dma_start(bias[:], bias_row.partition_broadcast(P)).then_inc(weights_loaded, 16)
            sp.dma_start(gamma[:], gamma_row.partition_broadcast(P)).then_inc(weights_loaded, 16)
            sp.dma_start(choice_w[:], expert_weights.rearrange("(c p) k -> p c k", p=P)).then_inc(weights_loaded, 16)

            sp.wait_ge(consts_made, 8)
            sp.dma_start(token_table.rearrange("(p t) a -> p (t a)", p=P),
                         zeros[:, 0:NT].bitcast(I32)).then_inc(table_zeroed, 16)

            def load_expert(e):
                half = ew[:, e % 2, :]
                sp.dma_start(half[:, 0:DC * FF].rearrange("p (c n) -> p c n", c=DC),
                             w1[e].rearrange("(c p) n -> p c n", p=P)).then_inc(expert_loaded[0], 16)
                sp.dma_start(half[:, DC * FF:SET].rearrange("p (c n) -> p c n", c=FC),
                             w2[e].rearrange("(c p) n -> p c n", p=P)).then_inc(expert_loaded[1], 16)

            def announce_expert(f, e):
                for loaded in expert_loaded:
                    sp.wait_ge(loaded, 16 * (f * E + e + 1))
                sp.sem_inc(expert_ready, 1)

            def turn(i):
                if has(i, 2, 1, B - 1):
                    load_x(i + 2)
                if has(i, -2, NB, B - 1):
                    s = seq(i - 2)
                    await_step(sp, fin, s, "o")
                    dst = out[i - 2] if isinstance(i, int) else out[bass.DynSlice(i - 2, 1)].rearrange("a t d -> (a t) d")
                    sp.dma_start(dst.rearrange("(c p) d -> p c d", p=P), fo[:]).then_inc(out_stored, 16)

            def experts(f):
                if f:
                    await_step(sp, rec, B - 1, "h1")
                load_expert(0)
                announce_expert(f, 0)
                if f == 0:
                    sp.wait_ge(table_written, 16 * NCH * TOPK)
                    sp.dma_start(token_of_slot[:], token_table.rearrange("(t p) a -> p (t a)", p=P),
                                 allow_slow_non_contiguous=True).then_inc(table_loaded, 16)
                await_step(sp, hatf, f, f"h{NCH - 1}")
                sp.dma_start(xf_rows.rearrange("(c p) d -> p c d", p=P), xfn).then_inc(xf_stored, 16)
                if f:
                    await_step(sp, fin, B - 1, "o")
                load_expert(1)
                announce_expert(f, 1)
                if f == 0:
                    await_step(sp, route, 0, "tab1")
                for e in range(2, E):
                    last = sp.value_load(table[0:1, NT + e - 2:NT + e - 1], min_val=0, max_val=NT)
                    sp.wait_ge(tiles_done, last + (1 + f * NT))
                    load_expert(e)
                    announce_expert(f, e)
                if f:
                    await_step(sp, merged, 1, f"q{NCH - 1}")
                    sp.dma_start(out[0:NB].rearrange("a (c p) d -> p (a c) d", p=P), xf[:]).then_inc(out_stored, 16)
                    sp.wait_ge(out_stored, 16 * (B - NB + 1))

            turns(sp, turn, experts)

        @block.gpsimd
        def _(pool):
            pool.memset(ident[:], 0.0).then_inc(consts_made, 1)
            pool.memset(zeros[:], 0.0).then_inc(consts_made, 1)
            pool.memset(half_neg[:], -0.5).then_inc(consts_made, 1)
            pool.memset(ones_e[:], 1.0).then_inc(consts_made, 1)
            pool.memset(before[:], 1.0).then_inc(consts_made, 1)
            pool.memset(upto[:], 1.0).then_inc(consts_made, 1)
            pool.iota(token_id[:], pattern=[[P, NCH]], base=0, channel_multiplier=1).then_inc(consts_made, 1)
            pool.wait_ge(consts_made, 7)
            pool.affine_select(out=ident[:], in_=ident[:], compare_op=ALU.not_equal, fill=1.0, base=0,
                               pattern=[[-1, P]], channel_multiplier=1).then_inc(consts_made, 1)
            pool.affine_select(out=before[:], in_=before[:], compare_op=ALU.is_gt, fill=0.0, base=0,
                               pattern=[[1, E]], channel_multiplier=-1).then_inc(consts_made, 1)
            pool.affine_select(out=upto[:], in_=upto[:], compare_op=ALU.is_ge, fill=0.0, base=0,
                               pattern=[[1, E]], channel_multiplier=-1).then_inc(consts_made, 1)
            pool.iota(expert_id[:], pattern=[[0, 1]], base=0, channel_multiplier=1,
                      allow_small_or_imprecise_dtypes=True).then_inc(consts_made, 1)
            pool.iota(tile_no[:], pattern=[[1, NT]], base=0, channel_multiplier=0,
                      allow_small_or_imprecise_dtypes=True).then_inc(consts_made, 1)
            pool.memset(euler[:], 2.718281828459045).then_inc(consts_made, 1)
            pool.wait_ge(log_steps, 1)
            pool.wait_ge(consts_made, 13)
            pool.tensor_tensor(la[0][:], euler[:], la[3][:], ALU.pow).then_inc(exp_made, 1)
            pool.sem_inc(tiles_done, 1)
            pool.sem_inc(y_out, 1)
            pool.sem_inc(y_stored, 16)

            def power(dst, src, done):
                pool.tensor_tensor(dst, src, half_neg[:, 0:src.shape[1]], ALU.pow).then_inc(done, 1)

            def scale_rows(dst, src, n, col0, st, b, name):
                for c in range(dst.shape[1]):
                    pool.tensor_scalar(dst[:, c, :], src[:, c, :], negmean[n][:, c:c + 1],
                                       rstd[n][:, col0 + c:col0 + c + 1], ALU.add, ALU.mult).then_inc(st.sem, 1)

            def norm1(b):
                await_step(pool, ln1, b, "v1")
                await_step(pool, keep_y, b - 1, "xb")
                power(rstd[0][:], varis[0][:], hat1.sem)
                await_step(pool, tr_in, b - 1, "t")
                await_apart(pool, hat1.sem, hat1.count(b, "pow"))
                scale_rows(xhat[0], x_in, 0, TC, hat1, b, "h")

            def keep1(b):
                await_step(pool, zsum, b - 1, "z")
                await_step(pool, keep_xz, b - 1, "xz")
                await_step(pool, hat2, b - 1, f"h{TC - 1}")
                await_apart(pool, hat1.sem, hat1.count(b, "pow"))
                scale_rows(y, x_in, 0, 0, keep_y, b, "y")
                await_step(pool, keep_xz, b - 1, "xz")
                first = isinstance(b, int) and b < NB
                pool.tensor_tensor(xb[:], x_in[:], wide(zeros if first else bias, TC), ALU.add).then_inc(keep_y.sem, 1)

            def norm2(b):
                await_step(pool, ln2, b, "v0")
                await_step(pool, hat2, b - 1, f"h{TC - 1}")
                power(rstd[1][:, 0:TC], varis[1][:, 0:TC], hat2.sem)
                await_step(pool, tr_mid, b - 1, "t")
                await_apart(pool, hat2.sem, hat2.count(b, "pow"))
                scale_rows(xhat[1], z, 1, 0, hat2, b, "h")

            def keep2(b):
                await_step(pool, zsum, b, "z")
                await_step(pool, keep_y, b, "xb")
                await_step(pool, comb, b - 1, "x")
                pool.tensor_tensor(xz[:], xb[:], z[:], ALU.add).then_inc(keep_xz.sem, 1)

            def source3(i):
                return xf[:, TC * (i - B):TC * (i - B + 1), :] if isinstance(i, int) and i >= B else x2[:]

            def norm3(i):
                s = seq(i)
                await_step(pool, ln3, s, "v0")
                await_step(pool, hat3, s - 1, f"h{TC - 1}")
                power(rstd[2][:, 0:TC], varis[2][:, 0:TC], hat3.sem)
                await_step(pool, tr_rec, s - 1, "t")
                await_apart(pool, hat3.sem, hat3.count(s, "pow"))
                scale_rows(xhat[2], source3(i), 2, 0, hat3, s, "h")

            def keep3(i):
                s = seq(i)
                if isinstance(i, int) and i >= B:
                    await_step(pool, merged, 0, f"q{NCH - 1}")
                else:
                    await_step(pool, comb, i, "x")
                await_step(pool, fin, s - 1, "o")
                first = isinstance(i, int) and i >= B
                pool.tensor_tensor(x2b[:], source3(i), wide(zeros if first else bias, TC), ALU.add).then_inc(keep_x2.sem, 1)

            def turn(i):
                if has(i, 0, 0, B - 1):
                    await_step(pool, wkv_act, i, "g")
                    await_step(pool, kvr_out, i, "v1")
                    await_step(pool, wkv, i - 1, "num")
                    pool.tensor_tensor(gv[:], g[:], vc[:], ALU.mult).then_inc(wkv_gv.sem, 1)
                if has(i, -1, 0, B - 1):
                    for j in range(FC):
                        await_step(pool, relu, i - 1, f"f{j}")
                        pool.tensor_tensor(hid[:, j, :], hid[:, j, :], hid[:, j, :], ALU.mult).then_inc(sq.sem, 1)
                if has(i, 1, 0, B - 1):
                    norm1(i + 1)
                if has(i, -2, NB, B + NB - 1):
                    keep3(i - 2)
                if has(i, 0, 0, B - 1):
                    norm2(i)
                if has(i, -1, NB, B + NB - 1):
                    norm3(i - 1)
                if has(i, -2, NB, B + NB - 1):
                    await_step(pool, fin, seq(i - 2), "ms")
                    power(rms[:], msq[:], fin_pow.sem)
                if has(i, 0, 0, B - 1):
                    keep2(i)
                if has(i, 1, 0, B - 1):
                    if at(i, -1):
                        pool.wait_ge(weights_loaded, 13 * 16)
                    keep1(i + 1)
                if at(i, 1):
                    await_step(pool, route, 0, "slot")
                    pool.wait_ge(table_zeroed, 16)
                    for c in range(NCH):
                        for k in range(TOPK):
                            n = c * TOPK + k
                            pool.indirect_dma_start(
                                out=token_table, out_offset=bass.IndirectOffsetOnAxis(ap=slot_i[:, n:n + 1], axis=0),
                                in_=token_id[:, c:c + 1], in_offset=None).then_inc(table_written, 16)

            def experts(f):
                await_step(pool, lnf, f, "v0")
                power(rstd[0][:, 0:NCH], varis[0][:, 0:NCH], hatf.sem)
                await_step(pool, hatf, f, "pow")
                if f == 0:
                    await_step(pool, fv, 1, "v")
                else:
                    await_step(pool, fv, B - 1, "v")
                scale_rows(xfn, xf, 0, 0, hatf, f, "h")
                if f == 0:
                    pool.wait_ge(table_loaded, 16)
                pool.wait_ge(xf_stored, 16 * (f + 1))

                def gather(t, n):
                    src = token_of_slot[:, bass.DynSlice(t, 1)]
                    pool.tensor_copy(token_idx[:], src).then_inc(idx_copied, 1)
                    await_apart(pool, idx_copied, n + 1)
                    pool.indirect_dma_start(out=xs[:], out_offset=None, in_=xf_rows,
                                            in_offset=bass.IndirectOffsetOnAxis(ap=token_idx[:, 0:1], axis=0)).then_inc(gathered, 16)

                if f:
                    pool.wait_ge(xs_t, NT)
                gather(0, f * NT)
                with pool.Fori(1, NT) as t:
                    pool.wait_ge(xs_t, t + f * NT)
                    gather(t, t + f * NT)
                pool.wait_ge(y_stored, 16 * (NT * (f + 1) + 1))
                for c in range(NCH):
                    if c or f:
                        pool.wait_ge(merged.sem, f * 3 * NCH + 3 * c)
                    for k in range(TOPK):
                        n = c * TOPK + k
                        pool.indirect_dma_start(
                            out=picked[:, k, :], out_offset=None, in_=ys_rows,
                            in_offset=bass.IndirectOffsetOnAxis(ap=slot_i[:, n:n + 1], axis=0)).then_inc(picks[k], 16)

            turns(pool, turn, experts)

        @block.scalar
        def _(act):
            act.wait_ge(consts_loaded, 16)
            LOG_EXP = "natural_log_exp_and_others"
            nc.scalar.preload_act_table_set(LOG_EXP)
            nc.scalar.activation(decay[:], vec[:, COL["decay"]:COL["decay"] + DC], ACT.Exp).then_inc(vec_made, 1)
            act.wait_ge(vec_made, 1)
            nc.scalar.mul(decay[:], decay[:], -1.0).then_inc(vec_made, 1)
            act.wait_ge(cols_made, 5)
            act.wait_ge(log_steps, LOG_STEPS)

            def norm_out(dst, w, b, ev):
                for c in range(DC):
                    nc.scalar.activation(dst[:, c, 1:T + 1], bank_t[:, c, :], ACT.Identity, bias=col(b, c),
                                         scale=col(w, c)).then_inc(ev.sem, 1)

            def keys(b):
                await_step(act, wkv, b - 1, "out")
                for n, (name, dst) in enumerate((("k", kc), ("v", vc), ("r", sr))):
                    for c in range(DC):
                        await_step(act, kvr, b, f"{name}{c}")
                        nc.scalar.activation(dst[:, c, :], ring[(2 * n + c) % 4], ACT.Sigmoid if name == "r" else ACT.Copy)\
                            .then_inc(kvr_out.sem, 1)

            def conv_in(s):
                await_step(act, tr_rec, s, "t")
                await_step(act, rec, s - 1, "in")
                await_step(act, gates, s - 1, "i1")
                for c in range(DC):
                    nc.scalar.activation(xc[:, c, 3:T + 3], bank_t[:, c, :], ACT.Copy).then_inc(ev3.sem, 1)
                for c in range(DC):
                    nc.scalar.activation(cv[:, c, :], bank_t[:, c, :], ACT.Identity, bias=col("conv_b", c),
                                         scale=col("conv3", c)).then_inc(ev3.sem, 1)

            def relus(b, lo, hi):
                if lo == 0:
                    await_step(act, fv, b - 1, "v")
                for j in range(lo, hi):
                    await_step(act, fk, b, f"f{j}")
                    nc.scalar.activation(hid[:, j, :], ring[(j + 2) % 4], ACT.Relu).then_inc(relu.sem, 1)

            def turn(i):
                now, next_, channel, recur = (has(i, 0, 0, B - 1), has(i, 1, 0, B - 1), has(i, -1, 0, B - 1),
                                              has(i, -2, NB, B + NB - 1))
                if now:
                    keys(i)
                if recur:
                    s = seq(i - 2)
                    conv_in(s)
                if channel:
                    relus(i - 1, 0, 2)
                if now:
                    nc.scalar.preload_act_table_set(LOG_EXP)
                    await_step(act, wkv, i, "cap")
                    await_step(act, wkv_gv, i - 1, "gv")
                    nc.scalar.activation(g[:], g[:], ACT.Exp).then_inc(wkv_act.sem, 1)
                    await_step(act, wkv, i, "in")
                    nc.scalar.activation(dec[:], dec[:], ACT.Exp).then_inc(wkv_act.sem, 1)
                if channel:
                    relus(i - 1, 2, FC)
                if now:
                    await_step(act, wkv, i, "den")
                    nc.scalar.activation(den[:], den[:], ACT.Ln).then_inc(wkv_act.sem, 1)
                    await_step(act, wkv_act, i, "ln")
                    nc.scalar.activation(den[:], den[:], ACT.Exp, scale=-1.0).then_inc(wkv_act.sem, 1)
                if channel:
                    await_step(act, fr, i - 1, "f")
                    await_step(act, comb, i - 2, "x")
                    nc.scalar.activation(sf[:].rearrange("p c d -> p (c d)"), ring_rows.rearrange("p a t -> p (a t)"),
                                         ACT.Sigmoid).then_inc(fr_out.sem, 1)
                if recur:
                    await_step(act, rec, s - 1, "h1")
                    for n, (name, dst, b_) in enumerate((("r", rg, "b_r"), ("i", ig, "b_i"))):
                        for c in range(DC):
                            await_step(act, gates, s, f"{name}{c}")
                            nc.scalar.activation(dst[:, c, :], ring[2 * n + c], ACT.Sigmoid, bias=col(b_, c))\
                                .then_inc(gates_out.sem, 1)
                    nc.scalar.preload_act_table_set(LOG_EXP)
                    for c in range(DC):
                        await_step(act, gates_out, s, f"r{c}")
                        nc.scalar.activation(aa[:, c, :], rg[:, c, :], ACT.Exp, scale=log_a8[:, c:c + 1])\
                            .then_inc(gates_out.sem, 1)
                if next_:
                    await_step(act, tr_in, i + 1, "t")
                    await_step(act, mix1, i, "r1")
                    norm_out(xn1, "ln1_w", "ln1_b", ev1)
                if recur:
                    await_step(act, rec, s, "om")
                    nc.scalar.activation(om[:], om[:], ACT.Ln).then_inc(gates_out.sem, 1)
                    await_step(act, gates_out, s, "ln")
                    nc.scalar.activation(om[:], om[:], ACT.Exp, scale=0.5).then_inc(gates_out.sem, 1)
                    await_step(act, rproj, s, "o")
                    await_step(act, fin, s - 1, "ms")
                    for c in range(TC):
                        if c:
                            await_step(act, sumsq, s, f"s{c - 1}")
                        nc.scalar.activation(square[:], rows4[:, c, :], ACT.Square, accum_out=ssq[:, c:c + 1])\
                            .then_inc(sumsq.sem, 1)
                if now:
                    await_step(act, tr_mid, i, "t")
                    await_step(act, mix2, i - 1, "r1")
                    norm_out(xn2, "ln2_w", "ln2_b", ev2)

            def experts(f):
                base = f * NT

                def hidden(t):
                    act.wait_ge(up_done, t + (1 + base))
                    nc.scalar.activation(hb.rearrange("p a t -> p (a t)"), psum[:, 2:4, :].rearrange("p a t -> p (a t)"),
                                         ACT.Gelu).then_inc(gelu_done, 1)

                def rows_back(t):
                    act.wait_ge(tiles_done, t + (2 + base))
                    act.wait_ge(y_stored, (t + (1 + base)) * 16)
                    nc.scalar.activation(ys[:], psum[:, 6, 0:D], ACT.Copy).then_inc(y_out, 1)
                    act.wait_ge(y_out, t + (2 + base))
                    dst = ys_rows[t * P:(t + 1) * P, :] if isinstance(t, int) else ys_rows[bass.DynSlice(t * P, P), :]
                    act.dma_start(dst, ys[:]).then_inc(y_stored, 16)

                await_step(act, wkv, B - 1 if f else 2, "out")
                if f:
                    act.wait_ge(hid_t, base)
                hidden(0)
                with act.Fori(1, NT) as t:
                    act.wait_ge(hid_t, t + base)
                    hidden(t)
                    rows_back(t - 1)
                rows_back(NT - 1)

            turns(act, turn, experts)

        @block.tensor
        def _(pe):
            pe.wait_ge(consts_made, 12)

            def transposes(src, st):
                for c in range(DC):
                    for k in range(TC):
                        last = nc.tensor.transpose(bank_t[:, c, k * P:(k + 1) * P], src[:, k, c * P:(c + 1) * P], ident[:])
                last.then_inc(st.sem, 1)

            def columns(dst, w, m, src, st):
                for c in range(DC):
                    last = nc.tensor.matmul(dst, w[:, c, m * P:(m + 1) * P], src[:, c, :], start=c == 0, stop=c == DC - 1)
                last.then_inc(st.sem, 1)

            def rows(dst, src, w, chunks, st):
                for k in range(TC):
                    for c in range(chunks):
                        last = nc.tensor.matmul(dst[:, k, :], src[:, c, k * P:(k + 1) * P], w[:, c, :],
                                                start=c == 0, stop=c == chunks - 1)
                last.then_inc(st.sem, 1)

            def turn(i):
                if has(i, 0, 0, B - 1):
                    if at(i, 0):
                        pe.wait_ge(weights_loaded, 13 * 16)
                    await_step(pe, relu, i - 2, f"f{FC - 1}")
                    await_step(pe, fr_out, i - 2, "s")
                    if not isinstance(i, int) or i - 3 >= NB:
                        await_step(pe, gates_out, seq(i - 3), "i1")
                    for n, (name, w, src) in enumerate((("k", wk, xk), ("v", wv, xv), ("r", wr, xr))):
                        await_step(pe, mix1, i, f"{name}{DC - 1}")
                        for c in range(DC):
                            if name == "r":
                                await_step(pe, kvr_out, i, f"k{c}")
                            columns(ring[(2 * n + c) % 4], w, c, src, kvr)
                if at(i, 1):
                    await_step(pe, route, 0, "ni")
                    await_step(pe, ev1, 1, "e1")
                    await_step(pe, ev2, 0, "e1")
                    nc.tensor.matmul(psum[0:E, 0, 0:1], before[:], ntiles[:], start=True, stop=True)
                    nc.tensor.matmul(psum[0:E, 0, 1:2], upto[:], ntiles[:], start=True, stop=True)
                    nc.tensor.matmul(psum[0:1, 0, 2:2 + E], ntiles[:], upto[:], start=True, stop=True).then_inc(route_pe.sem, 1)
                    await_step(pe, route, 0, "pos")
                    by_token = rank.rearrange("e (c p k) -> e c k p", p=P, k=TOPK)
                    for c in range(NCH):
                        for k in range(TOPK):
                            n = 16 + c * TOPK + k
                            last = nc.tensor.matmul(psum[:, 0, n:n + 1], by_token[:, c, k, :], ones_e[:, 0:1],
                                                    start=True, stop=True)
                    last.then_inc(route_pe.sem, 1)
                    await_step(pe, route, 0, "past")
                    nc.tensor.matmul(psum[0:1, 0, 40:40 + NT], ones_e[:, 0:1], past[:], start=True, stop=True)\
                        .then_inc(route_pe.sem, 1)
                if has(i, -2, NB, B + NB - 1):
                    s = seq(i - 2)
                    await_step(pe, hat3, s, f"h{TC - 1}")
                    await_step(pe, ev2, i - 1, "e1")
                    await_step(pe, ev3, s - 1, "c1")
                    transposes(xhat[2], tr_rec)
                if has(i, -1, 0, B - 1):
                    await_step(pe, mix2, i - 1, "k1")
                    if not isinstance(i, int) or i - 3 >= NB:
                        await_step(pe, gates_out, seq(i - 3), "i1")
                    for j in range(FC):
                        if j < 4:
                            await_step(pe, kvr_out, i, ("v0", "v1", "r0", "r1")[j])
                        else:
                            await_step(pe, relu, i - 1, f"f{j - 4}")
                        columns(ring[(j + 2) % 4], fwk, j, xfk, fk)
                    await_step(pe, mix2, i - 1, "r1")
                    await_step(pe, relu, i - 1, f"f{FC - 3}")
                    rows(fr4, xfr, fwr, DC, fr)
                if has(i, -2, NB, B + NB - 1):
                    await_step(pe, conv, s, "c01")
                    await_step(pe, relu, i - 1, f"f{FC - 1}")
                    await_step(pe, gates_out, s - 1, "i1")
                    for n, w in enumerate((gwr, gwi)):
                        if n:
                            await_step(pe, fr_out, i - 1, "s")
                        for c in range(DC):
                            columns(ring[2 * n + c], w, c, cv, gates)
                if has(i, 0, 0, B - 1):
                    await_step(pe, wkv, i, "out")
                    await_step(pe, comb, i - 2, "g")
                    if not isinstance(i, int) or i - 3 >= NB:
                        await_step(pe, fin, seq(i - 3), f"f{TC - 1}")
                    rows(rows4, mixed, wo, DC, proj)
                if has(i, 1, 0, B - 1):
                    await_step(pe, hat1, i + 1, f"h{TC - 1}")
                    await_step(pe, ev2, i - 1, "e1")
                    if not isinstance(i, int) or i - 2 >= NB:
                        await_step(pe, ev3, seq(i - 2), "c1")
                    if at(i, 1):
                        await_step(pe, route, 0, "slot")
                    transposes(xhat[0], tr_in)
                if has(i, -1, 0, B - 1):
                    await_step(pe, sq, i - 1, f"f{FC - 1}")
                    await_step(pe, zsum, i, "z")
                    if not isinstance(i, int) or i - 3 >= NB:
                        await_step(pe, fin, seq(i - 3), f"f{TC - 1}")
                    rows(rows4, hid, fwv, FC, fv)
                if has(i, -2, NB, B + NB - 1):
                    await_step(pe, rec, s, "h1")
                    await_step(pe, comb, i - 1, "g")
                    await_step(pe, fin, s - 1, f"f{TC - 1}")
                    rows(rows4, hs, gwo, DC, rproj)
                if has(i, 0, 0, B - 1):
                    await_step(pe, hat2, i, f"h{TC - 1}")
                    await_step(pe, ev1, i + 1, "e1")
                    if not isinstance(i, int) or i - 2 >= NB:
                        await_step(pe, ev3, seq(i - 2), "c1")
                    transposes(xhat[1], tr_mid)

            def experts(f):
                base = f * NT

                def tile_in(t):
                    pe.wait_ge(gathered, (t + (1 + base)) * 16)
                    for c in range(DC):
                        last = nc.tensor.transpose(psum[:, 0, c * P:(c + 1) * P], xs[:, c * P:(c + 1) * P], ident[:])
                    last.then_inc(xs_t, 1)

                def up(t):
                    pe.wait_ge(xst_ready, t + (1 + base))
                    e = pe.value_load(table[0:1, bass.DynSlice(t, 1)], min_val=0, max_val=E - 1)
                    pe.wait_ge(expert_ready, e + (1 + f * E))
                    for h in range(FF // T):
                        for c in range(DC):
                            w = ew[:, bass.DynSlice(e % 2, 1), c * FF + h * T:c * FF + (h + 1) * T]
                            last = nc.tensor.matmul(psum[:, 2 + h, :], xst[:, c, :], w.rearrange("p a n -> p (a n)"),
                                                    start=c == 0, stop=c == DC - 1)
                    last.then_inc(up_done, 1)

                def turn_hidden(t):
                    pe.wait_ge(gelu_done, t + (1 + base))
                    flat = hb.rearrange("p a t -> p (a t)")
                    for j in range(FC):
                        last = nc.tensor.transpose(psum[:, 4 + j // 4, (j % 4) * P:(j % 4 + 1) * P],
                                                   flat[:, j * P:(j + 1) * P], ident[:])
                    last.then_inc(hid_t, 1)

                def down(t):
                    pe.wait_ge(hidt_ready, t + (1 + base))
                    pe.wait_ge(y_out, t + (1 + base))
                    e = pe.value_load(table[0:1, bass.DynSlice(t, 1)], min_val=0, max_val=E - 1)
                    for j in range(FC):
                        w = ew[:, bass.DynSlice(e % 2, 1), DC * FF + j * D:DC * FF + (j + 1) * D]
                        last = nc.tensor.matmul(psum[:, 6, 0:D], hbt[:, j, :], w.rearrange("p a n -> p (a n)"),
                                                start=j == 0, stop=j == FC - 1)
                    last.then_inc(tiles_done, 1)

                last = B - 1 if f else 2
                await_step(pe, ev1, last + 1, "e1")
                await_step(pe, ev2, last, "e1")
                await_step(pe, kvr_out, last, "r1")
                await_step(pe, relu, B - 1 if f else 1, f"f{FC - 1}")
                await_step(pe, fr_out, B - 1 if f else 1, "s")
                await_step(pe, zsum, last, "z")
                await_step(pe, comb, B - 1 if f else 1, "x")
                await_step(pe, route, 0, "tab1")
                if f:
                    await_step(pe, ev3, B - 1, "c1")
                    await_step(pe, gates_out, B - 1, "i1")
                    await_step(pe, fin, B - 1, "o")
                tile_in(0)
                up(0)
                with pe.Fori(1, NT) as t:
                    tile_in(t)
                    turn_hidden(t - 1)
                    up(t)
                    down(t - 1)
                turn_hidden(NT - 1)
                down(NT - 1)
                pe.wait_ge(y_out, NT + 1 + base)

            turns(pe, turn, experts)

        @block.vector
        def _(dve):
            def log_of_sigmoid():
                x_, (s_, s2, p, t) = vec[:, COL["log_a"]:COL["log_a"] + DC], [b_[:] for b_ in la]
                done = [0]

                def step(ins):
                    ins.then_inc(log_steps, 1)
                    done[0] += 1
                    dve.wait_ge(log_steps, done[0])

                dve.wait_ge(consts_loaded, 16)
                step(nc.vector.scalar_tensor_tensor(t, x_, -1.0, x_, ALU.mult, ALU.min))
                dve.wait_ge(exp_made, 1)
                step(nc.vector.tensor_scalar(t, s_, 2.0, None, ALU.add))
                step(nc.vector.reciprocal(t, t))
                step(nc.vector.tensor_tensor(s_, s_, t, ALU.mult))
                step(nc.vector.tensor_tensor(s2, s_, s_, ALU.mult))
                step(nc.vector.tensor_scalar(p, s2, 1.0 / LOG_TERMS[0], None, ALU.mult))
                for n in LOG_TERMS[1:]:
                    step(nc.vector.scalar_tensor_tensor(p, p, 1.0 / n, s2, ALU.add, ALU.mult))
                step(nc.vector.scalar_tensor_tensor(p, p, 1.0, s_, ALU.add, ALU.mult))
                step(nc.vector.tensor_scalar(t, x_, 0.0, 8.0, ALU.min, ALU.mult))
                step(nc.vector.scalar_tensor_tensor(log_a8[:], p, -16.0, t, ALU.mult, ALU.add))
                assert done[0] == LOG_STEPS

            for buf in (xn1, xn2, alpha, beta):
                nc.vector.memset(buf[:, :, 0:1], 0.0).then_inc(cols_made, 1)
            nc.vector.memset(top[:, :, 0:1], -1e30).then_inc(cols_made, 1)
            dve.wait_ge(vec_made, 2)
            log_of_sigmoid()

            def norm_stats(src, n, st, b, chunks):
                for c in range(chunks):
                    nc.vector.bn_stats(stats[n][:, c, :], src[:, c, :]).then_inc(st.sem, 1)
                await_apart(dve, st.sem, st.count(b, f"st{chunks - 1}"))
                for c in range(chunks):
                    nc.vector.bn_aggr(moments[n][:, c, :], stats[n][:, c, :]).then_inc(st.sem, 1)
                await_step(dve, st, b, f"ag{chunks - 1}")
                nc.vector.tensor_scalar(negmean[n][:, 0:chunks], moments[n][:, 0:chunks, 0], -1.0, None, ALU.mult)\
                    .then_inc(st.sem, 1)
                nc.vector.tensor_scalar(varis[n][:, 0:chunks], moments[n][:, 0:chunks, 1], EPS, None, ALU.add)\
                    .then_inc(st.sem, 1)

            def mix(src, st, b, outs):
                nc.vector.tensor_tensor(diff, src[:, :, 1:T + 1], src[:, :, 0:T], ALU.subtract).then_inc(st.sem, 1)
                await_step(dve, st, b, "d")
                for dst, m in outs:
                    for c in range(DC):
                        nc.vector.scalar_tensor_tensor(dst[:, c, :], diff[:, c, :], col(m, c), src[:, c, 0:T],
                                                       ALU.mult, ALU.add).then_inc(st.sem, 1)

            def mix_first(b):
                await_step(dve, ev1, b, "e1")
                await_step(dve, kvr, b - 1, "r1")
                mix(xn1, mix1, b, ((xk, "mix_k"), (xv, "mix_v"), (xr, "mix_r")))

            def mix_second(b):
                await_step(dve, ev2, b, "e1")
                await_step(dve, fr, b - 1, "f")
                mix(xn2, mix2, b, ((xfk, "fmix_k"), (xfr, "fmix_r")))

            def weights_of(b):
                was = top[:, :, 0:T]
                for c in range(DC):
                    await_step(dve, kvr_out, b, f"k{c}")
                    nc.vector.tensor_tensor_scan(top[:, c, 1:T + 1], decay[:, c:c + 1].to_broadcast([P, T]), kc[:, c, :],
                                                 -1e30, ALU.add, ALU.max).then_inc(wkv.sem, 1)
                for c in range(DC):
                    await_step(dve, wkv, b, f"m{c}")
                    nc.vector.scalar_tensor_tensor(g[:, c, :], kc[:, c, :], col("first", c), was[:, c, :],
                                                   ALU.add, ALU.subtract).then_inc(wkv.sem, 1)
                await_step(dve, wkv, b, "q1")
                nc.vector.tensor_scalar(g[:], g[:], LOGIT_CAP, None, ALU.min).then_inc(wkv.sem, 1)
                for c in range(DC):
                    nc.vector.scalar_tensor_tensor(dec[:, 0, c, :], was[:, c, :], decay[:, c:c + 1], top[:, c, 1:T + 1],
                                                   ALU.add, ALU.subtract).then_inc(wkv.sem, 1)
                nc.vector.tensor_tensor(dec[:, 1], kc[:], top[:, :, 1:T + 1], ALU.subtract).then_inc(wkv.sem, 1)

            def sums(b):
                await_step(dve, wkv_act, b, "dec")
                for c in range(DC):
                    nc.vector.tensor_tensor_scan(beta[:, c, 1:T + 1], dec[:, 0, c, :], dec[:, 1, c, :], 0.0,
                                                 ALU.mult, ALU.add).then_inc(wkv.sem, 1)
                await_step(dve, wkv, b, "b1")
                await_step(dve, kvr_out, b, "v1")
                nc.vector.tensor_tensor(dv, dec[:, 1], vc[:], ALU.mult).then_inc(wkv.sem, 1)
                await_step(dve, wkv, b, "dv")
                for c in range(DC):
                    nc.vector.tensor_tensor_scan(alpha[:, c, 1:T + 1], dec[:, 0, c, :], dv[:, c, :], 0.0,
                                                 ALU.mult, ALU.add).then_inc(wkv.sem, 1)

            def quotient(b):
                await_step(dve, wkv, b, "a1")
                await_step(dve, wkv_gv, b, "gv")
                nc.vector.tensor_tensor(num, alpha[:, :, 0:T], gv[:], ALU.add).then_inc(wkv.sem, 1)
                nc.vector.tensor_tensor(den[:], beta[:, :, 0:T], g[:], ALU.add).then_inc(wkv.sem, 1)

            def gated(b):
                await_step(dve, wkv_act, b, "inv")
                await_step(dve, kvr_out, b, "r1")
                nc.vector.tensor_tensor(den[:], den[:], sr[:], ALU.mult).then_inc(wkv.sem, 1)
                await_step(dve, wkv, b, "gate")
                nc.vector.tensor_tensor(mixed[:], den[:], num, ALU.mult).then_inc(wkv.sem, 1)

            def convolve(s):
                await_step(dve, ev3, s, "c1")
                for j in (2, 1, 0):
                    for c in range(DC):
                        if j < 2:
                            await_step(dve, conv, s, f"c{j + 1}{c}")
                        nc.vector.scalar_tensor_tensor(cv[:, c, :], xc[:, c, j:j + T], col(f"conv{j}", c), cv[:, c, :],
                                                       ALU.mult, ALU.add).then_inc(conv.sem, 1)

            def scales(s):
                await_step(dve, gates_out, s, "a1")
                nc.vector.scalar_tensor_tensor(om[:], aa[:], -1.0, aa[:], ALU.mult, ALU.mult).then_inc(rec.sem, 1)
                await_step(dve, rec, s, "na")
                nc.vector.tensor_scalar(om[:], om[:], 1.0, TINY, ALU.add, ALU.max).then_inc(rec.sem, 1)
                nc.vector.tensor_tensor(ig[:], ig[:], cv[:], ALU.mult).then_inc(rec.sem, 1)

            def recur(s):
                await_step(dve, gates_out, s, "sc")
                await_step(dve, rec, s, "in")
                nc.vector.tensor_tensor(ig[:], ig[:], om[:], ALU.mult).then_inc(rec.sem, 1)
                await_step(dve, rec, s, "b")
                await_step(dve, rproj, s - 1, "o")
                for c in range(DC):
                    nc.vector.tensor_tensor_scan(hs[:, c, :], aa[:, c, :], ig[:, c, :], 0.0, ALU.mult, ALU.add)\
                        .then_inc(rec.sem, 1)

            def route_first():
                dve.wait_ge(idx_loaded, 16)
                nc.vector.tensor_copy(rank, asg_i).then_inc(route.sem, 1)
                await_step(dve, route, 0, "idx")
                nc.vector.tensor_scalar(onehot, rank, expert_id[:], None, ALU.is_equal).then_inc(route.sem, 1)
                await_step(dve, route, 0, "one")
                nc.vector.tensor_tensor_scan(rank, ones_e[:, 0:1].to_broadcast([E, NASG]), onehot, 0.0,
                                             ALU.mult, ALU.add).then_inc(route.sem, 1)
                await_step(dve, route, 0, "rank")
                nc.vector.tensor_scalar(ntiles_i[:, 0:1], rank[:, NASG - 1:NASG], float(P - 1), None, ALU.add)\
                    .then_inc(route.sem, 1)
                await_step(dve, route, 0, "n")
                nc.vector.tensor_scalar(ntiles_i[:, 1:2], ntiles_i[:, 0:1], P.bit_length() - 1, None,
                                        ALU.logical_shift_right).then_inc(route.sem, 1)
                await_step(dve, route, 0, "nf")
                nc.vector.tensor_copy(ntiles[:], ntiles_i[:, 1:2]).then_inc(route.sem, 1)

            def route_second():
                await_step(dve, route_pe, 0, "ends")
                nc.vector.tensor_scalar(starts[:], psum[0:E, 0, 0:1], float(P), -1.0, ALU.mult, ALU.add).then_inc(route.sem, 1)
                nc.vector.tensor_copy(ends[:], psum[0:E, 0, 1:2]).then_inc(route.sem, 1)
                nc.vector.tensor_copy(table[0:1, NT:NT + E], psum[0:1, 0, 2:2 + E]).then_inc(route.sem, 1)
                await_step(dve, route, 0, "end")
                nc.vector.scalar_tensor_tensor(rank, rank, starts[:], onehot, ALU.add, ALU.mult).then_inc(route.sem, 1)
                nc.vector.tensor_scalar(past[:], tile_no[:], ends[:], None, ALU.is_ge).then_inc(route.sem, 1)
                await_step(dve, route_pe, 0, "experts")
                nc.vector.tensor_scalar(table[0:1, 0:NT], psum[0:1, 0, 40:40 + NT], float(E - 1), None, ALU.min)\
                    .then_inc(route.sem, 1)
                nc.vector.tensor_copy(slot_i[:], psum[:, 0, 16:16 + NCH * TOPK]).then_inc(route.sem, 1)

            def turn(i):
                now, next_, channel, recurs = (has(i, 0, 0, B - 1), has(i, 1, 0, B - 1), has(i, -1, 0, B - 1),
                                               has(i, -2, NB, B + NB - 1))
                s = seq(i - 2)
                if at(i, 1):
                    route_second()
                if channel:
                    mix_second(i - 1)
                if now:
                    weights_of(i)
                if recurs:
                    convolve(s)
                if now:
                    sums(i)
                    quotient(i)
                if next_:
                    dve.wait_ge(x_loaded, (i + 2) * 16)
                    await_step(dve, keep_y, i, "xb")
                    norm_stats(x_in, 0, ln1, i + 1, TC)
                    await_step(dve, ln1, i + 1, "v0")
                    nc.vector.tensor_scalar(varis[0][:, TC:2 * TC], moments[0][:, 0:TC, 1], 1.0 + EPS, EPS * EPS,
                                            ALU.mult, ALU.add).then_inc(ln1.sem, 1)
                if now:
                    gated(i)
                    await_step(dve, proj, i, "o")
                    await_step(dve, keep_y, i, "xb")
                    nc.vector.tensor_tensor(z[:], rows4, y[:], ALU.add).then_inc(zsum.sem, 1)
                    await_step(dve, zsum, i, "z")
                    await_step(dve, hat2, i - 1, f"h{TC - 1}")
                    norm_stats(z, 1, ln2, i, TC)
                if recurs:
                    scales(s)
                if at(i, 0):
                    route_first()
                if next_:
                    mix_first(i + 1)
                if recurs:
                    recur(s)
                if channel:
                    b = i - 1
                    await_step(dve, fv, b, "v")
                    await_step(dve, fr_out, b, "s")
                    nc.vector.tensor_tensor(sf[:], rows4, sf[:], ALU.mult).then_inc(comb.sem, 1)
                    await_step(dve, comb, b, "g")
                    await_step(dve, keep_xz, b, "xz")
                    early = isinstance(b, int) and b < NB
                    if not early and not (isinstance(b, int) and b == NB):
                        await_step(dve, keep_x2, seq(b - 1), "x2b")
                        await_step(dve, hat3, seq(b - 1), f"h{TC - 1}")
                    nc.vector.tensor_tensor(xf[:, TC * b:TC * (b + 1), :] if early else x2[:], sf[:], xz[:], ALU.add)\
                        .then_inc(comb.sem, 1)
                if has(i, -1, NB, B + NB - 1):
                    late = isinstance(i, int) and i - 1 >= B
                    if late:
                        await_step(dve, merged, 0, f"q{NCH - 1}")
                    else:
                        await_step(dve, comb, i - 1, "x")
                    await_step(dve, hat3, seq(i - 2), f"h{TC - 1}") if not isinstance(i, int) or i - 2 >= NB else None
                    norm_stats(xf[:, TC * (i - 1 - B):TC * (i - B), :] if late else x2, 2, ln3, seq(i - 1), TC)
                if recurs:
                    await_step(dve, sumsq, s, f"s{TC - 1}")
                    nc.vector.tensor_scalar(msq[:], ssq[:], 1.0 / D, EPS_RMS, ALU.mult, ALU.add).then_inc(fin.sem, 1)
                    await_step(dve, fin_pow, s, "p")
                    if not isinstance(s, int) or s > 0:
                        dve.wait_ge(out_stored, (s if not isinstance(s, int) else min(s, B - NB)) * 16)
                    for c in range(TC):
                        nc.vector.scalar_tensor_tensor(fo[:, c, :], rows4[:, c, :], rms[:, c:c + 1], gamma[:],
                                                       ALU.mult, ALU.mult).then_inc(fin.sem, 1)
                    await_step(dve, fin, s, f"f{TC - 1}")
                    await_step(dve, keep_x2, s, "x2b")
                    late = isinstance(i, int) and i - 2 >= B
                    nc.vector.tensor_tensor(xf[:, TC * (i - 2 - B):TC * (i - 1 - B), :] if late else fo, fo, x2b[:],
                                            ALU.add).then_inc(fin.sem, 1)

            def experts(f):
                base = f * NT
                await_step(dve, keep_y, B - 1 if f else 3, "xb")
                if f:
                    await_step(dve, fin, B - 1, "o")
                else:
                    await_step(dve, comb, NB - 1, "x")
                norm_stats(xf, 0, lnf, f, NCH)

                def tile(t):
                    dve.wait_ge(xs_t, t + (1 + base))
                    if f or not isinstance(t, int):
                        dve.wait_ge(up_done, t + base)
                    nc.vector.tensor_copy(xst[:].rearrange("p a n -> p (a n)"), psum[:, 0, 0:D]).then_inc(xst_ready, 1)

                def hidden(t):
                    dve.wait_ge(hid_t, t + (1 + base))
                    dve.wait_ge(tiles_done, t + (1 + base))
                    nc.vector.tensor_copy(hbt.rearrange("p j n -> p (j n)"), psum[:, 4:6, :].rearrange("p a t -> p (a t)"))\
                        .then_inc(hidt_ready, 1)

                tile(0)
                with dve.Fori(1, NT) as t:
                    tile(t)
                    hidden(t - 1)
                hidden(NT - 1)
                for c in range(NCH):
                    nc.vector.tensor_tensor(xf[:, c, :], xf[:, c, :], bias[:], ALU.add).then_inc(merged.sem, 1)
                    for k, name in enumerate(("b", "p")):
                        dve.wait_ge(picks[k], 16 * (f * NCH + c + 1))
                        await_step(dve, merged, f, f"{name}{c}")
                        nc.vector.scalar_tensor_tensor(xf[:, c, :], picked[:, k, :], choice_w[:, c, k:k + 1], xf[:, c, :],
                                                       ALU.mult, ALU.add).then_inc(merged.sem, 1)
                if f == 0:
                    nc.vector.memset(xc[:, :, 0:3], 0.0).then_inc(cols_made, 1)

            turns(dve, turn, experts)


def kernel(**inputs):
    import numpy as np
    import concourse.bacc as bacc
    from concourse.bass_utils import run_bass_kernel_spmd

    def given(name):
        return np.asarray(inputs[name])

    a, b = "L0_attn_a_", "L0_attn_b_"
    conv_w = given(b + "conv_w")
    vectors = [given(a + "ln1_w"), given(a + "ln1_b"), given(a + "ln2_w"), given(a + "ln2_b"),
               given(a + "time_decay"), given(a + "time_first"), given(a + "time_mix_k").reshape(-1),
               given(a + "time_mix_v").reshape(-1), given(a + "time_mix_r").reshape(-1),
               given(a + "f_time_mix_k").reshape(-1), given(a + "f_time_mix_r").reshape(-1),
               given(b + "conv_b"), given(b + "b_r"), given(b + "b_i"), given(b + "log_a")]
    vectors += [conv_w[:, 0, j] for j in range(4)]
    packed = np.concatenate([v.reshape(2, 128).T for v in vectors], axis=1)
    arrays = {
        "x": given(a + "x"), "vecs": packed, "bias": given("L0_ffn_bias"), "gamma": given(b + "gamma"),
        "w_key": given(a + "w_key"), "w_value": given(a + "w_value"), "w_recept": given(a + "w_recept"),
        "w_output": given(a + "w_output"), "f_w_key": given(a + "f_w_key"), "f_w_recept": given(a + "f_w_recept"),
        "f_w_value": given(a + "f_w_value"), "w_r_t": given(b + "W_r").T, "w_i_t": given(b + "W_i").T,
        "w_out_t": given(b + "W_out").T, "expert_weights": given("L0_ffn_expert_weights"),
        "expert_indices": given("L0_ffn_expert_indices"), "w1": given("L0_ffn_w1"), "w2": given("L0_ffn_w2"),
    }
    arrays = {name: np.ascontiguousarray(v) for name, v in arrays.items()}
    nc = bacc.Bacc("TRN2", target_bir_lowering=False, num_devices=1)
    args = [nc.dram_tensor("in_" + name, v.shape, mybir.dt.from_np(v.dtype), kind="ExternalInput").ap()
            for name, v in arrays.items()]
    out = nc.dram_tensor("out", (B, T, D), F32, kind="ExternalOutput").ap()
    hybrid_kernel(nc, *args, out)
    r = run_bass_kernel_spmd(nc, [{"in_" + name: v for name, v in arrays.items()}], core_ids=[0])
    return r.results[0]["out"]
```

```python
import concourse.bass as bass
from concourse import mybir
from contextlib import ExitStack

F32 = mybir.dt.float32
F32R = mybir.dt.float32r
I32 = mybir.dt.int32
ALU = mybir.AluOpType
ACT = mybir.ActivationFunctionType

B, T, D = 16, 512, 256
P = 128
DC = D // P
TC = T // P
FF = 1024
FC = FF // P
E, TOPK = 8, 2
NB = 2
NTOK = NB * T
NASG = NTOK * TOPK
NCH = NTOK // P
NT = NASG // P + E - 1
EPS = 1e-5
EPS_RMS = 1e-6
LOGIT_CAP = 40.0
TINY = 2.0 ** -60
SPECIAL = 3
FIRST, LAST = 5, 13

LOG_TERMS = range(15, 1, -2)
LOG_STEPS = 6 + len(LOG_TERMS) - 1 + 3

VECS = ["ln1_w", "ln1_b", "ln2_w", "ln2_b", "decay", "first", "mix_k", "mix_v", "mix_r", "fmix_k", "fmix_r",
        "conv_b", "b_r", "b_i", "log_a", "conv0", "conv1", "conv2", "conv3"]
COL = {name: DC * n for n, name in enumerate(VECS)}


class Steps:

    def __init__(self, sem, names, runs):
        self.sem, self.names, self.runs = sem, names, runs

    def count(self, run, name):
        return run * len(self.names) + self.names.index(name) + 1


def await_step(eng, steps, run, name):
    if isinstance(run, int):
        if run < 0:
            return
        run = min(run, steps.runs - 1)
    eng.wait_ge(steps.sem, steps.count(run, name))


def numbered(name, n):
    return [f"{name}{k}" for k in range(n)]


def hybrid_kernel(nc, x, vecs, bias_row, gamma_row, w_key, w_value, w_recept, w_output, f_w_key, f_w_recept,
                  f_w_value, w_r_t, w_i_t, w_out_t, expert_weights, expert_indices, w1, w2, out):
    ctx = ExitStack()
    with ctx:
        def sb(name, shape, dt=F32):
            return ctx.enter_context(nc.sbuf_tensor(name, shape, dt))

        def sem(name):
            return ctx.enter_context(nc.semaphore(name))

        def steps(name, names, runs):
            return Steps(sem(name), names, runs)

        ident = sb("ident", [P, P])
        half_neg = sb("half_neg", [P, 8])
        vec = sb("vec", [P, DC * len(VECS)])
        decay = sb("decay", [P, DC])
        log_a8 = sb("log_a8", [P, DC])
        euler = sb("euler", [P, DC])
        la = [sb(f"la{n}", [P, DC]) for n in range(4)]
        gamma = sb("gamma", [P, D])
        bias = sb("bias", [P, D])
        wk = sb("wk", [P, DC, D])
        wv = sb("wv", [P, DC, D])
        wr = sb("wr", [P, DC, D])
        wo = sb("wo", [P, DC, D])
        fwk = [sb(f"fwk_{part}", [P, DC, FF], F32R) for part in ("hi", "lo")]
        fwr = sb("fwr", [P, DC, D])
        fwv = sb("fwv", [P, FC, D])
        gw = [sb(f"gw_{part}", [P, 2, DC, D], F32R) for part in ("hi", "lo")]
        gwo = sb("gwo", [P, DC, D])

        x_in = sb("x_in", [P, TC, D])
        y = sb("y", [P, TC, D])
        xb = sb("xb", [P, TC, D])
        z = y
        xz = sb("xz", [P, TC, D])
        x2_space = sb("x2_space", [P, 2, TC, D])
        x2 = x2_space[:, 0]
        x2b = x2_space[:, 1]
        xhat = [sb(f"xhat{n}", [P, TC, D]) for n in range(2)]
        xhat.append(xhat[0])
        stats = [sb(f"stats{n}", [P, (TC if n in (1, 2) else 2 * TC), 6]) for n in range(4)]
        moments = [sb(f"moments{n}", [P, (TC if n in (1, 2) else 2 * TC), 2]) for n in range(4)]
        negmean = [sb(f"negmean{n}", [P, (TC if n in (1, 2) else 2 * TC)]) for n in range(4)]
        varis = [sb(f"varis{n}", [P, (TC if n in (1, 2) else 2 * TC)]) for n in range(4)]
        rstd = [sb(f"rstd{n}", [P, (TC if n in (1, 2) else 2 * TC)]) for n in range(4)]

        def carver(space):
            place = [0]

            def carve(*shape):
                n = shape[0] * shape[1]
                part = space[:, place[0]:place[0] + n].rearrange("p (a b) -> p a b", a=shape[0])
                place[0] += n
                return part
            return carve

        mix_space = sb("mix_space", [P, 8 * DC * T])
        carve = carver(mix_space)
        xn1 = sb("xn1", [P, DC, T + 1])
        xn2 = sb("xn2", [P, DC, T + 1])
        xk = carve(DC, T)
        xv = carve(DC, T)
        xr = carve(DC, T)
        xfk_hi = sb("xfk_hi", [P, DC, T], F32R)
        kc = carve(DC, T)
        vc = carve(DC, T)
        sr = carve(DC, T)
        top = sb("top", [P, DC, T + 1])
        dec = sb("dec", [P, 2, DC, T])
        diff = dec[:, 0]
        xfk_whole = dec[:, 1]
        dv = dec[:, 1]
        num = dec[:, 0]
        g = carve(DC, T)
        xfr = carve(DC, T)
        alpha = sb("alpha", [P, DC, T + 1])
        beta = sb("beta", [P, DC, T + 1])
        gv = vc
        den = kc
        mixed = sr
        hid = sb("hid", [P, FC, T])
        sf = sb("sf", [P, TC, D])

        place_of_a = DC * (T + 3) + 3 * DC * T
        with nc.sbuf_tensor("lead", [P, place_of_a + DC * T], F32), \
             nc.sbuf_tensor("parts", [P, 3, DC, T], F32R) as parts:
            cv_parts = [parts[:, 0], parts[:, 1]]
            xfk = [xfk_hi, parts[:, 2]]
        space = sb("space", [P, place_of_a + 4 * DC * T])
        carve = carver(space)
        xc = carve(DC, T + 3)
        cv = carve(DC, T)
        rg = carve(DC, T)
        ig = carve(DC, T)
        aa = carve(DC, T)
        om = carve(DC, T)
        hs = carve(DC, T)
        fo = aa.rearrange("p a (b n) -> p (a b) n", n=D)
        fwk_whole = space[:, 0:DC * FF].rearrange("p (c n) -> p c n", c=DC)
        gw_whole = space[:, DC * FF:DC * FF + 2 * DC * D].rearrange("p (g c n) -> p g c n", g=2, c=DC)
        SET = DC * FF + FC * D
        expert_sets = [s_[:, 0:2 * SET].rearrange("p (s n) -> p s n", s=2) for s_ in (space, mix_space)]
        picked = space[:, place_of_a:place_of_a + NCH * TOPK * D].rearrange("p (c k n) -> p c k n", c=NCH, k=TOPK)
        ssq = sb("ssq", [P, TC])
        msq = sb("msq", [P, TC])
        rms = sb("rms", [P, TC])

        xf = sb("xf", [P, NCH, D])
        choice_w = sb("choice_w", [P, NCH, TOPK])
        slot_i = sb("slot_i", [P, NCH * TOPK], I32)
        token_id = sb("token_id", [P, NCH], I32)
        token_of_slot = sb("token_of_slot", [P, NT], I32)
        token_idx = sb("token_idx", [P, 1], I32)
        table = sb("table", [1, NT + E], I32)
        xs = sb("xs", [P, D])
        xst = sb("xst", [P, DC, P])
        ys = sb("ys", [P, D])
        square = ys
        lent = [x2_space[:].rearrange("p w a n -> p w (a n)"), dec[:].rearrange("p w a n -> p w (a n)")]
        tile_rows = [s_[:, 1] for s_ in lent]
        tile_cols = [s_[:, 0].rearrange("p (j n) -> p j n", n=P) for s_ in lent]
        xfn = [s_.rearrange("p w (c n) -> p (w c) n", n=D) for s_ in lent]

        psum = ctx.enter_context(nc.psum_tensor("psum", [P, 8, T], F32))
        bank_t = psum[:, 0:DC, :]
        ring = [psum[:, 2 + n, :] for n in range(4)]
        ring_rows = psum[:, 4:6, :]
        rows_out = psum[:, 6:8, :]
        rows4 = psum[:, 6:8, :].rearrange("p a (b n) -> p (a b) n", n=D)
        fr4 = psum[:, 4:6, :].rearrange("p a (b n) -> p (a b) n", n=D)

        rank = space[0:E, place_of_a:place_of_a + NASG]
        onehot = x2_space[0:E].rearrange("p w c n -> p (w c n)")
        asg_i = onehot.bitcast(I32)
        note_at = [0]

        def note(n):
            note_at[0] += n
            return ys[0:E, note_at[0] - n:note_at[0]]

        ones_e, tile_no, past = note(NT), note(NT), note(NT)
        before = note(E)
        upto = note(E)
        expert_id, ntiles, ends, starts = note(1), note(1), note(1), note(1)
        ntiles_i = note(2).bitcast(I32)

        token_table = nc.dram_tensor("token_table", (NT * P, 1), I32, kind="Internal").ap()
        xf_rows = nc.dram_tensor("xf_rows", (NTOK, D), F32, kind="Internal").ap()
        ys_rows = nc.dram_tensor("ys_rows", (NT * P, D), F32, kind="Internal").ap()

        x_loaded = sem("x_loaded")
        passed = sem("passed")
        consts_loaded = sem("consts_loaded")
        consts_made = sem("consts_made")
        cols_made = sem("cols_made")
        split_his = sem("split_his")
        split_los = sem("split_los")
        weights_loaded = sem("weights_loaded")
        vec_made = sem("vec_made")
        log_steps = sem("log_steps")
        exp_made = sem("exp_made")
        out_stored = sem("out_stored")
        tr_in = steps("tr_in", ["t"], B)
        tr_mid = steps("tr_mid", ["t"], B)
        tr_rec = steps("tr_rec", ["t"], B)
        ln1 = steps("ln1", numbered("st", TC) + numbered("ag", TC) + ["neg", "v0", "v1"], B)
        ln2 = steps("ln2", numbered("st", TC) + numbered("ag", TC) + ["neg", "v0"], B)
        ln3 = steps("ln3", numbered("st", TC) + numbered("ag", TC) + ["neg", "v0"], B)
        hat1 = steps("hat1", ["pow"] + numbered("h", TC), B)
        hat2 = steps("hat2", ["pow"] + numbered("h", TC), B)
        hat3 = steps("hat3", ["pow"] + numbered("h", TC), B)
        keep_y = steps("keep_y", numbered("y", TC) + ["xb"], B)
        keep_xz = steps("keep_xz", ["xz"], B)
        keep_x2 = steps("keep_x2", ["x2b"], B)
        ev1 = steps("ev1", numbered("e", DC), B)
        ev2 = steps("ev2", numbered("e", DC), B)
        ev3 = steps("ev3", numbered("x", DC) + numbered("c", DC), B)
        mix1 = steps("mix1", ["d"] + numbered("k", DC) + numbered("v", DC) + numbered("r", DC), B)
        mix2 = steps("mix2", ["d"] + numbered("k", DC) + ["hi", "lo"] + numbered("r", DC), B)
        kvr = steps("kvr", numbered("k", DC) + numbered("v", DC) + numbered("r", DC), B)
        kvr_out = steps("kvr_out", numbered("k", DC) + numbered("v", DC) + numbered("r", DC), B)
        wkv = steps("wkv", ["m0", "m1", "q0", "q1", "cap", "z0", "z1", "in", "b0", "b1", "dv", "a0", "a1",
                            "num", "den", "gate", "out"], B)
        wkv_act = steps("wkv_act", ["g", "dec", "ln", "inv"], B)
        wkv_gv = steps("wkv_gv", ["gv"], B)
        proj = steps("proj", ["o"], B)
        zsum = steps("zsum", ["z"], B)
        fk = steps("fk", numbered("f", FC), B)
        relu = steps("relu", numbered("f", FC), B)
        sq = steps("sq", numbered("f", FC), B)
        fr = steps("fr", ["f"], B)
        fr_out = steps("fr_out", ["s"], B)
        fv = steps("fv", ["a", "v"], B)
        comb = steps("comb", ["a", "g", "x"], B)
        conv = steps("conv", [f"c{j}{c}" for j in (2, 1, 0) for c in range(DC)] + ["hi", "lo"], B)
        gates = steps("gates", numbered("r", DC) + numbered("i", DC), B)
        gates_out = steps("gates_out", numbered("r", DC) + numbered("i", DC) + numbered("a", DC) + ["ln", "sc"], B)
        rec = steps("rec", ["na", "om", "b", "h0", "h1"], B)
        rproj = steps("rproj", ["a", "o"], B)
        sumsq = steps("sumsq", numbered("s", TC), B)
        fin = steps("fin", ["ms"] + numbered("f", TC), B)
        fin_pow = steps("fin_pow", ["p"], B)
        res = steps("res", ["o"], B)
        gin = steps("gin", ["in"], B)

        route = steps("route", ["idx", "one", "rank", "n", "nf", "ni", "start", "end", "tab0", "pos", "past", "tab1",
                                "slot"], 1)
        route_pe = steps("route_pe", ["ends", "slots", "experts"], 1)
        idx_loaded = sem("idx_loaded")
        table_zeroed = sem("table_zeroed")
        table_written = sem("table_written")
        table_loaded = sem("table_loaded")
        lnf = steps("lnf", numbered("st", NCH) + numbered("ag", NCH) + ["neg", "v0"], 2)
        powf = sem("powf")
        hatf = steps("hatf", numbered("h", NCH), 2)
        xf_stored = sem("xf_stored")
        expert_loaded = [sem(f"expert_loaded{n}") for n in range(2)]
        expert_ready = sem("expert_ready")
        gathered = sem("gathered")
        idx_copied = sem("idx_copied")
        xs_t = sem("xs_t")
        xst_ready = sem("xst_ready")
        up_done = sem("up_done")
        gelu_done = sem("gelu_done")
        hid_t = sem("hid_t")
        hidt_ready = sem("hidt_ready")
        tiles_done = sem("tiles_done")
        y_out = sem("y_out")
        y_stored = sem("y_stored")
        picks = [sem(f"picks{c}") for c in range(NCH)]
        merged = steps("merged", [f"{n}{c}" for c in range(NCH) for n in ("b", "p", "q")], 2)

        block = ctx.enter_context(nc.Block())

        def wide(ap, n):
            return ap[:].unsqueeze(1).to_broadcast([P, n, D])

        def col(name, c):
            return vec[:, COL[name] + c:COL[name] + c + 1]

        def turns(eng, turn):
            for i in range(-1, FIRST):
                turn(i)
            with eng.Fori(FIRST, LAST + 1) as i:
                turn(i)
            for i in range(LAST + 1, B + 2):
                turn(i)

        def has(i, shift, low, high):
            return not isinstance(i, int) or low <= i + shift <= high

        def at(i, n):
            return isinstance(i, int) and i == n

        def rows_of(b):
            return xf[:, TC * b:TC * (b + 1), :] if isinstance(b, int) and b < NB else x2

        def await_apart(eng, semaphore, value):
            eng.wait_ge(semaphore, value)
            eng.sem_inc(passed, 1)

        @block.sync
        def _(sp):
            def load_x(b):
                await_step(sp, ln1, b - 1, "st3")
                await_step(sp, keep_y, b - 1, "xb")
                src = x[b] if isinstance(b, int) else x[bass.DynSlice(b, 1)].rearrange("a t d -> (a t) d")
                sp.dma_start(x_in[:], src.rearrange("(c p) d -> p c d", p=P)).then_inc(x_loaded, 16)

            sp.dma_start(vec[:], vecs).then_inc(consts_loaded, 16)
            load_x(0)
            sp.dma_start(asg_i[:], expert_indices.rearrange("n k -> (n k)").partition_broadcast(E)).then_inc(idx_loaded, 16)
            for dst, src in ((wk[:], w_key), (wv[:], w_value), (wr[:], w_recept), (wo[:], w_output), (fwk_whole, f_w_key),
                             (fwr[:], f_w_recept), (fwv[:], f_w_value), (gw_whole[:, 0], w_r_t), (gw_whole[:, 1], w_i_t),
                             (gwo[:], w_out_t)):
                sp.dma_start(dst, src.rearrange("(c p) n -> p c n", p=P)).then_inc(weights_loaded, 16)
            sp.dma_start(bias[:], bias_row.partition_broadcast(P)).then_inc(weights_loaded, 16)
            sp.dma_start(gamma[:], gamma_row.partition_broadcast(P)).then_inc(weights_loaded, 16)
            sp.dma_start(choice_w[:], expert_weights.rearrange("(c p) k -> p c k", p=P)).then_inc(weights_loaded, 16)

            sp.wait_ge(consts_made, 8)
            sp.dma_start(token_table.rearrange("(p t) a -> p (t a)", p=P),
                         xs[:, 0:NT].bitcast(I32)).then_inc(table_zeroed, 16)

            def load_expert(f, e):
                half = expert_sets[f][:, e % 2, :]
                sp.dma_start(half[:, 0:DC * FF].rearrange("p (c n) -> p c n", c=DC),
                             w1[e].rearrange("(c p) n -> p c n", p=P)).then_inc(expert_loaded[e % 2], 16)
                sp.dma_start(half[:, DC * FF:SET].rearrange("p (c n) -> p c n", c=FC),
                             w2[e].rearrange("(c p) n -> p c n", p=P)).then_inc(expert_loaded[e % 2], 16)

            def announce_expert(f, e):
                sp.wait_ge(expert_loaded[e % 2], 32 * (f * E // 2 + e // 2 + 1))
                sp.sem_inc(expert_ready, 1)

            def turn(i):
                if at(i, B):
                    await_step(sp, proj, B - 1, "o")
                    load_expert(1, 0)
                    normalised_out(1)
                    await_step(sp, fr, B - 1, "f")
                    load_expert(1, 1)
                    announce_expert(1, 0)
                    announce_expert(1, 1)
                if at(i, 1):
                    sp.wait_ge(split_los, 2)
                    load_expert(0, 0)
                if at(i, SPECIAL):
                    normalised_out(0)
                    await_step(sp, fk, SPECIAL - 1, f"f{FC - 1}")
                    load_expert(0, 1)
                    experts(0)
                if has(i, 2, 1, B - 1):
                    load_x(i + 2)
                if has(i, -2, NB, B - 1):
                    await_step(sp, res, i - 2, "o")
                    dst = out[i - 2] if isinstance(i, int) else out[bass.DynSlice(i - 2, 1)].rearrange("a t d -> (a t) d")
                    sp.dma_start(dst.rearrange("(c p) d -> p c d", p=P), fo[:]).then_inc(out_stored, 16)

            def normalised_out(f):
                if f == 0:
                    sp.wait_ge(table_written, 16 * NCH * TOPK)
                    sp.dma_start(token_of_slot[:], token_table.rearrange("(t p) a -> p (t a)", p=P),
                                 allow_slow_non_contiguous=True).then_inc(table_loaded, 16)
                await_step(sp, hatf, f, f"h{NCH - 1}")
                sp.dma_start(xf_rows.rearrange("(c p) d -> p c d", p=P), xfn[f]).then_inc(xf_stored, 16)

            def experts(f):
                if f == 0:
                    announce_expert(f, 0)
                    announce_expert(f, 1)
                    await_step(sp, route, 0, "tab1")
                for e in range(2, E):
                    last = sp.value_load(table[0:1, NT + e - 2:NT + e - 1], min_val=0, max_val=NT)
                    sp.wait_ge(tiles_done, last + (1 + f * NT))
                    load_expert(f, e)
                    announce_expert(f, e)

            turns(sp, turn)
            experts(1)
            for b in range(NB):
                await_step(sp, merged, 1, f"q{TC * (b + 1) - 1}")
                sp.dma_start(out[b].rearrange("(c p) d -> p c d", p=P), xf[:, TC * b:TC * (b + 1), :])\
                    .then_inc(out_stored, 16)
            sp.wait_ge(out_stored, 16 * B)

        @block.gpsimd
        def _(pool):
            pool.memset(ident[:], 0.0).then_inc(consts_made, 1)
            pool.memset(xs[:], 0.0).then_inc(consts_made, 1)
            pool.memset(half_neg[:], -0.5).then_inc(consts_made, 1)
            pool.memset(ones_e, 1.0).then_inc(consts_made, 1)
            pool.memset(before, 1.0).then_inc(consts_made, 1)
            pool.memset(upto, 1.0).then_inc(consts_made, 1)
            pool.iota(token_id[:], pattern=[[P, NCH]], base=0, channel_multiplier=1).then_inc(consts_made, 1)
            pool.wait_ge(consts_made, 7)
            pool.affine_select(out=ident[:], in_=ident[:], compare_op=ALU.not_equal, fill=1.0, base=0,
                               pattern=[[-1, P]], channel_multiplier=1).then_inc(consts_made, 1)
            pool.affine_select(out=before, in_=before, compare_op=ALU.is_gt, fill=0.0, base=0,
                               pattern=[[1, E]], channel_multiplier=-1).then_inc(consts_made, 1)
            pool.affine_select(out=upto, in_=upto, compare_op=ALU.is_ge, fill=0.0, base=0,
                               pattern=[[1, E]], channel_multiplier=-1).then_inc(consts_made, 1)
            pool.iota(expert_id, pattern=[[0, 1]], base=0, channel_multiplier=1,
                      allow_small_or_imprecise_dtypes=True).then_inc(consts_made, 1)
            pool.iota(tile_no, pattern=[[1, NT]], base=0, channel_multiplier=0,
                      allow_small_or_imprecise_dtypes=True).then_inc(consts_made, 1)
            pool.memset(euler[:], 2.718281828459045).then_inc(consts_made, 1)
            pool.wait_ge(log_steps, 1)
            pool.wait_ge(consts_made, 13)
            pool.tensor_tensor(la[0][:], euler[:], la[3][:], ALU.pow).then_inc(exp_made, 1)
            pool.sem_inc(tiles_done, 1)
            pool.sem_inc(y_out, 1)
            pool.sem_inc(y_stored, 16)

            def power(dst, src, done):
                pool.tensor_tensor(dst, src, half_neg[:, 0:src.shape[1]], ALU.pow).then_inc(done, 1)

            def scale_rows(dst, src, n, col0, st, b, name):
                for c in range(dst.shape[1]):
                    pool.tensor_scalar(dst[:, c, :], src[:, c, :], negmean[n][:, c:c + 1],
                                       rstd[n][:, col0 + c:col0 + c + 1], ALU.add, ALU.mult).then_inc(st.sem, 1)

            def norm1(b):
                await_step(pool, ln1, b, "v1")
                await_step(pool, keep_y, b - 1, "xb")
                power(rstd[0][:], varis[0][:], hat1.sem)
                await_step(pool, tr_in, b - 1, "t")
                await_step(pool, tr_rec, -1 if isinstance(b, int) and b <= SPECIAL + 1 else b - 3, "t")
                await_apart(pool, hat1.sem, hat1.count(b, "pow"))
                scale_rows(xhat[0], x_in, 0, TC, hat1, b, "h")

            def keep1(b):
                await_step(pool, zsum, b - 1, "z")
                await_step(pool, keep_xz, b - 1, "xz")
                await_step(pool, hat2, b - 1, f"h{TC - 1}")
                await_apart(pool, hat1.sem, hat1.count(b, "pow"))
                scale_rows(y, x_in, 0, 0, keep_y, b, "y")
                await_step(pool, keep_xz, b - 1, "xz")
                if isinstance(b, int) and b < NB:
                    pool.tensor_copy(xb[:], x_in[:]).then_inc(keep_y.sem, 1)
                else:
                    pool.tensor_tensor(xb[:], x_in[:], wide(bias, TC), ALU.add).then_inc(keep_y.sem, 1)

            def norm2(b):
                await_step(pool, ln2, b, "v0")
                await_step(pool, hat2, b - 1, f"h{TC - 1}")
                power(rstd[1][:, 0:TC], varis[1][:, 0:TC], hat2.sem)
                await_step(pool, tr_mid, b - 1, "t")
                await_apart(pool, hat2.sem, hat2.count(b, "pow"))
                scale_rows(xhat[1], z, 1, 0, hat2, b, "h")

            def keep2(b):
                await_step(pool, zsum, b, "z")
                await_step(pool, keep_y, b, "xb")
                await_step(pool, comb, b - 1, "x")
                pool.tensor_tensor(xz[:], xb[:], z[:], ALU.add).then_inc(keep_xz.sem, 1)

            def norm3(b):
                await_step(pool, ln3, b, "v0")
                await_step(pool, hat3, b - 1, f"h{TC - 1}")
                power(rstd[2][:, 0:TC], varis[2][:, 0:TC], hat3.sem)
                await_step(pool, tr_rec, b - 1, "t")
                await_step(pool, tr_in, SPECIAL + 1 if isinstance(b, int) and b < NB else b + 2, "t")
                await_apart(pool, hat3.sem, hat3.count(b, "pow"))
                scale_rows(xhat[2], rows_of(b), 2, 0, hat3, b, "h")

            def keep3(b):
                early = isinstance(b, int) and b < NB
                if early:
                    await_step(pool, merged, 0, f"q{TC * (b + 1) - 1}")
                else:
                    await_step(pool, comb, b, "x")
                await_step(pool, res, b - 1, "o")
                if early:
                    pool.tensor_copy(x2b, rows_of(b)).then_inc(keep_x2.sem, 1)
                else:
                    pool.tensor_tensor(x2b, rows_of(b), wide(bias, TC), ALU.add).then_inc(keep_x2.sem, 1)

            def gated_input(b):
                await_step(pool, gates_out, b, "i1")
                pool.tensor_tensor(ig[:], ig[:], cv[:], ALU.mult).then_inc(gin.sem, 1)

            def residual(b):
                await_step(pool, fin, b, f"f{TC - 1}")
                pool.tensor_tensor(rows_of(b) if isinstance(b, int) and b < NB else fo, fo, x2b, ALU.add).then_inc(res.sem, 1)

            def mean_power(b):
                await_step(pool, fin, b, "ms")
                power(rms[:], msq[:], fin_pow.sem)

            def weighted(b):
                await_step(pool, wkv_act, b, "g")
                await_step(pool, wkv, b, "dv")
                pool.tensor_tensor(gv[:], g[:], vc[:], ALU.mult).then_inc(wkv_gv.sem, 1)

            def squares(b):
                for j in range(FC):
                    await_step(pool, relu, b, f"f{j}")
                    pool.tensor_tensor(hid[:, j, :], hid[:, j, :], hid[:, j, :], ALU.mult).then_inc(sq.sem, 1)

            def turn(i):
                if at(i, 0):
                    pool.wait_ge(split_his, 2)
                    pool.tensor_tensor(fwk[1][:], fwk_whole, fwk[0][:].bitcast(F32), ALU.subtract).then_inc(split_los, 1)
                    pool.tensor_tensor(gw[1][:], gw_whole, gw[0][:].bitcast(F32), ALU.subtract).then_inc(split_los, 1)
                if at(i, SPECIAL):
                    first_gather(0)
                    squares(i - 1)
                    weighted(i)
                    norm1(i + 1)
                    more_gathers(0, 1)
                    picking(0, 0)
                    norm2(i)
                    picking(0, 1)
                if at(i, SPECIAL + 1):
                    keep3(1)
                    gated_input(1)
                if has(i, -1, 0, B - 1) and not at(i, SPECIAL):
                    squares(i - 1)
                if has(i, 0, 0, B - 1) and not at(i, SPECIAL):
                    weighted(i)
                if at(i, SPECIAL + 1):
                    mean_power(1)
                    residual(1)
                if has(i, 1, 0, B - 1) and not at(i, SPECIAL):
                    norm1(i + 1)
                if at(i, SPECIAL - 1):
                    await_step(pool, route, 0, "slot")
                    pool.wait_ge(table_zeroed, 16)
                    for c in range(NCH):
                        for k in range(TOPK):
                            n = c * TOPK + k
                            pool.indirect_dma_start(
                                out=token_table, out_offset=bass.IndirectOffsetOnAxis(ap=slot_i[:, n:n + 1], axis=0),
                                in_=token_id[:, c:c + 1], in_offset=None).then_inc(table_written, 16)
                if has(i, -2, NB, B - 1):
                    keep3(i - 2)
                    if at(i, B):
                        first_gather(1)
                    if at(i, B + 1):
                        later_gather(1, 2)
                    gated_input(i - 2)
                    if at(i, B):
                        later_gather(1, 1)
                    if at(i, B + 1):
                        later_gather(1, 3)
                if at(i, B - 1):
                    norm_power(1)
                if has(i, 0, 0, B - 1) and not at(i, SPECIAL):
                    norm2(i)
                if at(i, SPECIAL):
                    norm3(0)
                    keep3(0)
                    keep2(i)
                    keep1(i + 1)
                    gated_input(0)
                    norm3(1)
                    mean_power(0)
                    residual(0)
                if has(i, -2, NB, B - 1):
                    mean_power(i - 2)
                if has(i, -1, NB, B - 1):
                    norm3(i - 1)
                if has(i, -2, NB, B - 1):
                    residual(i - 2)
                if has(i, 0, 0, B - 1) and not at(i, SPECIAL):
                    keep2(i)
                if at(i, SPECIAL - 1):
                    norm_power(0)
                if has(i, 1, 0, B - 1) and not at(i, SPECIAL):
                    if at(i, -1):
                        pool.wait_ge(weights_loaded, 13 * 16)
                    keep1(i + 1)

            def norm_power(f):
                await_step(pool, lnf, f, "v0")
                pool.tensor_tensor(rstd[3][:, 0:NCH], varis[3][:, 0:NCH], half_neg[:, 0:NCH], ALU.pow).then_inc(powf, 1)

            def gather(t, n):
                src = token_of_slot[:, bass.DynSlice(t, 1)]
                pool.tensor_copy(token_idx[:], src).then_inc(idx_copied, 1)
                await_apart(pool, idx_copied, n + 1)
                pool.indirect_dma_start(out=xs[:], out_offset=None, in_=xf_rows,
                                        in_offset=bass.IndirectOffsetOnAxis(ap=token_idx[:, 0:1], axis=0)).then_inc(gathered, 16)

            def first_gather(f):
                if f == 0:
                    pool.wait_ge(table_loaded, 16)
                else:
                    pool.wait_ge(xs_t, NT)
                pool.wait_ge(xf_stored, 16 * (f + 1))
                gather(0, f * NT)

            def later_gather(f, t):
                pool.wait_ge(xs_t, t + f * NT)
                gather(t, t + f * NT)

            def more_gathers(f, start):
                with pool.Fori(start, NT) as t:
                    later_gather(f, t)

            def picking(f, b):
                pool.wait_ge(y_stored, 16 * (NT * (f + 1) + 1))
                for c in range(TC * b, TC * (b + 1)):
                    for k in range(TOPK):
                        n = c * TOPK + k
                        pool.indirect_dma_start(
                            out=picked[:, c, k, :], out_offset=None, in_=ys_rows,
                            in_offset=bass.IndirectOffsetOnAxis(ap=slot_i[:, n:n + 1], axis=0)).then_inc(picks[c], 16)

            turns(pool, turn)
            more_gathers(1, 4)
            for b in range(NB):
                picking(1, b)

        @block.scalar
        def _(act):
            act.wait_ge(consts_loaded, 16)
            LOG_EXP = "natural_log_exp_and_others"
            nc.scalar.preload_act_table_set(LOG_EXP)
            nc.scalar.activation(decay[:], vec[:, COL["decay"]:COL["decay"] + DC], ACT.Exp).then_inc(vec_made, 1)
            act.wait_ge(vec_made, 1)
            nc.scalar.mul(decay[:], decay[:], -1.0).then_inc(vec_made, 1)
            act.wait_ge(cols_made, 5)
            act.wait_ge(log_steps, LOG_STEPS)

            def norm_out(dst, w, b, ev):
                for c in range(DC):
                    nc.scalar.activation(dst[:, c, 1:T + 1], bank_t[:, c, :], ACT.Identity, bias=col(b, c),
                                         scale=col(w, c)).then_inc(ev.sem, 1)

            def keys(b):
                await_step(act, wkv, b - 1, "out")
                for n, (name, dst) in enumerate((("k", kc), ("v", vc), ("r", sr))):
                    for c in range(DC):
                        await_step(act, kvr, b, f"{name}{c}")
                        nc.scalar.activation(dst[:, c, :], ring[(2 * n + c) % 4], ACT.Sigmoid if name == "r" else ACT.Copy)\
                            .then_inc(kvr_out.sem, 1)

            def conv_in(b):
                await_step(act, tr_rec, b, "t")
                await_step(act, gin, b - 1, "in")
                await_step(act, gates, b - 1, "i1")
                if at(b, 0):
                    act.wait_ge(cols_made, 6)
                for c in range(DC):
                    nc.scalar.activation(xc[:, c, 3:T + 3], bank_t[:, c, :], ACT.Copy).then_inc(ev3.sem, 1)
                for c in range(DC):
                    nc.scalar.activation(cv[:, c, :], bank_t[:, c, :], ACT.Identity, bias=col("conv_b", c),
                                         scale=col("conv3", c)).then_inc(ev3.sem, 1)

            def gates_in(b):
                await_step(act, rec, b - 1, "h1")
                await_step(act, res, b - 1, "o")
                if not isinstance(b, int) or b > NB:
                    act.wait_ge(out_stored, (b - NB) * 16)
                for n, (name, dst, b_) in enumerate((("r", rg, "b_r"), ("i", ig, "b_i"))):
                    for c in range(DC):
                        await_step(act, gates, b, f"{name}{c}")
                        nc.scalar.activation(dst[:, c, :], ring[2 * n + c], ACT.Sigmoid, bias=col(b_, c))\
                            .then_inc(gates_out.sem, 1)

            def decays(b):
                for c in range(DC):
                    await_step(act, gates_out, b, f"r{c}")
                    nc.scalar.activation(aa[:, c, :], rg[:, c, :], ACT.Exp, scale=log_a8[:, c:c + 1])\
                        .then_inc(gates_out.sem, 1)

            def root(b):
                await_step(act, rec, b, "om")
                nc.scalar.activation(om[:], om[:], ACT.Ln).then_inc(gates_out.sem, 1)
                await_step(act, gates_out, b, "ln")
                nc.scalar.activation(om[:], om[:], ACT.Exp, scale=0.5).then_inc(gates_out.sem, 1)

            def sums_of_squares(b):
                await_step(act, rproj, b, "o")
                await_step(act, fin, b - 1, "ms")
                for c in range(TC):
                    if c:
                        await_step(act, sumsq, b, f"s{c - 1}")
                    nc.scalar.activation(square[:], rows4[:, c, :], ACT.Square, accum_out=ssq[:, c:c + 1])\
                        .then_inc(sumsq.sem, 1)

            def receptance(b):
                await_step(act, fr, b, "f")
                await_step(act, comb, b - 1, "x")
                nc.scalar.activation(sf[:].rearrange("p c d -> p (c d)"), ring_rows.rearrange("p a t -> p (a t)"),
                                     ACT.Sigmoid).then_inc(fr_out.sem, 1)

            def relus(b, lo, hi):
                if lo == 0:
                    await_step(act, fv, b - 1, "v")
                for j in range(lo, hi):
                    await_step(act, fk, b, f"f{j}")
                    nc.scalar.activation(hid[:, j, :], ring[(j + 2) % 4], ACT.Relu).then_inc(relu.sem, 1)

            def turn(i):
                if at(i, 0):
                    act.wait_ge(weights_loaded, 13 * 16)
                    nc.scalar.activation(fwk[0][:], fwk_whole, ACT.Copy).then_inc(split_his, 1)
                    nc.scalar.activation(gw[0][:], gw_whole, ACT.Copy).then_inc(split_his, 1)
                now, next_, channel, recur = (has(i, 0, 0, B - 1), has(i, 1, 0, B - 1), has(i, -1, 0, B - 1),
                                              has(i, -2, NB, B - 1))
                if now and not at(i, SPECIAL + 1):
                    keys(i)
                if at(i, SPECIAL + 1):
                    gates_in(1)
                    nc.scalar.preload_act_table_set(LOG_EXP)
                    decays(1)
                elif recur:
                    conv_in(i - 2)
                if channel:
                    relus(i - 1, 0, 2)
                if now:
                    nc.scalar.preload_act_table_set(LOG_EXP)
                    await_step(act, wkv, i, "cap")
                    await_step(act, wkv_gv, i - 1, "gv")
                    nc.scalar.activation(g[:], g[:], ACT.Exp).then_inc(wkv_act.sem, 1)
                if channel:
                    relus(i - 1, 2, 4)
                if now:
                    await_step(act, wkv, i, "in")
                    nc.scalar.activation(dec[:], dec[:], ACT.Exp).then_inc(wkv_act.sem, 1)
                if at(i, SPECIAL + 1):
                    root(1)
                if channel:
                    relus(i - 1, 4, FC)
                if channel:
                    receptance(i - 1)
                if at(i, SPECIAL + 1):
                    sums_of_squares(1)
                    conv_in(i - 2)
                elif recur:
                    if at(i, B + 1):
                        hidden(1, 1)
                        rows_back(1, 0)
                    gates_in(i - 2)
                if at(i, SPECIAL):
                    hidden(0, 0)
                nc.scalar.preload_act_table_set(LOG_EXP)
                if now:
                    await_step(act, wkv, i, "den")
                    nc.scalar.activation(den[:], den[:], ACT.Ln).then_inc(wkv_act.sem, 1)
                    await_step(act, wkv_act, i, "ln")
                    nc.scalar.activation(den[:], den[:], ACT.Exp, scale=-1.0).then_inc(wkv_act.sem, 1)
                if at(i, SPECIAL):
                    experts(0)
                elif recur and not at(i, SPECIAL + 1):
                    decays(i - 2)
                if next_:
                    await_step(act, tr_in, i + 1, "t")
                    await_step(act, mix1, i, "r1")
                    norm_out(xn1, "ln1_w", "ln1_b", ev1)
                if at(i, SPECIAL + 1):
                    gates_in(i - 2)
                    nc.scalar.preload_act_table_set(LOG_EXP)
                    decays(i - 2)
                if recur:
                    root(i - 2)
                    if at(i, B):
                        hidden(1, 0)
                    if at(i, B + 1):
                        hidden(1, 2)
                        rows_back(1, 1)
                        act.wait_ge(y_stored, 16 * (NT + 3))
                    sums_of_squares(i - 2)
                if now:
                    await_step(act, tr_mid, i, "t")
                    await_step(act, mix2, i - 1, "r1")
                    norm_out(xn2, "ln2_w", "ln2_b", ev2)
                if at(i, SPECIAL):
                    conv_in(0)
                    keys(i + 1)
                    gates_in(0)
                    nc.scalar.preload_act_table_set(LOG_EXP)
                    decays(0)
                    root(0)
                    sums_of_squares(0)
                    conv_in(1)

            def hidden(f, t):
                act.wait_ge(up_done, t + (1 + f * NT))
                if f or not isinstance(t, int):
                    act.wait_ge(hid_t, t + f * NT)
                nc.scalar.activation(tile_rows[f], psum[:, 2:4, :].rearrange("p a t -> p (a t)"),
                                     ACT.Gelu).then_inc(gelu_done, 1)

            def rows_back(f, t):
                base = f * NT
                act.wait_ge(tiles_done, t + (2 + base))
                act.wait_ge(y_stored, (t + (1 + base)) * 16)
                nc.scalar.activation(ys[:], psum[:, 1, 0:D], ACT.Copy).then_inc(y_out, 1)
                act.wait_ge(y_out, t + (2 + base))
                dst = ys_rows[t * P:(t + 1) * P, :] if isinstance(t, int) else ys_rows[bass.DynSlice(t * P, P), :]
                act.dma_start(dst, ys[:]).then_inc(y_stored, 16)

            def experts(f):
                with act.Fori(3 if f else 1, NT) as t:
                    hidden(f, t)
                    rows_back(f, t - 1)
                rows_back(f, NT - 1)

            turns(act, turn)
            experts(1)

        @block.tensor
        def _(pe):
            pe.wait_ge(consts_made, 12)

            def transposes(src, st):
                for c in range(DC):
                    for k in range(TC):
                        last = nc.tensor.transpose(bank_t[:, c, k * P:(k + 1) * P], src[:, k, c * P:(c + 1) * P], ident[:])
                last.then_inc(st.sem, 1)

            def columns(dst, w, m, src, st):
                for c in range(DC):
                    last = nc.tensor.matmul(dst, w[:, c, m * P:(m + 1) * P], src[:, c, :], start=c == 0, stop=c == DC - 1)
                last.then_inc(st.sem, 1)

            def columns_split(dst, w, m, src, st):
                terms = [(c, a, b) for a, b in ((0, 0), (0, 1), (1, 0)) for c in range(DC)]
                for n, (c, a, b) in enumerate(terms):
                    last = nc.tensor.matmul(dst, w[a][:, c, m * P:(m + 1) * P], src[b][:, c, :], start=n == 0,
                                            stop=n == len(terms) - 1)
                last.then_inc(st.sem, 1)

            def rows(dst, src, w, chunks, st, tokens=range(TC)):
                for k in tokens:
                    for c in range(chunks):
                        last = nc.tensor.matmul(dst[:, k, :], src[:, c, k * P:(k + 1) * P], w[:, c, :],
                                                start=c == 0, stop=c == chunks - 1)
                last.then_inc(st.sem, 1)

            def turn(i):
                if at(i, SPECIAL + 1):
                    gate_products(1)
                elif has(i, 0, 0, B - 1):
                    keys(i)
                if has(i, -2, NB, B - 1) and not at(i, SPECIAL + 1):
                    transposes_rec(i - 2, i - 1)
                if has(i, -1, 0, B - 1):
                    await_step(pe, mix2, i - 1, "lo")
                    if at(i, 1):
                        pe.wait_ge(split_los, 2)
                    await_step(pe, gates_out, -1 if isinstance(i, int) and i <= SPECIAL else i - 3, "i1")
                    for j in range(FC):
                        if j < 4:
                            await_step(pe, kvr_out, i, ("v0", "v1", "r0", "r1")[j])
                        else:
                            await_step(pe, relu, i - 1, f"f{j - 4}")
                        columns_split(ring[(j + 2) % 4], fwk, j, xfk, fk)
                    await_step(pe, mix2, i - 1, "r1")
                    await_step(pe, relu, i - 1, f"f{FC - 3}")
                    rows(fr4, xfr, fwr, DC, fr)
                if at(i, SPECIAL + 1):
                    rec_products(1, i - 2)
                    transposes_rec(i - 2, i - 1)
                if at(i, SPECIAL):
                    experts(0)
                elif has(i, -2, NB, B - 1) and not at(i, SPECIAL + 1):
                    if at(i, B + 1):
                        await_step(pe, ev3, B - 1, "c1")
                        tile_in(1, 1)
                        up(1, 1, expert_of(1))
                        down(1, 0)
                        pe.wait_ge(gelu_done, NT + 2)
                        pe.wait_ge(hidt_ready, NT + 1)
                    gate_products(i - 2)
                    if at(i, B):
                        tile_in(1, 0)
                    if at(i, B + 1):
                        await_step(pe, gates_out, B - 1, "i1")
                        turn_hidden(1, 1)
                        tile_in(1, 2)
                        up(1, 2, expert_of(2))
                        down(1, 1)
                if at(i, 1):
                    await_step(pe, route, 0, "ni")
                    await_step(pe, ev1, 1, "e1")
                    await_step(pe, ev2, 0, "e1")
                    nc.tensor.matmul(psum[0:E, 0, 0:1], before, ntiles, start=True, stop=True)
                    nc.tensor.matmul(psum[0:E, 0, 1:2], upto, ntiles, start=True, stop=True)
                    nc.tensor.matmul(psum[0:1, 0, 2:2 + E], ntiles, upto, start=True, stop=True).then_inc(route_pe.sem, 1)
                    await_step(pe, route, 0, "pos")
                    by_token = rank.rearrange("e (c p k) -> e c k p", p=P, k=TOPK)
                    for c in range(NCH):
                        for k in range(TOPK):
                            n = 16 + c * TOPK + k
                            last = nc.tensor.matmul(psum[:, 0, n:n + 1], by_token[:, c, k, :], ones_e[:, 0:1],
                                                    start=True, stop=True)
                    last.then_inc(route_pe.sem, 1)
                    await_step(pe, route, 0, "past")
                    nc.tensor.matmul(psum[0:1, 0, 40:40 + NT], ones_e[:, 0:1], past, start=True, stop=True)\
                        .then_inc(route_pe.sem, 1)
                if has(i, 1, 0, B - 1):
                    await_step(pe, hat1, i + 1, f"h{TC - 1}")
                    await_step(pe, ev2, i - 1, "e1")
                    await_step(pe, ev3, -1 if isinstance(i, int) and i <= SPECIAL else i - 2, "c1")
                    if at(i, 1):
                        await_step(pe, route, 0, "slot")
                    transposes(xhat[0], tr_in)
                if has(i, -1, 0, B - 1):
                    await_step(pe, sq, i - 1, f"f{FC - 1}")
                    await_step(pe, fin, -1 if at(i, SPECIAL) else i - 3, f"f{TC - 1}")
                    rows(rows4, hid, fwv, FC, fv, range(TC // 2))
                if has(i, 0, 0, B - 1):
                    await_step(pe, wkv, i, "out")
                    await_step(pe, fr_out, i - 1, "s")
                    await_step(pe, kvr_out, i, "v1")
                    await_step(pe, gates_out, 1 if at(i, SPECIAL + 1) else -1 if isinstance(i, int) and i < NB + 2 else i - 2, "i1")
                    rows(fr4, mixed, wo, DC, proj)
                if at(i, SPECIAL + 1):
                    await_step(pe, zsum, i, "z")
                    gate_products(i - 2)
                if at(i, B):
                    await_step(pe, gates_out, B - 2, "i1")
                    up(1, 0, expert_of(0))
                if has(i, -1, 0, B - 1):
                    rows(rows4, hid, fwv, FC, fv, range(TC // 2, TC))
                if has(i, -2, NB, B - 1):
                    rec_products(i - 2, i - 1)
                if at(i, B):
                    turn_hidden(1, 0)
                if has(i, 0, 0, B - 1):
                    await_step(pe, hat2, i, f"h{TC - 1}")
                    await_step(pe, ev1, i + 1, "e1")
                    await_step(pe, ev3, -1 if isinstance(i, int) and i <= SPECIAL else i - 2, "c1")
                    transposes(xhat[1], tr_mid)
                if at(i, SPECIAL):
                    transposes_rec(0, i)
                    keys(i + 1)
                    gate_products(0)
                    rec_products(0, i - 1)
                    transposes_rec(1, i)

            def keys(b):
                if at(b, 0):
                    pe.wait_ge(weights_loaded, 13 * 16)
                await_step(pe, relu, b - 2, f"f{FC - 1}")
                await_step(pe, fr_out, b - 2, "s")
                await_step(pe, zsum, b - 1, "z")
                await_step(pe, gates_out, -1 if isinstance(b, int) and b <= SPECIAL + 1 else b - 3, "i1")
                for n, (name, w, src) in enumerate((("k", wk, xk), ("v", wv, xv), ("r", wr, xr))):
                    await_step(pe, mix1, b, f"{name}{DC - 1}")
                    for c in range(DC):
                        if name == "r":
                            await_step(pe, kvr_out, b, f"k{c}")
                        columns(ring[(2 * n + c) % 4], w, c, src, kvr)

            def transposes_rec(b, mid):
                await_step(pe, hat3, b, f"h{TC - 1}")
                await_step(pe, ev2, mid, "e1")
                await_step(pe, ev3, b - 1, "c1")
                transposes(xhat[2], tr_rec)

            def gate_products(b):
                await_step(pe, conv, b, "lo")
                await_step(pe, gates_out, b - 1, "i1")
                if at(b, 0):
                    await_step(pe, kvr_out, SPECIAL + 1, "r1")
                elif not at(b, 1):
                    await_step(pe, relu, b + 1, f"f{FC - 1}")
                for n in range(2):
                    if n and not (isinstance(b, int) and b < NB):
                        await_step(pe, fr_out, b + 1, "s")
                    for c in range(DC):
                        columns_split(ring[2 * n + c], [w[:, n] for w in gw], c, cv_parts, gates)

            def rec_products(b, channel):
                await_step(pe, rec, b, "h1")
                await_step(pe, fin, b - 1, f"f{TC - 1}")
                for half, name in enumerate(("a", "g")):
                    await_step(pe, comb, channel, name)
                    rows(rows4, hs, gwo, DC, rproj, range(half * TC // 2, (half + 1) * TC // 2))

            def tile_in(f, t):
                pe.wait_ge(gathered, (t + (1 + f * NT)) * 16)
                for c in range(DC):
                    last = nc.tensor.transpose(psum[:, 0, c * P:(c + 1) * P], xs[:, c * P:(c + 1) * P], ident[:])
                last.then_inc(xs_t, 1)

            def expert_of(t):
                return pe.value_load(table[0:1, bass.DynSlice(t, 1)], min_val=0, max_val=E - 1)

            def up(f, t, e):
                pe.wait_ge(xst_ready, t + (1 + f * NT))
                pe.wait_ge(expert_ready, e + (1 + f * E))
                for h in range(FF // T):
                    for c in range(DC):
                        w = expert_sets[f][:, bass.DynSlice(e % 2, 1), c * FF + h * T:c * FF + (h + 1) * T]
                        last = nc.tensor.matmul(psum[:, 2 + h, :], xst[:, c, :], w.rearrange("p a n -> p (a n)"),
                                                start=c == 0, stop=c == DC - 1)
                last.then_inc(up_done, 1)

            def turn_hidden(f, t):
                pe.wait_ge(gelu_done, t + (1 + f * NT))
                for j in range(FC):
                    last = nc.tensor.transpose(psum[:, 4 + j // 4, (j % 4) * P:(j % 4 + 1) * P],
                                               tile_rows[f][:, j * P:(j + 1) * P], ident[:])
                last.then_inc(hid_t, 1)

            def down(f, t):
                pe.wait_ge(hidt_ready, t + (1 + f * NT))
                pe.wait_ge(y_out, t + (1 + f * NT))
                e = pe.value_load(table[0:1, bass.DynSlice(t, 1)], min_val=0, max_val=E - 1)
                for j in range(FC):
                    w = expert_sets[f][:, bass.DynSlice(e % 2, 1), DC * FF + j * D:DC * FF + (j + 1) * D]
                    last = nc.tensor.matmul(psum[:, 1, 0:D], tile_cols[f][:, j, :], w.rearrange("p a n -> p (a n)"),
                                            start=j == 0, stop=j == FC - 1)
                last.then_inc(tiles_done, 1)

            def experts(f):
                base = f * NT
                if f == 0:
                    await_step(pe, ev1, SPECIAL, "e1")
                    await_step(pe, ev2, SPECIAL - 1, "e1")
                    await_step(pe, zsum, SPECIAL - 1, "z")
                    await_step(pe, relu, SPECIAL - 1, f"f{FC - 1}")
                    await_step(pe, fr_out, SPECIAL - 1, "s")
                    await_step(pe, comb, SPECIAL - 2, "x")
                    await_step(pe, route, 0, "tab1")
                    tile_in(f, 0)
                    up(f, 0, expert_of(0))
                with pe.Fori(3 if f else 1, NT) as t:
                    e = expert_of(t)
                    tile_in(f, t)
                    turn_hidden(f, t - 1)
                    up(f, t, e)
                    down(f, t - 1)
                turn_hidden(f, NT - 1)
                down(f, NT - 1)
                pe.wait_ge(y_out, NT + 1 + base)
                pe.wait_ge(hidt_ready, NT + base)

            turns(pe, turn)
            experts(1)

        @block.vector
        def _(dve):
            def log_of_sigmoid():
                x_, (s_, s2, p, t) = vec[:, COL["log_a"]:COL["log_a"] + DC], [b_[:] for b_ in la]
                done = [0]

                def step(ins):
                    ins.then_inc(log_steps, 1)
                    done[0] += 1
                    dve.wait_ge(log_steps, done[0])

                dve.wait_ge(consts_loaded, 16)
                step(nc.vector.scalar_tensor_tensor(t, x_, -1.0, x_, ALU.mult, ALU.min))
                dve.wait_ge(exp_made, 1)
                step(nc.vector.tensor_scalar(t, s_, 2.0, None, ALU.add))
                step(nc.vector.reciprocal(t, t))
                step(nc.vector.tensor_tensor(s_, s_, t, ALU.mult))
                step(nc.vector.tensor_tensor(s2, s_, s_, ALU.mult))
                step(nc.vector.tensor_scalar(p, s2, 1.0 / LOG_TERMS[0], None, ALU.mult))
                for n in LOG_TERMS[1:]:
                    step(nc.vector.scalar_tensor_tensor(p, p, 1.0 / n, s2, ALU.add, ALU.mult))
                step(nc.vector.scalar_tensor_tensor(p, p, 1.0, s_, ALU.add, ALU.mult))
                step(nc.vector.tensor_scalar(t, x_, 0.0, 8.0, ALU.min, ALU.mult))
                step(nc.vector.scalar_tensor_tensor(log_a8[:], p, -16.0, t, ALU.mult, ALU.add))
                assert done[0] == LOG_STEPS

            for buf in (xn1, xn2, alpha, beta):
                nc.vector.memset(buf[:, :, 0:1], 0.0).then_inc(cols_made, 1)
            nc.vector.memset(top[:, :, 0:1], -1e30).then_inc(cols_made, 1)
            dve.wait_ge(vec_made, 2)
            log_of_sigmoid()

            def norm_stats(src, n, st, b, chunks):
                for c in range(chunks):
                    nc.vector.bn_stats(stats[n][:, c, :], src[:, c, :]).then_inc(st.sem, 1)
                await_apart(dve, st.sem, st.count(b, f"st{chunks - 1}"))
                for c in range(chunks):
                    nc.vector.bn_aggr(moments[n][:, c, :], stats[n][:, c, :]).then_inc(st.sem, 1)
                await_step(dve, st, b, f"ag{chunks - 1}")
                nc.vector.tensor_scalar(negmean[n][:, 0:chunks], moments[n][:, 0:chunks, 0], -1.0, None, ALU.mult)\
                    .then_inc(st.sem, 1)
                nc.vector.tensor_scalar(varis[n][:, 0:chunks], moments[n][:, 0:chunks, 1], EPS, None, ALU.add)\
                    .then_inc(st.sem, 1)

            def mix(src, st, b, outs):
                nc.vector.tensor_tensor(diff, src[:, :, 1:T + 1], src[:, :, 0:T], ALU.subtract).then_inc(st.sem, 1)
                await_step(dve, st, b, "d")
                for dst, m in outs:
                    mixed_part(src, st, dst, m)

            def mixed_part(src, st, dst, m):
                for c in range(DC):
                    nc.vector.scalar_tensor_tensor(dst[:, c, :], diff[:, c, :], col(m, c), src[:, c, 0:T],
                                                   ALU.mult, ALU.add).then_inc(st.sem, 1)

            def split(src, parts, st, b, name):
                await_step(dve, st, b, name)
                nc.vector.tensor_copy(parts[0][:, :, :], src).then_inc(st.sem, 1)
                await_step(dve, st, b, "hi")
                nc.vector.tensor_tensor(parts[1][:, :, :], src, parts[0][:, :, :].bitcast(F32), ALU.subtract).then_inc(st.sem, 1)

            def mix_first(b):
                await_step(dve, ev1, b, "e1")
                await_step(dve, kvr, b - 1, "r1")
                await_step(dve, wkv, b - 1, "out")
                mix(xn1, mix1, b, ((xk, "mix_k"), (xv, "mix_v"), (xr, "mix_r")))

            def mix_second(b):
                await_step(dve, ev2, b, "e1")
                await_step(dve, fr, b - 1, "f")
                mix(xn2, mix2, b, ((xfk_whole, "fmix_k"),))
                split(xfk_whole, xfk, mix2, b, "k1")
                mixed_part(xn2, mix2, xfr, "fmix_r")

            def weights_of(b):
                was = top[:, :, 0:T]
                for c in range(DC):
                    await_step(dve, kvr_out, b, f"k{c}")
                    nc.vector.tensor_tensor_scan(top[:, c, 1:T + 1], decay[:, c:c + 1].to_broadcast([P, T]), kc[:, c, :],
                                                 -1e30, ALU.add, ALU.max).then_inc(wkv.sem, 1)
                for c in range(DC):
                    await_step(dve, wkv, b, f"m{c}")
                    nc.vector.scalar_tensor_tensor(g[:, c, :], kc[:, c, :], col("first", c), was[:, c, :],
                                                   ALU.add, ALU.subtract).then_inc(wkv.sem, 1)
                await_step(dve, wkv, b, "q1")
                nc.vector.tensor_scalar(g[:], g[:], LOGIT_CAP, None, ALU.min).then_inc(wkv.sem, 1)
                for c in range(DC):
                    nc.vector.scalar_tensor_tensor(dec[:, 0, c, :], was[:, c, :], decay[:, c:c + 1], top[:, c, 1:T + 1],
                                                   ALU.add, ALU.subtract).then_inc(wkv.sem, 1)
                nc.vector.tensor_tensor(dec[:, 1], kc[:], top[:, :, 1:T + 1], ALU.subtract).then_inc(wkv.sem, 1)

            def sums(b):
                await_step(dve, wkv_act, b, "dec")
                for c in range(DC):
                    nc.vector.tensor_tensor_scan(beta[:, c, 1:T + 1], dec[:, 0, c, :], dec[:, 1, c, :], 0.0,
                                                 ALU.mult, ALU.add).then_inc(wkv.sem, 1)
                await_step(dve, wkv, b, "b1")
                await_step(dve, kvr_out, b, "v1")
                nc.vector.tensor_tensor(dv, dec[:, 1], vc[:], ALU.mult).then_inc(wkv.sem, 1)
                await_step(dve, wkv, b, "dv")
                for c in range(DC):
                    nc.vector.tensor_tensor_scan(alpha[:, c, 1:T + 1], dec[:, 0, c, :], dv[:, c, :], 0.0,
                                                 ALU.mult, ALU.add).then_inc(wkv.sem, 1)

            def quotient(b):
                await_step(dve, wkv, b, "a1")
                await_step(dve, wkv_gv, b, "gv")
                nc.vector.tensor_tensor(num, alpha[:, :, 0:T], gv[:], ALU.add).then_inc(wkv.sem, 1)
                nc.vector.tensor_tensor(den[:], beta[:, :, 0:T], g[:], ALU.add).then_inc(wkv.sem, 1)

            def gated(b):
                await_step(dve, wkv_act, b, "inv")
                await_step(dve, kvr_out, b, "r1")
                nc.vector.tensor_tensor(den[:], den[:], sr[:], ALU.mult).then_inc(wkv.sem, 1)
                await_step(dve, wkv, b, "gate")
                nc.vector.tensor_tensor(mixed[:], den[:], num, ALU.mult).then_inc(wkv.sem, 1)

            def convolve(s):
                await_step(dve, ev3, s, "c1")
                for j in (2, 1, 0):
                    for c in range(DC):
                        if j < 2:
                            await_step(dve, conv, s, f"c{j + 1}{c}")
                        nc.vector.scalar_tensor_tensor(cv[:, c, :], xc[:, c, j:j + T], col(f"conv{j}", c), cv[:, c, :],
                                                       ALU.mult, ALU.add).then_inc(conv.sem, 1)
                await_step(dve, rec, s - 1, "b")
                await_step(dve, rproj, s - 1, "o")
                split(cv, cv_parts, conv, s, "c01")

            def scales(s):
                await_step(dve, gates_out, s, "a1")
                nc.vector.scalar_tensor_tensor(om[:], aa[:], -1.0, aa[:], ALU.mult, ALU.mult).then_inc(rec.sem, 1)
                await_step(dve, rec, s, "na")
                nc.vector.tensor_scalar(om[:], om[:], 1.0, TINY, ALU.add, ALU.max).then_inc(rec.sem, 1)

            def recur(s):
                await_step(dve, gates_out, s, "sc")
                await_step(dve, gin, s, "in")
                nc.vector.tensor_tensor(ig[:], ig[:], om[:], ALU.mult).then_inc(rec.sem, 1)
                await_step(dve, rec, s, "b")
                await_step(dve, rproj, s - 1, "o")
                for c in range(DC):
                    nc.vector.tensor_tensor_scan(hs[:, c, :], aa[:, c, :], ig[:, c, :], 0.0, ALU.mult, ALU.add)\
                        .then_inc(rec.sem, 1)

            def route_first():
                dve.wait_ge(idx_loaded, 16)
                nc.vector.tensor_copy(rank, asg_i).then_inc(route.sem, 1)
                await_step(dve, route, 0, "idx")
                nc.vector.tensor_scalar(onehot, rank, expert_id, None, ALU.is_equal).then_inc(route.sem, 1)
                await_step(dve, route, 0, "one")
                nc.vector.tensor_tensor_scan(rank, ones_e[:, 0:1].to_broadcast([E, NASG]), onehot, 0.0,
                                             ALU.mult, ALU.add).then_inc(route.sem, 1)
                await_step(dve, route, 0, "rank")
                nc.vector.tensor_scalar(ntiles_i[:, 0:1], rank[:, NASG - 1:NASG], float(P - 1), None, ALU.add)\
                    .then_inc(route.sem, 1)
                await_step(dve, route, 0, "n")
                nc.vector.tensor_scalar(ntiles_i[:, 1:2], ntiles_i[:, 0:1], P.bit_length() - 1, None,
                                        ALU.logical_shift_right).then_inc(route.sem, 1)
                await_step(dve, route, 0, "nf")
                nc.vector.tensor_copy(ntiles, ntiles_i[:, 1:2]).then_inc(route.sem, 1)

            def route_second():
                await_step(dve, route_pe, 0, "ends")
                nc.vector.tensor_scalar(starts, psum[0:E, 0, 0:1], float(P), -1.0, ALU.mult, ALU.add).then_inc(route.sem, 1)
                nc.vector.tensor_copy(ends, psum[0:E, 0, 1:2]).then_inc(route.sem, 1)
                nc.vector.tensor_copy(table[0:1, NT:NT + E], psum[0:1, 0, 2:2 + E]).then_inc(route.sem, 1)
                await_step(dve, route, 0, "end")
                nc.vector.scalar_tensor_tensor(rank, rank, starts, onehot, ALU.add, ALU.mult).then_inc(route.sem, 1)
                nc.vector.tensor_scalar(past, tile_no, ends, None, ALU.is_ge).then_inc(route.sem, 1)
                await_step(dve, route_pe, 0, "experts")
                nc.vector.tensor_scalar(table[0:1, 0:NT], psum[0:1, 0, 40:40 + NT], float(E - 1), None, ALU.min)\
                    .then_inc(route.sem, 1)
                nc.vector.tensor_copy(slot_i[:], psum[:, 0, 16:16 + NCH * TOPK]).then_inc(route.sem, 1)

            def combine(b):
                await_step(dve, fr_out, b, "s")
                for half, name in enumerate(("a", "v")):
                    part = slice(half * TC // 2, (half + 1) * TC // 2)
                    await_step(dve, fv, b, name)
                    nc.vector.tensor_tensor(sf[:, part, :], rows4[:, part, :], sf[:, part, :], ALU.mult).then_inc(comb.sem, 1)
                await_step(dve, comb, b, "g")
                await_step(dve, keep_xz, b, "xz")
                if not isinstance(b, int) or b > NB:
                    await_step(dve, keep_x2, b - 1, "x2b")
                    await_step(dve, hat3, b - 1, f"h{TC - 1}")
                nc.vector.tensor_tensor(rows_of(b), sf[:], xz[:], ALU.add).then_inc(comb.sem, 1)

            def third_stats(b):
                if isinstance(b, int) and b < NB:
                    await_step(dve, merged, 0, f"q{TC * (b + 1) - 1}")
                else:
                    await_step(dve, comb, b, "x")
                await_step(dve, hat3, b - 1, f"h{TC - 1}")
                norm_stats(rows_of(b), 2, ln3, b, TC)

            def finish(b):
                await_step(dve, sumsq, b, f"s{TC - 1}")
                nc.vector.tensor_scalar(msq[:], ssq[:], 1.0 / D, EPS_RMS, ALU.mult, ALU.add).then_inc(fin.sem, 1)
                await_step(dve, fin_pow, b, "p")
                await_step(dve, res, b - 1, "o")
                early = isinstance(b, int) and b < NB
                if not early and not at(b, NB):
                    dve.wait_ge(out_stored, (b - NB) * 16)
                for c in range(TC):
                    nc.vector.scalar_tensor_tensor(fo[:, c, :], rows4[:, c, :], rms[:, c:c + 1], gamma[:],
                                                   ALU.mult, ALU.mult).then_inc(fin.sem, 1)

            def turn(i):
                now, next_, channel, recurs = (has(i, 0, 0, B - 1), has(i, 1, 0, B - 1), has(i, -1, 0, B - 1),
                                               has(i, -2, NB, B - 1))
                if at(i, SPECIAL):
                    experts_norm(0)
                if channel and not at(i, SPECIAL + 1):
                    mix_second(i - 1)
                if at(i, SPECIAL):
                    experts_rows(0)
                if now:
                    weights_of(i)
                if at(i, SPECIAL + 1):
                    scales(1)
                elif recurs:
                    if at(i, B + 1):
                        tile_columns(1, 1)
                    convolve(i - 2)
                if at(i, B - 1):
                    experts_norm(1)
                if at(i, B):
                    experts_rows(1)
                    tile_columns(1, 0)
                if at(i, B + 1):
                    hidden_columns(1, 1)
                    tile_columns(1, 2)
                if now:
                    sums(i)
                if at(i, SPECIAL + 1):
                    recur(1)
                if next_:
                    dve.wait_ge(x_loaded, (i + 2) * 16)
                    await_step(dve, keep_y, i, "xb")
                    norm_stats(x_in, 0, ln1, i + 1, TC)
                    await_step(dve, ln1, i + 1, "v0")
                    nc.vector.tensor_scalar(varis[0][:, TC:2 * TC], moments[0][:, 0:TC, 1], 1.0 + EPS, EPS * EPS,
                                            ALU.mult, ALU.add).then_inc(ln1.sem, 1)
                if at(i, -1):
                    route_first()
                if at(i, 1):
                    route_second()
                if at(i, SPECIAL):
                    tile_columns(0, 0)
                if now:
                    quotient(i)
                if at(i, SPECIAL + 1):
                    finish(1)
                    convolve(i - 2)
                if now:
                    gated(i)
                if at(i, SPECIAL):
                    experts(0)
                if recurs and not at(i, SPECIAL + 1):
                    scales(i - 2)
                if next_:
                    mix_first(i + 1)
                if now:
                    await_step(dve, proj, i, "o")
                    await_step(dve, keep_y, i, "xb")
                    nc.vector.tensor_tensor(z[:], fr4, y[:], ALU.add).then_inc(zsum.sem, 1)
                    await_step(dve, zsum, i, "z")
                    await_step(dve, hat2, i - 1, f"h{TC - 1}")
                    norm_stats(z, 1, ln2, i, TC)
                if at(i, SPECIAL + 1):
                    scales(i - 2)
                if recurs:
                    recur(i - 2)
                if channel and not at(i, SPECIAL):
                    combine(i - 1)
                if at(i, SPECIAL):
                    merge(0, 0)
                    third_stats(0)
                    combine(i - 1)
                    merge(0, 1)
                    convolve(0)
                    third_stats(1)
                    mix_second(i)
                    scales(0)
                    recur(0)
                    finish(0)
                if has(i, -1, NB, B - 1):
                    third_stats(i - 1)
                if at(i, B):
                    hidden_columns(1, 0)
                if recurs:
                    finish(i - 2)
                if at(i, SPECIAL):
                    convolve(1)

            def experts_norm(f):
                if f:
                    await_step(dve, res, 1, "o")
                else:
                    await_step(dve, comb, NB - 1, "x")
                norm_stats(xf, 3, lnf, f, NCH)

            def experts_rows(f):
                if f:
                    await_step(dve, mix2, B - 1, "r1")
                dve.wait_ge(powf, f + 1)
                for c in range(NCH):
                    nc.vector.tensor_scalar(xfn[f][:, c, :], xf[:, c, :], negmean[3][:, c:c + 1], rstd[3][:, c:c + 1],
                                            ALU.add, ALU.mult).then_inc(hatf.sem, 1)

            def tile_columns(f, t):
                base = f * NT
                dve.wait_ge(xs_t, t + (1 + base))
                if f or not isinstance(t, int):
                    dve.wait_ge(up_done, t + base)
                nc.vector.tensor_copy(xst[:].rearrange("p a n -> p (a n)"), psum[:, 0, 0:D]).then_inc(xst_ready, 1)

            def hidden_columns(f, t):
                base = f * NT
                dve.wait_ge(hid_t, t + (1 + base))
                dve.wait_ge(tiles_done, t + (1 + base))
                nc.vector.tensor_copy(tile_cols[f].rearrange("p j n -> p (j n)"), psum[:, 4:6, :].rearrange("p a t -> p (a t)"))\
                    .then_inc(hidt_ready, 1)

            def experts(f):
                base = f * NT
                with dve.Fori(3 if f else 1, NT) as t:
                    tile_columns(f, t)
                    hidden_columns(f, t - 1)
                hidden_columns(f, NT - 1)
                dve.wait_ge(tiles_done, NT + 1 + base)
                if f == 0:
                    nc.vector.memset(xc[:, :, 0:3], 0.0).then_inc(cols_made, 1)

            def merge(f, b):
                for c in range(TC * b, TC * (b + 1)):
                    nc.vector.tensor_tensor(xf[:, c, :], xf[:, c, :], bias[:], ALU.add).then_inc(merged.sem, 1)
                    dve.wait_ge(picks[c], 16 * TOPK * (f + 1))
                    for k, name in enumerate(("b", "p")):
                        await_step(dve, merged, f, f"{name}{c}")
                        nc.vector.scalar_tensor_tensor(xf[:, c, :], picked[:, c, k, :], choice_w[:, c, k:k + 1], xf[:, c, :],
                                                       ALU.mult, ALU.add).then_inc(merged.sem, 1)

            turns(dve, turn)
            experts(1)
            for b in range(NB):
                merge(1, b)


def kernel(**inputs):
    import numpy as np
    import concourse.bacc as bacc
    from concourse.bass_utils import run_bass_kernel_spmd

    def given(name):
        return np.asarray(inputs[name])

    a, b = "L0_attn_a_", "L0_attn_b_"
    conv_w = given(b + "conv_w")
    vectors = [given(a + "ln1_w"), given(a + "ln1_b"), given(a + "ln2_w"), given(a + "ln2_b"),
               given(a + "time_decay"), given(a + "time_first"), given(a + "time_mix_k").reshape(-1),
               given(a + "time_mix_v").reshape(-1), given(a + "time_mix_r").reshape(-1),
               given(a + "f_time_mix_k").reshape(-1), given(a + "f_time_mix_r").reshape(-1),
               given(b + "conv_b"), given(b + "b_r"), given(b + "b_i"), given(b + "log_a")]
    vectors += [conv_w[:, 0, j] for j in range(4)]
    packed = np.concatenate([v.reshape(2, 128).T for v in vectors], axis=1)
    arrays = {
        "x": given(a + "x"), "vecs": packed, "bias": given("L0_ffn_bias"), "gamma": given(b + "gamma"),
        "w_key": given(a + "w_key"), "w_value": given(a + "w_value"), "w_recept": given(a + "w_recept"),
        "w_output": given(a + "w_output"), "f_w_key": given(a + "f_w_key"), "f_w_recept": given(a + "f_w_recept"),
        "f_w_value": given(a + "f_w_value"), "w_r_t": given(b + "W_r").T, "w_i_t": given(b + "W_i").T,
        "w_out_t": given(b + "W_out").T, "expert_weights": given("L0_ffn_expert_weights"),
        "expert_indices": given("L0_ffn_expert_indices"), "w1": given("L0_ffn_w1"), "w2": given("L0_ffn_w2"),
    }
    arrays = {name: np.ascontiguousarray(v) for name, v in arrays.items()}
    nc = bacc.Bacc("TRN2", target_bir_lowering=False, num_devices=1)
    args = [nc.dram_tensor("in_" + name, v.shape, mybir.dt.from_np(v.dtype), kind="ExternalInput").ap()
            for name, v in arrays.items()]
    out = nc.dram_tensor("out", (B, T, D), F32, kind="ExternalOutput").ap()
    hybrid_kernel(nc, *args, out)
    r = run_bass_kernel_spmd(nc, [{"in_" + name: v for name, v in arrays.items()}], core_ids=[0])
    return r.results[0]["out"]
```

```python
import concourse.bass as bass
from concourse import mybir
from contextlib import ExitStack

F32 = mybir.dt.float32
F32R = mybir.dt.float32r
I32 = mybir.dt.int32
ALU = mybir.AluOpType
ACT = mybir.ActivationFunctionType

B, T, D = 16, 512, 256
P = 128
DC = D // P
TC = T // P
FF = 1024
FC = FF // P
E, TOPK = 8, 2
NB = 2
NTOK = NB * T
NASG = NTOK * TOPK
NCH = NTOK // P
NT = NASG // P + E - 1
EPS = 1e-5
EPS_RMS = 1e-6
LOGIT_CAP = 40.0
TINY = 2.0 ** -60
SPECIAL = 3
FIRST, LAST = 6, 13

LOG_TERMS = range(15, 1, -2)
LOG_STEPS = 6 + len(LOG_TERMS) - 1 + 3

VECS = ["ln1_w", "ln1_b", "ln2_w", "ln2_b", "decay", "first", "mix_k", "mix_v", "mix_r", "fmix_k", "fmix_r",
        "conv_b", "b_r", "b_i", "log_a", "conv0", "conv1", "conv2", "conv3"]
COL = {name: DC * n for n, name in enumerate(VECS)}


class Steps:

    def __init__(self, sem, names, runs):
        self.sem, self.names, self.runs = sem, names, runs

    def count(self, run, name):
        return run * len(self.names) + self.names.index(name) + 1


def await_step(eng, steps, run, name):
    if isinstance(run, int):
        if run < 0:
            return
        run = min(run, steps.runs - 1)
    eng.wait_ge(steps.sem, steps.count(run, name))


def numbered(name, n):
    return [f"{name}{k}" for k in range(n)]


def hybrid_kernel(nc, x, vecs, bias_row, gamma_row, w_key, w_value, w_recept, w_output, f_w_key, f_w_recept,
                  f_w_value, w_r_t, w_i_t, w_out_t, expert_weights, expert_indices, w1, w2, out):
    ctx = ExitStack()
    with ctx:
        def sb(name, shape, dt=F32):
            return ctx.enter_context(nc.sbuf_tensor(name, shape, dt))

        def sem(name):
            return ctx.enter_context(nc.semaphore(name))

        def steps(name, names, runs):
            return Steps(sem(name), names, runs)

        ident = sb("ident", [P, P])
        half_neg = sb("half_neg", [P, 8])
        vec = sb("vec", [P, DC * len(VECS)])
        decay = sb("decay", [P, DC])
        log_a8 = sb("log_a8", [P, DC])
        euler = sb("euler", [P, DC])
        la = [sb(f"la{n}", [P, DC]) for n in range(4)]
        gamma = sb("gamma", [P, D])
        bias = sb("bias", [P, D])
        wk = sb("wk", [P, DC, D])
        wv = sb("wv", [P, DC, D])
        wr = sb("wr", [P, DC, D])
        wo = sb("wo", [P, DC, D])
        fwk = [sb(f"fwk_{part}", [P, DC, FF], F32R) for part in ("hi", "lo")]
        fwr = sb("fwr", [P, DC, D])
        fwv = sb("fwv", [P, FC, D])
        gw = [sb(f"gw_{part}", [P, 2, DC, D], F32R) for part in ("hi", "lo")]
        gwo = sb("gwo", [P, DC, D])

        x_in = sb("x_in", [P, TC, D])
        y = sb("y", [P, TC, D])
        xb = sb("xb", [P, TC, D])
        z = y
        xz = sb("xz", [P, TC, D])
        x2_space = sb("x2_space", [P, 2, TC, D])
        x2 = x2_space[:, 0]
        x2b = x2_space[:, 1]
        xhat = [sb(f"xhat{n}", [P, TC, D]) for n in range(2)]
        xhat.append(xhat[0])
        stats = [sb(f"stats{n}", [P, (TC if n in (1, 2) else 2 * TC), 6]) for n in range(4)]
        moments = [sb(f"moments{n}", [P, (TC if n in (1, 2) else 2 * TC), 2]) for n in range(4)]
        negmean = [sb(f"negmean{n}", [P, (TC if n in (1, 2) else 2 * TC)]) for n in range(4)]
        varis = [sb(f"varis{n}", [P, (TC if n in (1, 2) else 2 * TC)]) for n in range(4)]
        rstd = [sb(f"rstd{n}", [P, (TC if n in (1, 2) else 2 * TC)]) for n in range(4)]

        def carver(space):
            place = [0]

            def carve(*shape):
                n = shape[0] * shape[1]
                part = space[:, place[0]:place[0] + n].rearrange("p (a b) -> p a b", a=shape[0])
                place[0] += n
                return part
            return carve

        mix_space = sb("mix_space", [P, 8 * DC * T])
        carve = carver(mix_space)
        xn1 = sb("xn1", [P, DC, T + 1])
        xn2 = sb("xn2", [P, DC, T + 1])
        xk = carve(DC, T)
        xv = carve(DC, T)
        xr = carve(DC, T)
        xfk_hi = sb("xfk_hi", [P, DC, T], F32R)
        kc = carve(DC, T)
        vc = carve(DC, T)
        sr = carve(DC, T)
        top = sb("top", [P, DC, T + 1])
        dec = sb("dec", [P, 2, DC, T])
        diff = dec[:, 0]
        xfk_whole = dec[:, 1]
        dv = dec[:, 1]
        num = dec[:, 0]
        g = carve(DC, T)
        xfr = carve(DC, T)
        alpha = sb("alpha", [P, DC, T + 1])
        beta = sb("beta", [P, DC, T + 1])
        gv = vc
        den = kc
        mixed = sr
        hid = sb("hid", [P, FC, T])
        sf = sb("sf", [P, TC, D])

        place_of_a = DC * (T + 3) + 3 * DC * T
        with nc.sbuf_tensor("lead", [P, place_of_a + DC * T], F32), \
             nc.sbuf_tensor("parts", [P, 3, DC, T], F32R) as parts:
            cv_parts = [parts[:, 0], parts[:, 1]]
            xfk = [xfk_hi, parts[:, 2]]
        space = sb("space", [P, place_of_a + 4 * DC * T])
        carve = carver(space)
        xc = carve(DC, T + 3)
        cv = carve(DC, T)
        rg = carve(DC, T)
        ig = carve(DC, T)
        aa = carve(DC, T)
        om = carve(DC, T)
        hs = carve(DC, T)
        fo = aa.rearrange("p a (b n) -> p (a b) n", n=D)
        fwk_whole = space[:, 0:DC * FF].rearrange("p (c n) -> p c n", c=DC)
        gw_whole = space[:, DC * FF:DC * FF + 2 * DC * D].rearrange("p (g c n) -> p g c n", g=2, c=DC)
        SET = DC * FF + FC * D
        expert_sets = [s_[:, 0:2 * SET].rearrange("p (s n) -> p s n", s=2) for s_ in (space, mix_space)]
        picked = space[:, place_of_a:place_of_a + NCH * TOPK * D].rearrange("p (c k n) -> p c k n", c=NCH, k=TOPK)
        ssq = sb("ssq", [P, TC])
        msq = sb("msq", [P, TC])
        rms = sb("rms", [P, TC])

        xf = sb("xf", [P, NCH, D])
        choice_w = sb("choice_w", [P, NCH, TOPK])
        slot_i = sb("slot_i", [P, NCH * TOPK], I32)
        token_id = sb("token_id", [P, NCH], I32)
        token_of_slot = sb("token_of_slot", [P, NT], I32)
        token_idx = sb("token_idx", [P, 1], I32)
        table = sb("table", [1, NT + E], I32)
        xs = sb("xs", [P, D])
        xst = sb("xst", [P, DC, P])
        ys = sb("ys", [P, D])
        square = ys
        lent = [x2_space[:].rearrange("p w a n -> p w (a n)"), dec[:].rearrange("p w a n -> p w (a n)")]
        tile_rows = [s_[:, 1] for s_ in lent]
        tile_cols = [s_[:, 0].rearrange("p (j n) -> p j n", n=P) for s_ in lent]
        xfn = [s_.rearrange("p w (c n) -> p (w c) n", n=D) for s_ in lent]

        psum = ctx.enter_context(nc.psum_tensor("psum", [P, 8, T], F32))
        bank_t = psum[:, 0:DC, :]
        ring = [psum[:, 2 + n, :] for n in range(4)]
        ring_rows = psum[:, 4:6, :]
        rows4 = psum[:, 6:8, :].rearrange("p a (b n) -> p (a b) n", n=D)
        fr4 = psum[:, 4:6, :].rearrange("p a (b n) -> p (a b) n", n=D)

        rank = space[0:E, place_of_a:place_of_a + NASG]
        onehot = x2_space[0:E].rearrange("p w c n -> p (w c n)")
        asg_i = onehot.bitcast(I32)
        note_at = [0]

        def note(n):
            note_at[0] += n
            return ys[0:E, note_at[0] - n:note_at[0]]

        ones_e, tile_no, past = note(NT), note(NT), note(NT)
        before = note(E)
        upto = note(E)
        expert_id, ntiles, ends, starts = note(1), note(1), note(1), note(1)
        ntiles_i = note(2).bitcast(I32)

        token_table = nc.dram_tensor("token_table", (NT * P, 1), I32, kind="Internal").ap()
        xf_rows = nc.dram_tensor("xf_rows", (NTOK, D), F32, kind="Internal").ap()
        ys_rows = nc.dram_tensor("ys_rows", (NT * P, D), F32, kind="Internal").ap()

        x_loaded = sem("x_loaded")
        passed = sem("passed")
        consts_loaded = sem("consts_loaded")
        consts_made = sem("consts_made")
        cols_made = sem("cols_made")
        split_his = sem("split_his")
        split_los = sem("split_los")
        weights_loaded = sem("weights_loaded")
        vec_made = sem("vec_made")
        log_steps = sem("log_steps")
        exp_made = sem("exp_made")
        out_stored = sem("out_stored")
        ln1 = steps("ln1", numbered("st", TC) + numbered("ag", TC) + ["neg", "v0", "v1"], B)
        ln2 = steps("ln2", numbered("st", TC) + numbered("ag", TC) + ["neg", "v0"], B)
        ln3 = steps("ln3", numbered("st", TC) + numbered("ag", TC) + ["neg", "v0"], B)
        hat1 = steps("hat1", ["pow"] + numbered("h", TC), B)
        hat2 = steps("hat2", ["pow"] + numbered("h", TC), B)
        hat3 = steps("hat3", ["pow"] + numbered("h", TC), B)
        tr_in = steps("tr_in", ["t"], B)
        tr_mid = steps("tr_mid", ["t"], B)
        tr_rec = steps("tr_rec", ["t"], B)
        ev1 = steps("ev1", numbered("e", DC), B)
        ev2 = steps("ev2", numbered("e", DC), B)
        ev3 = steps("ev3", numbered("x", DC) + numbered("c", DC), B)
        keep_y = steps("keep_y", numbered("y", TC) + ["xb"], B)
        keep_xz = steps("keep_xz", ["xz"], B)
        keep_x2 = steps("keep_x2", ["x2b"], B)
        mix1 = steps("mix1", ["d"] + numbered("k", DC) + numbered("v", DC) + numbered("r", DC), B)
        kvr = steps("kvr", numbered("k", DC) + numbered("v", DC) + numbered("r", DC), B)
        kvr_out = steps("kvr_out", numbered("k", DC) + numbered("v", DC) + numbered("r", DC), B)
        wkv = steps("wkv", ["m0", "m1", "q0", "q1", "cap", "z0", "z1", "in", "b0", "b1", "dv", "a0", "a1",
                            "num", "den", "gate", "out"], B)
        wkv_act = steps("wkv_act", ["g", "dec", "ln", "inv"], B)
        wkv_gv = steps("wkv_gv", ["gv"], B)
        proj = steps("proj", ["o"], B)
        zsum = steps("zsum", ["z"], B)
        mix2 = steps("mix2", ["d"] + numbered("k", DC) + ["hi", "lo"] + numbered("r", DC), B)
        fk = steps("fk", numbered("f", FC), B)
        relu = steps("relu", numbered("f", FC), B)
        sq = steps("sq", numbered("f", FC), B)
        fr = steps("fr", ["f"], B)
        fr_out = steps("fr_out", ["s"], B)
        fv = steps("fv", ["a", "v"], B)
        comb = steps("comb", ["a", "g", "x"], B)
        conv = steps("conv", [f"c{j}{c}" for j in (2, 1, 0) for c in range(DC)] + ["hi", "lo"], B)
        gates = steps("gates", numbered("r", DC) + numbered("i", DC), B)
        gates_out = steps("gates_out", numbered("r", DC) + numbered("i", DC) + numbered("a", DC) + ["ln", "sc"], B)
        gin = steps("gin", ["in", "b"], B)
        rec = steps("rec", ["na", "om", "h0", "h1"], B)
        rproj = steps("rproj", ["a", "o"], B)
        sumsq = steps("sumsq", numbered("s", TC), B)
        fin = steps("fin", ["ms"] + numbered("f", TC), B)
        fin_pow = steps("fin_pow", ["p"], B)
        res = steps("res", ["o"], B)

        route = steps("route", ["idx", "one", "rank", "n", "nf", "ni", "start", "end", "tab0", "pos", "past", "tab1",
                                "slot"], 1)
        route_pe = steps("route_pe", ["ends", "slots", "experts"], 1)
        idx_loaded = sem("idx_loaded")
        table_zeroed = sem("table_zeroed")
        table_written = sem("table_written")
        table_loaded = sem("table_loaded")
        lnf = steps("lnf", numbered("st", NCH) + numbered("ag", NCH) + ["neg", "v0"], 2)
        experts_rstd = sem("experts_rstd")
        experts_hat = steps("experts_hat", numbered("h", NCH), 2)
        xf_stored = sem("xf_stored")
        expert_loaded = [sem(f"expert_loaded{n}") for n in range(2)]
        expert_ready = sem("expert_ready")
        idx_copied = sem("idx_copied")
        gathered = sem("gathered")
        xs_t = sem("xs_t")
        xst_ready = sem("xst_ready")
        up_done = sem("up_done")
        gelu_done = sem("gelu_done")
        hid_t = sem("hid_t")
        hidt_ready = sem("hidt_ready")
        tiles_done = sem("tiles_done")
        y_out = sem("y_out")
        y_stored = sem("y_stored")
        picks = [sem(f"picks{c}") for c in range(NCH)]
        merged = steps("merged", [f"{n}{c}" for c in range(NCH) for n in ("b", "p", "q")], 2)

        block = ctx.enter_context(nc.Block())

        def wide(ap, n):
            return ap[:].unsqueeze(1).to_broadcast([P, n, D])

        def col(name, c):
            return vec[:, COL[name] + c:COL[name] + c + 1]

        def turns(eng, turn, catch_up):
            for i in range(-1, FIRST):
                (catch_up if i == SPECIAL + 1 else turn)(i)
            with eng.Fori(FIRST, LAST + 1) as i:
                turn(i)
            for i in range(LAST + 1, B + 2):
                turn(i)

        def has(i, shift, low, high):
            return not isinstance(i, int) or low <= i + shift <= high

        def at(i, n):
            return isinstance(i, int) and i == n

        def rows_of(b):
            return xf[:, TC * b:TC * (b + 1), :] if isinstance(b, int) and b < NB else x2

        def await_apart(eng, semaphore, value):
            eng.wait_ge(semaphore, value)
            eng.sem_inc(passed, 1)

        @block.sync
        def _(sp):
            def load_x(b):
                await_step(sp, ln1, b - 1, "st3")
                await_step(sp, keep_y, b - 1, "xb")
                src = x[b] if isinstance(b, int) else x[bass.DynSlice(b, 1)].rearrange("a t d -> (a t) d")
                sp.dma_start(x_in[:], src.rearrange("(c p) d -> p c d", p=P)).then_inc(x_loaded, 16)

            sp.dma_start(vec[:], vecs).then_inc(consts_loaded, 16)
            load_x(0)
            sp.dma_start(asg_i[:], expert_indices.rearrange("n k -> (n k)").partition_broadcast(E)).then_inc(idx_loaded, 16)
            for dst, src in ((wk[:], w_key), (wv[:], w_value), (wr[:], w_recept), (wo[:], w_output), (fwk_whole, f_w_key),
                             (fwr[:], f_w_recept), (fwv[:], f_w_value), (gw_whole[:, 0], w_r_t), (gw_whole[:, 1], w_i_t),
                             (gwo[:], w_out_t)):
                sp.dma_start(dst, src.rearrange("(c p) n -> p c n", p=P)).then_inc(weights_loaded, 16)
            sp.dma_start(bias[:], bias_row.partition_broadcast(P)).then_inc(weights_loaded, 16)
            sp.dma_start(gamma[:], gamma_row.partition_broadcast(P)).then_inc(weights_loaded, 16)
            sp.dma_start(choice_w[:], expert_weights.rearrange("(c p) k -> p c k", p=P)).then_inc(weights_loaded, 16)

            sp.wait_ge(consts_made, 8)
            sp.dma_start(token_table.rearrange("(p t) a -> p (t a)", p=P),
                         xs[:, 0:NT].bitcast(I32)).then_inc(table_zeroed, 16)

            def load_expert(f, e):
                half = expert_sets[f][:, e % 2, :]
                sp.dma_start(half[:, 0:DC * FF].rearrange("p (c n) -> p c n", c=DC),
                             w1[e].rearrange("(c p) n -> p c n", p=P)).then_inc(expert_loaded[e % 2], 16)
                sp.dma_start(half[:, DC * FF:SET].rearrange("p (c n) -> p c n", c=FC),
                             w2[e].rearrange("(c p) n -> p c n", p=P)).then_inc(expert_loaded[e % 2], 16)

            def announce_expert(f, e):
                sp.wait_ge(expert_loaded[e % 2], 32 * (f * E // 2 + e // 2 + 1))
                sp.sem_inc(expert_ready, 1)

            def turn(i):
                if at(i, B):
                    await_step(sp, proj, B - 1, "o")
                    load_expert(1, 0)
                    normalised_out(1)
                    await_step(sp, fr, B - 1, "f")
                    load_expert(1, 1)
                    announce_expert(1, 0)
                    announce_expert(1, 1)
                if at(i, 1):
                    sp.wait_ge(split_los, 2)
                    load_expert(0, 0)
                if at(i, SPECIAL):
                    normalised_out(0)
                    await_step(sp, fk, SPECIAL - 1, f"f{FC - 1}")
                    load_expert(0, 1)
                    experts(0)
                if has(i, 2, 1, B - 1):
                    load_x(i + 2)
                if has(i, -2, NB, B - 1):
                    await_step(sp, res, i - 2, "o")
                    dst = out[i - 2] if isinstance(i, int) else out[bass.DynSlice(i - 2, 1)].rearrange("a t d -> (a t) d")
                    sp.dma_start(dst.rearrange("(c p) d -> p c d", p=P), fo[:]).then_inc(out_stored, 16)

            def normalised_out(f):
                if f == 0:
                    sp.wait_ge(table_written, 16 * NCH * TOPK)
                    sp.dma_start(token_of_slot[:], token_table.rearrange("(t p) a -> p (t a)", p=P),
                                 allow_slow_non_contiguous=True).then_inc(table_loaded, 16)
                await_step(sp, experts_hat, f, f"h{NCH - 1}")
                sp.dma_start(xf_rows.rearrange("(c p) d -> p c d", p=P), xfn[f]).then_inc(xf_stored, 16)

            def experts(f):
                if f == 0:
                    announce_expert(f, 0)
                    announce_expert(f, 1)
                    await_step(sp, route, 0, "tab1")
                for e in range(2, E):
                    last = sp.value_load(table[0:1, NT + e - 2:NT + e - 1], min_val=0, max_val=NT)
                    sp.wait_ge(tiles_done, last + (1 + f * NT))
                    load_expert(f, e)
                    announce_expert(f, e)

            turns(sp, turn, turn)
            experts(1)
            for b in range(NB):
                await_step(sp, merged, 1, f"q{TC * (b + 1) - 1}")
                sp.dma_start(out[b].rearrange("(c p) d -> p c d", p=P), xf[:, TC * b:TC * (b + 1), :])\
                    .then_inc(out_stored, 16)
            sp.wait_ge(out_stored, 16 * B)

        @block.gpsimd
        def _(pool):
            pool.memset(ident[:], 0.0).then_inc(consts_made, 1)
            pool.memset(xs[:], 0.0).then_inc(consts_made, 1)
            pool.memset(half_neg[:], -0.5).then_inc(consts_made, 1)
            pool.memset(ones_e, 1.0).then_inc(consts_made, 1)
            pool.memset(before, 1.0).then_inc(consts_made, 1)
            pool.memset(upto, 1.0).then_inc(consts_made, 1)
            pool.iota(token_id[:], pattern=[[P, NCH]], base=0, channel_multiplier=1).then_inc(consts_made, 1)
            pool.wait_ge(consts_made, 7)
            pool.affine_select(out=ident[:], in_=ident[:], compare_op=ALU.not_equal, fill=1.0, base=0,
                               pattern=[[-1, P]], channel_multiplier=1).then_inc(consts_made, 1)
            pool.affine_select(out=before, in_=before, compare_op=ALU.is_gt, fill=0.0, base=0,
                               pattern=[[1, E]], channel_multiplier=-1).then_inc(consts_made, 1)
            pool.affine_select(out=upto, in_=upto, compare_op=ALU.is_ge, fill=0.0, base=0,
                               pattern=[[1, E]], channel_multiplier=-1).then_inc(consts_made, 1)
            pool.iota(expert_id, pattern=[[0, 1]], base=0, channel_multiplier=1,
                      allow_small_or_imprecise_dtypes=True).then_inc(consts_made, 1)
            pool.iota(tile_no, pattern=[[1, NT]], base=0, channel_multiplier=0,
                      allow_small_or_imprecise_dtypes=True).then_inc(consts_made, 1)
            pool.memset(euler[:], 2.718281828459045).then_inc(consts_made, 1)
            pool.wait_ge(log_steps, 1)
            pool.wait_ge(consts_made, 13)
            pool.tensor_tensor(la[0][:], euler[:], la[3][:], ALU.pow).then_inc(exp_made, 1)
            pool.sem_inc(tiles_done, 1)
            pool.sem_inc(y_out, 1)
            pool.sem_inc(y_stored, 16)

            def power(dst, src, done):
                pool.tensor_tensor(dst, src, half_neg[:, 0:src.shape[1]], ALU.pow).then_inc(done, 1)

            def scale_rows(dst, src, n, col0, st):
                for c in range(dst.shape[1]):
                    pool.tensor_scalar(dst[:, c, :], src[:, c, :], negmean[n][:, c:c + 1],
                                       rstd[n][:, col0 + c:col0 + c + 1], ALU.add, ALU.mult).then_inc(st.sem, 1)

            def norm1(b):
                await_step(pool, ln1, b, "v1")
                await_step(pool, keep_y, b - 1, "xb")
                power(rstd[0][:], varis[0][:], hat1.sem)
                await_step(pool, tr_in, b - 1, "t")
                early = isinstance(b, int) and b <= SPECIAL + 1
                await_step(pool, tr_rec, -1 if early else 1 if at(b, SPECIAL + 2) else b - 3, "t")
                await_apart(pool, hat1.sem, hat1.count(b, "pow"))
                scale_rows(xhat[0], x_in, 0, TC, hat1)

            def keep1(b):
                await_step(pool, zsum, b - 1, "z")
                await_step(pool, keep_xz, b - 1, "xz")
                await_step(pool, hat2, b - 1, f"h{TC - 1}")
                await_apart(pool, hat1.sem, hat1.count(b, "pow"))
                scale_rows(y, x_in, 0, 0, keep_y)
                await_step(pool, keep_xz, b - 1, "xz")
                if isinstance(b, int) and b < NB:
                    pool.tensor_copy(xb[:], x_in[:]).then_inc(keep_y.sem, 1)
                else:
                    pool.tensor_tensor(xb[:], x_in[:], wide(bias, TC), ALU.add).then_inc(keep_y.sem, 1)

            def norm2(b):
                await_step(pool, ln2, b, "v0")
                await_step(pool, hat2, b - 1, f"h{TC - 1}")
                power(rstd[1][:, 0:TC], varis[1][:, 0:TC], hat2.sem)
                await_step(pool, tr_mid, b - 1, "t")
                await_apart(pool, hat2.sem, hat2.count(b, "pow"))
                scale_rows(xhat[1], z, 1, 0, hat2)

            def keep2(b):
                await_step(pool, zsum, b, "z")
                await_step(pool, keep_y, b, "xb")
                await_step(pool, comb, b - 1, "x")
                pool.tensor_tensor(xz[:], xb[:], z[:], ALU.add).then_inc(keep_xz.sem, 1)

            def norm3(b):
                await_step(pool, ln3, b, "v0")
                await_step(pool, hat3, b - 1, f"h{TC - 1}")
                power(rstd[2][:, 0:TC], varis[2][:, 0:TC], hat3.sem)
                await_step(pool, tr_rec, b - 1, "t")
                first = (SPECIAL + 1, SPECIAL + 1, SPECIAL + 2)[b] if isinstance(b, int) and b <= NB else b + 2
                await_step(pool, tr_in, first, "t")
                await_apart(pool, hat3.sem, hat3.count(b, "pow"))
                scale_rows(xhat[2], rows_of(b), 2, 0, hat3)

            def keep3(b):
                early = isinstance(b, int) and b < NB
                if early:
                    await_step(pool, merged, 0, f"q{TC * (b + 1) - 1}")
                else:
                    await_step(pool, comb, b, "x")
                await_step(pool, res, b - 1, "o")
                if early:
                    pool.tensor_copy(x2b, rows_of(b)).then_inc(keep_x2.sem, 1)
                else:
                    pool.tensor_tensor(x2b, rows_of(b), wide(bias, TC), ALU.add).then_inc(keep_x2.sem, 1)

            def scaled_input(b):
                await_step(pool, gates_out, b, "sc")
                await_step(pool, gin, b, "in")
                pool.tensor_tensor(ig[:], ig[:], om[:], ALU.mult).then_inc(gin.sem, 1)

            def gated_input(b):
                await_step(pool, gates_out, b, "i1")
                pool.tensor_tensor(ig[:], ig[:], cv[:], ALU.mult).then_inc(gin.sem, 1)

            def residual(b):
                await_step(pool, fin, b, f"f{TC - 1}")
                pool.tensor_tensor(rows_of(b) if isinstance(b, int) and b < NB else fo, fo, x2b, ALU.add).then_inc(res.sem, 1)

            def mean_power(b):
                await_step(pool, fin, b, "ms")
                power(rms[:], msq[:], fin_pow.sem)

            def weighted(b):
                await_step(pool, wkv_act, b, "g")
                await_step(pool, wkv, b, "dv")
                pool.tensor_tensor(gv[:], g[:], vc[:], ALU.mult).then_inc(wkv_gv.sem, 1)

            def squares(b, lo=0, hi=FC):
                for j in range(lo, hi):
                    await_step(pool, relu, b, f"f{j}")
                    pool.tensor_tensor(hid[:, j, :], hid[:, j, :], hid[:, j, :], ALU.mult).then_inc(sq.sem, 1)

            def turn(i):
                if at(i, 0):
                    pool.wait_ge(split_his, 2)
                    pool.tensor_tensor(fwk[1][:], fwk_whole, fwk[0][:].bitcast(F32), ALU.subtract).then_inc(split_los, 1)
                    pool.tensor_tensor(gw[1][:], gw_whole, gw[0][:].bitcast(F32), ALU.subtract).then_inc(split_los, 1)
                if at(i, SPECIAL):
                    first_gather(0)
                    squares(i - 1)
                    weighted(i)
                    norm1(i + 1)
                    more_gathers(0, 1)
                    picking(0, 0)
                    picking(0, 1)
                if at(i, SPECIAL + 2):
                    mean_power(NB)
                    residual(NB)
                if has(i, -1, 0, B - 1) and not at(i, SPECIAL):
                    squares(i - 1)
                if at(i, 0):
                    norm1(1)
                if has(i, 0, 0, B - 1) and not at(i, SPECIAL):
                    weighted(i)
                if has(i, 1, 0, B - 1) and not at(i, SPECIAL) and not at(i, 0):
                    norm1(i + 1)
                if at(i, SPECIAL - 1):
                    await_step(pool, route, 0, "slot")
                    pool.wait_ge(table_zeroed, 16)
                    for c in range(NCH):
                        for k in range(TOPK):
                            n = c * TOPK + k
                            pool.indirect_dma_start(
                                out=token_table, out_offset=bass.IndirectOffsetOnAxis(ap=slot_i[:, n:n + 1], axis=0),
                                in_=token_id[:, c:c + 1], in_offset=None).then_inc(table_written, 16)
                if has(i, -2, NB, B - 1):
                    keep3(i - 2)
                    if at(i, B):
                        first_gather(1)
                    if at(i, B + 1):
                        later_gather(1, 2)
                    gated_input(i - 2)
                    if at(i, B):
                        later_gather(1, 1)
                    if at(i, B + 1):
                        later_gather(1, 3)
                    scaled_input(i - 2)
                if at(i, B - 1):
                    norm_power(1)
                if has(i, 0, 0, B - 1) and not at(i, SPECIAL):
                    norm2(i)
                if at(i, SPECIAL):
                    norm3(0)
                    norm2(i)
                    keep3(0)
                    keep2(i)
                    keep1(i + 1)
                    norm3(1)
                    gated_input(0)
                if has(i, -2, NB, B - 1):
                    mean_power(i - 2)
                if has(i, -1, NB, B - 1) and not at(i, SPECIAL):
                    norm3(i - 1)
                if has(i, -2, NB, B - 1):
                    residual(i - 2)
                if has(i, 0, 0, B - 1) and not at(i, SPECIAL):
                    keep2(i)
                if at(i, SPECIAL - 1):
                    norm_power(0)
                if has(i, 1, 0, B - 1) and not at(i, SPECIAL):
                    if at(i, -1):
                        pool.wait_ge(weights_loaded, 13 * 16)
                    keep1(i + 1)

            def catch_up(i):
                squares(i - 1, 0, 4)
                scaled_input(0)
                squares(i - 1, 4, FC)
                weighted(i)
                mean_power(0)
                norm1(i + 1)
                residual(0)
                keep3(1)
                norm3(2)
                gated_input(1)
                scaled_input(1)
                norm2(i)
                mean_power(1)
                residual(1)
                keep3(2)
                gated_input(2)
                norm3(3)
                scaled_input(2)
                keep2(i)
                keep1(i + 1)

            def norm_power(f):
                await_step(pool, lnf, f, "v0")
                pool.tensor_tensor(rstd[3][:, 0:NCH], varis[3][:, 0:NCH], half_neg[:, 0:NCH], ALU.pow).then_inc(experts_rstd, 1)

            def gather(t, n):
                src = token_of_slot[:, bass.DynSlice(t, 1)]
                pool.tensor_copy(token_idx[:], src).then_inc(idx_copied, 1)
                await_apart(pool, idx_copied, n + 1)
                pool.indirect_dma_start(out=xs[:], out_offset=None, in_=xf_rows,
                                        in_offset=bass.IndirectOffsetOnAxis(ap=token_idx[:, 0:1], axis=0)).then_inc(gathered, 16)

            def first_gather(f):
                if f == 0:
                    pool.wait_ge(table_loaded, 16)
                else:
                    pool.wait_ge(xs_t, NT)
                pool.wait_ge(xf_stored, 16 * (f + 1))
                gather(0, f * NT)

            def later_gather(f, t):
                pool.wait_ge(xs_t, t + f * NT)
                gather(t, t + f * NT)

            def more_gathers(f, start):
                with pool.Fori(start, NT) as t:
                    later_gather(f, t)

            def picking(f, b):
                pool.wait_ge(y_stored, 16 * (NT * (f + 1) + 1))
                for c in range(TC * b, TC * (b + 1)):
                    for k in range(TOPK):
                        n = c * TOPK + k
                        pool.indirect_dma_start(
                            out=picked[:, c, k, :], out_offset=None, in_=ys_rows,
                            in_offset=bass.IndirectOffsetOnAxis(ap=slot_i[:, n:n + 1], axis=0)).then_inc(picks[c], 16)

            turns(pool, turn, catch_up)
            more_gathers(1, 4)
            for b in range(NB):
                picking(1, b)

        @block.scalar
        def _(act):
            act.wait_ge(consts_loaded, 16)
            LOG_EXP = "natural_log_exp_and_others"
            nc.scalar.preload_act_table_set(LOG_EXP)
            nc.scalar.activation(decay[:], vec[:, COL["decay"]:COL["decay"] + DC], ACT.Exp).then_inc(vec_made, 1)
            act.wait_ge(vec_made, 1)
            nc.scalar.mul(decay[:], decay[:], -1.0).then_inc(vec_made, 1)
            act.wait_ge(cols_made, 5)
            act.wait_ge(log_steps, LOG_STEPS)

            def norm_out(dst, w, b, ev):
                for c in range(DC):
                    nc.scalar.activation(dst[:, c, 1:T + 1], bank_t[:, c, :], ACT.Identity, bias=col(b, c),
                                         scale=col(w, c)).then_inc(ev.sem, 1)

            def keys(b):
                await_step(act, wkv, b - 1, "out")
                for n, (name, dst) in enumerate((("k", kc), ("v", vc), ("r", sr))):
                    for c in range(DC):
                        await_step(act, kvr, b, f"{name}{c}")
                        nc.scalar.activation(dst[:, c, :], ring[(2 * n + c) % 4], ACT.Sigmoid if name == "r" else ACT.Copy)\
                            .then_inc(kvr_out.sem, 1)

            def conv_in(b):
                await_step(act, tr_rec, b, "t")
                await_step(act, gin, b - 1, "in")
                await_step(act, gates, b - 1, "i1")
                if at(b, 0):
                    act.wait_ge(cols_made, 6)
                for c in range(DC):
                    nc.scalar.activation(xc[:, c, 3:T + 3], bank_t[:, c, :], ACT.Copy).then_inc(ev3.sem, 1)
                for c in range(DC):
                    nc.scalar.activation(cv[:, c, :], bank_t[:, c, :], ACT.Identity, bias=col("conv_b", c),
                                         scale=col("conv3", c)).then_inc(ev3.sem, 1)

            def gates_in(b):
                await_step(act, rec, b - 1, "h1")
                await_step(act, res, b - 1, "o")
                if not isinstance(b, int) or b > NB:
                    act.wait_ge(out_stored, (b - NB) * 16)
                for n, (name, dst, b_) in enumerate((("r", rg, "b_r"), ("i", ig, "b_i"))):
                    for c in range(DC):
                        await_step(act, gates, b, f"{name}{c}")
                        nc.scalar.activation(dst[:, c, :], ring[2 * n + c], ACT.Sigmoid, bias=col(b_, c))\
                            .then_inc(gates_out.sem, 1)

            def decays(b):
                for c in range(DC):
                    await_step(act, gates_out, b, f"r{c}")
                    nc.scalar.activation(aa[:, c, :], rg[:, c, :], ACT.Exp, scale=log_a8[:, c:c + 1])\
                        .then_inc(gates_out.sem, 1)

            def root(b):
                await_step(act, rec, b, "om")
                nc.scalar.activation(om[:], om[:], ACT.Ln).then_inc(gates_out.sem, 1)
                await_step(act, gates_out, b, "ln")
                nc.scalar.activation(om[:], om[:], ACT.Exp, scale=0.5).then_inc(gates_out.sem, 1)

            def sums_of_squares(b):
                await_step(act, rproj, b, "o")
                await_step(act, fin, b - 1, "ms")
                for c in range(TC):
                    if c:
                        await_step(act, sumsq, b, f"s{c - 1}")
                    nc.scalar.activation(square[:], rows4[:, c, :], ACT.Square, accum_out=ssq[:, c:c + 1])\
                        .then_inc(sumsq.sem, 1)

            def receptance(b):
                await_step(act, fr, b, "f")
                await_step(act, comb, b - 1, "x")
                nc.scalar.activation(sf[:].rearrange("p c d -> p (c d)"), ring_rows.rearrange("p a t -> p (a t)"),
                                     ACT.Sigmoid).then_inc(fr_out.sem, 1)

            def relus(b, lo, hi):
                if lo == 0:
                    await_step(act, fv, b - 1, "v")
                for j in range(lo, hi):
                    await_step(act, fk, b, f"f{j}")
                    nc.scalar.activation(hid[:, j, :], ring[(j + 2) % 4], ACT.Relu).then_inc(relu.sem, 1)

            def turn(i):
                if at(i, 0):
                    act.wait_ge(weights_loaded, 13 * 16)
                    nc.scalar.activation(fwk[0][:], fwk_whole, ACT.Copy).then_inc(split_his, 1)
                    nc.scalar.activation(gw[0][:], gw_whole, ACT.Copy).then_inc(split_his, 1)
                now, next_, channel, recur = (has(i, 0, 0, B - 1), has(i, 1, 0, B - 1), has(i, -1, 0, B - 1),
                                              has(i, -2, NB, B - 1))
                if now:
                    keys(i)
                if at(i, SPECIAL + 2):
                    sums_of_squares(NB)
                if recur:
                    conv_in(i - 2)
                if channel:
                    relus(i - 1, 0, 2)
                if now:
                    nc.scalar.preload_act_table_set(LOG_EXP)
                    weight_exps(i, "g")
                if channel:
                    relus(i - 1, 2, 4)
                if now:
                    weight_exps(i, "dec")
                if channel:
                    relus(i - 1, 4, FC)
                if channel:
                    receptance(i - 1)
                if recur:
                    if at(i, B + 1):
                        hidden(1, 1)
                        rows_back(1, 0)
                    gates_in(i - 2)
                if at(i, SPECIAL):
                    hidden(0, 0)
                nc.scalar.preload_act_table_set(LOG_EXP)
                if now:
                    inverse(i)
                if at(i, SPECIAL):
                    experts(0)
                elif recur:
                    decays(i - 2)
                if next_:
                    norm_in(i + 1)
                if recur:
                    root(i - 2)
                    if at(i, B):
                        hidden(1, 0)
                    if at(i, B + 1):
                        hidden(1, 2)
                        rows_back(1, 1)
                        act.wait_ge(y_stored, 16 * (NT + 3))
                    sums_of_squares(i - 2)
                if now and not at(i, SPECIAL):
                    norm_mid(i)
                if at(i, SPECIAL):
                    conv_in(0)
                    keys(i + 1)
                    norm_mid(i)
                    gates_in(0)
                    nc.scalar.preload_act_table_set(LOG_EXP)
                    decays(0)

            def catch_up(i):
                relus(i - 1, 0, 2)
                conv_in(1)
                weight_exps(i, "g")
                relus(i - 1, 2, 4)
                weight_exps(i, "dec")
                root(0)
                relus(i - 1, 4, FC)
                receptance(i - 1)
                sums_of_squares(0)
                gates_in(1)
                nc.scalar.preload_act_table_set(LOG_EXP)
                inverse(i)
                decays(1)
                norm_in(i + 1)
                root(1)
                conv_in(2)
                sums_of_squares(1)
                norm_mid(i)
                gates_in(2)
                nc.scalar.preload_act_table_set(LOG_EXP)
                decays(2)
                root(2)

            def weight_exps(b, which):
                if which == "g":
                    await_step(act, wkv, b, "cap")
                    await_step(act, wkv_gv, b - 1, "gv")
                    nc.scalar.activation(g[:], g[:], ACT.Exp).then_inc(wkv_act.sem, 1)
                else:
                    await_step(act, wkv, b, "in")
                    nc.scalar.activation(dec[:], dec[:], ACT.Exp).then_inc(wkv_act.sem, 1)

            def inverse(b):
                await_step(act, wkv, b, "den")
                nc.scalar.activation(den[:], den[:], ACT.Ln).then_inc(wkv_act.sem, 1)
                await_step(act, wkv_act, b, "ln")
                nc.scalar.activation(den[:], den[:], ACT.Exp, scale=-1.0).then_inc(wkv_act.sem, 1)

            def norm_in(b):
                await_step(act, tr_in, b, "t")
                await_step(act, mix1, b - 1, "r1")
                norm_out(xn1, "ln1_w", "ln1_b", ev1)

            def norm_mid(b):
                await_step(act, tr_mid, b, "t")
                await_step(act, mix2, b - 1, "r1")
                norm_out(xn2, "ln2_w", "ln2_b", ev2)

            def hidden(f, t):
                act.wait_ge(up_done, t + (1 + f * NT))
                if f or not isinstance(t, int):
                    act.wait_ge(hid_t, t + f * NT)
                nc.scalar.activation(tile_rows[f], psum[:, 2:4, :].rearrange("p a t -> p (a t)"),
                                     ACT.Gelu).then_inc(gelu_done, 1)

            def rows_back(f, t):
                base = f * NT
                act.wait_ge(tiles_done, t + (2 + base))
                act.wait_ge(y_stored, (t + (1 + base)) * 16)
                nc.scalar.activation(ys[:], psum[:, 1, 0:D], ACT.Copy).then_inc(y_out, 1)
                act.wait_ge(y_out, t + (2 + base))
                dst = ys_rows[t * P:(t + 1) * P, :] if isinstance(t, int) else ys_rows[bass.DynSlice(t * P, P), :]
                act.dma_start(dst, ys[:]).then_inc(y_stored, 16)

            def experts(f):
                with act.Fori(3 if f else 1, NT) as t:
                    hidden(f, t)
                    rows_back(f, t - 1)
                rows_back(f, NT - 1)

            turns(act, turn, catch_up)
            experts(1)

        @block.tensor
        def _(pe):
            pe.wait_ge(consts_made, 12)

            def transposes(src, st):
                for c in range(DC):
                    for k in range(TC):
                        last = nc.tensor.transpose(bank_t[:, c, k * P:(k + 1) * P], src[:, k, c * P:(c + 1) * P], ident[:])
                last.then_inc(st.sem, 1)

            def columns(dst, w, m, src, st):
                for c in range(DC):
                    last = nc.tensor.matmul(dst, w[:, c, m * P:(m + 1) * P], src[:, c, :], start=c == 0, stop=c == DC - 1)
                last.then_inc(st.sem, 1)

            def columns_split(dst, w, m, src, st):
                terms = [(c, a, b) for a, b in ((0, 0), (0, 1), (1, 0)) for c in range(DC)]
                for n, (c, a, b) in enumerate(terms):
                    last = nc.tensor.matmul(dst, w[a][:, c, m * P:(m + 1) * P], src[b][:, c, :], start=n == 0,
                                            stop=n == len(terms) - 1)
                last.then_inc(st.sem, 1)

            def rows(dst, src, w, chunks, st, tokens=range(TC)):
                for k in tokens:
                    for c in range(chunks):
                        last = nc.tensor.matmul(dst[:, k, :], src[:, c, k * P:(k + 1) * P], w[:, c, :],
                                                start=c == 0, stop=c == chunks - 1)
                if st is not None:
                    last.then_inc(st.sem, 1)

            def turn(i):
                if has(i, 0, 0, B - 1):
                    keys(i, "kvr" if at(i, 0) else "vr")
                if at(i, SPECIAL + 2):
                    rec_products(NB, SPECIAL)
                if has(i, -2, NB, B - 1):
                    transposes_rec(i - 2, i - 1)
                if has(i, -1, 0, B - 1):
                    if at(i, 1):
                        pe.wait_ge(split_los, 2)
                    channel_keys(i - 1)
                if at(i, SPECIAL):
                    experts(0)
                elif has(i, -2, NB, B - 1):
                    if at(i, B + 1):
                        await_step(pe, ev3, B - 1, "c1")
                        tile_in(1, 1)
                        up(1, 1, expert_of(1))
                        down(1, 0)
                        pe.wait_ge(gelu_done, NT + 2)
                        pe.wait_ge(hidt_ready, NT + 1)
                    gate_products(i - 2)
                    if at(i, B):
                        tile_in(1, 0)
                    if at(i, B + 1):
                        await_step(pe, gates_out, B - 1, "i1")
                        turn_hidden(1, 1)
                        tile_in(1, 2)
                        up(1, 2, expert_of(2))
                        down(1, 1)
                if at(i, 1):
                    await_step(pe, route, 0, "ni")
                    await_step(pe, ev1, 1, "e1")
                    await_step(pe, ev2, 0, "e1")
                    nc.tensor.matmul(psum[0:E, 0, 0:1], before, ntiles, start=True, stop=True)
                    nc.tensor.matmul(psum[0:E, 0, 1:2], upto, ntiles, start=True, stop=True)
                    nc.tensor.matmul(psum[0:1, 0, 2:2 + E], ntiles, upto, start=True, stop=True).then_inc(route_pe.sem, 1)
                if has(i, -1, 0, B - 1):
                    values(i - 1, 0, 1, -1 if at(i, SPECIAL) else i - 3)
                if at(i, 1):
                    await_step(pe, route, 0, "pos")
                    by_token = rank.rearrange("e (c p k) -> e c k p", p=P, k=TOPK)
                    for c in range(NCH):
                        for k in range(TOPK):
                            n = 16 + c * TOPK + k
                            last = nc.tensor.matmul(psum[:, 0, n:n + 1], by_token[:, c, k, :], ones_e[:, 0:1],
                                                    start=True, stop=True)
                    last.then_inc(route_pe.sem, 1)
                    await_step(pe, route, 0, "past")
                    nc.tensor.matmul(psum[0:1, 0, 40:40 + NT], ones_e[:, 0:1], past, start=True, stop=True)\
                        .then_inc(route_pe.sem, 1)
                if has(i, 1, 0, B - 1):
                    if at(i, 1):
                        await_step(pe, route, 0, "slot")
                    transposes_in(i + 1, -1 if isinstance(i, int) and i <= SPECIAL else i - 2)
                if has(i, -1, 0, B - 1):
                    values(i - 1, 1, 2, -1 if at(i, SPECIAL) else i - 3)
                if has(i, 0, 0, B - 1):
                    outputs(i, -1 if isinstance(i, int) and i < NB + 2 else i - 2)
                if at(i, B):
                    await_step(pe, gates_out, B - 2, "i1")
                    up(1, 0, expert_of(0))
                if has(i, -1, 0, B - 1):
                    values(i - 1, 2, TC, -1 if at(i, SPECIAL) else i - 3)
                if has(i, -2, NB, B - 1):
                    rec_products(i - 2, i - 1)
                if at(i, B):
                    turn_hidden(1, 0)
                if has(i, 1, 1, B - 1) and not at(i, SPECIAL):
                    keys(i + 1, "k")
                if has(i, 0, 0, B - 1) and not at(i, SPECIAL):
                    transposes_mid(i, -1 if isinstance(i, int) and i < SPECIAL else i - 2)
                if at(i, SPECIAL):
                    await_step(pe, ev1, i + 1, "e1")
                    transposes_rec(0, i - 1)
                    keys(i + 1)
                    transposes_mid(i, 0)
                    gate_products(0)
                    transposes_rec(1, i)

            def catch_up(i):
                channel_keys(i - 1)
                rec_products(0, i - 2)
                gate_products(1)
                transposes_in(i + 1, 1)
                values(i - 1, 0, 2, 0)
                outputs(i, 1)
                await_step(pe, ev1, i + 1, "e1")
                transposes_rec(2, i - 1)
                values(i - 1, 2, TC, 0)
                rec_products(1, i - 1)
                await_step(pe, zsum, i, "z")
                transposes_mid(i, 2)
                gate_products(2)
                keys(i + 1, "k")

            def transposes_in(b, rec):
                await_step(pe, hat1, b, f"h{TC - 1}")
                await_step(pe, ev2, b - 2, "e1")
                await_step(pe, ev3, rec, "c1")
                transposes(xhat[0], tr_in)

            def transposes_mid(b, rec):
                await_step(pe, hat2, b, f"h{TC - 1}")
                await_step(pe, ev1, b + 1, "e1")
                await_step(pe, ev3, rec, "c1")
                transposes(xhat[1], tr_mid)

            def channel_keys(b):
                await_step(pe, mix2, b, "lo")
                await_step(pe, gates_out, b - NB if not isinstance(b, int) or b > SPECIAL else b - SPECIAL, "i1")
                for j in range(FC):
                    if j < 4:
                        await_step(pe, kvr_out, b + 1, ("v0", "v1", "r0", "r1")[j])
                    else:
                        await_step(pe, relu, b, f"f{j - 4}")
                    columns_split(ring[(j + 2) % 4], fwk, j, xfk, fk)
                await_step(pe, mix2, b, "r1")
                await_step(pe, relu, b, f"f{FC - 3}")
                rows(fr4, xfr, fwr, DC, fr)

            def values(b, start, stop, last):
                await_step(pe, sq, b, f"f{FC - 1}")
                await_step(pe, fin, last, f"f{TC - 1}")
                rows(rows4, hid, fwv, FC, fv if stop % 2 == 0 else None, range(start, stop))

            def outputs(b, last):
                await_step(pe, wkv, b, "out")
                await_step(pe, fr_out, b - 1, "s")
                await_step(pe, kvr_out, b, "v1")
                await_step(pe, gates_out, last, "i1")
                rows(fr4, mixed, wo, DC, proj)

            def keys(b, names="kvr"):
                if at(b, 0):
                    pe.wait_ge(weights_loaded, 13 * 16)
                await_step(pe, relu, b - 2, f"f{FC - 1}")
                await_step(pe, fr_out, b - 2, "s")
                await_step(pe, zsum, b - 1, "z")
                await_step(pe, gates_out, -1 if isinstance(b, int) and b <= SPECIAL + 1 else b - 3, "i1")
                for name, w, src in (("k", wk, xk), ("v", wv, xv), ("r", wr, xr)):
                    if name not in names:
                        continue
                    n = "kvr".index(name)
                    await_step(pe, mix1, b, f"{name}{DC - 1}")
                    for c in range(DC):
                        if name == "r":
                            await_step(pe, kvr_out, b, f"k{c}")
                        columns(ring[(2 * n + c) % 4], w, c, src, kvr)

            def transposes_rec(b, mid):
                await_step(pe, hat3, b, f"h{TC - 1}")
                await_step(pe, ev2, mid, "e1")
                await_step(pe, ev3, b - 1, "c1")
                transposes(xhat[2], tr_rec)

            def gate_products(b):
                await_step(pe, conv, b, "lo")
                await_step(pe, gates_out, b - 1, "i1")
                if at(b, 0):
                    await_step(pe, kvr_out, SPECIAL + 1, "r1")
                else:
                    channel = SPECIAL if at(b, 1) else b + 1
                    await_step(pe, relu, channel, f"f{FC - 1}")
                for n in range(2):
                    if n and not at(b, 0):
                        await_step(pe, fr_out, channel, "s")
                    for c in range(DC):
                        columns_split(ring[2 * n + c], [w[:, n] for w in gw], c, cv_parts, gates)

            def rec_products(b, channel):
                await_step(pe, rec, b, "h1")
                await_step(pe, fin, b - 1, f"f{TC - 1}")
                for half, name in enumerate(("a", "g")):
                    await_step(pe, comb, channel, name)
                    rows(rows4, hs, gwo, DC, rproj, range(half * TC // 2, (half + 1) * TC // 2))

            def tile_in(f, t):
                pe.wait_ge(gathered, (t + (1 + f * NT)) * 16)
                for c in range(DC):
                    last = nc.tensor.transpose(psum[:, 0, c * P:(c + 1) * P], xs[:, c * P:(c + 1) * P], ident[:])
                last.then_inc(xs_t, 1)

            def expert_of(t):
                return pe.value_load(table[0:1, bass.DynSlice(t, 1)], min_val=0, max_val=E - 1)

            def up(f, t, e):
                pe.wait_ge(xst_ready, t + (1 + f * NT))
                pe.wait_ge(expert_ready, e + (1 + f * E))
                for h in range(FF // T):
                    for c in range(DC):
                        w = expert_sets[f][:, bass.DynSlice(e % 2, 1), c * FF + h * T:c * FF + (h + 1) * T]
                        last = nc.tensor.matmul(psum[:, 2 + h, :], xst[:, c, :], w.rearrange("p a n -> p (a n)"),
                                                start=c == 0, stop=c == DC - 1)
                last.then_inc(up_done, 1)

            def turn_hidden(f, t):
                pe.wait_ge(gelu_done, t + (1 + f * NT))
                for j in range(FC):
                    last = nc.tensor.transpose(psum[:, 4 + j // 4, (j % 4) * P:(j % 4 + 1) * P],
                                               tile_rows[f][:, j * P:(j + 1) * P], ident[:])
                last.then_inc(hid_t, 1)

            def down(f, t):
                pe.wait_ge(hidt_ready, t + (1 + f * NT))
                pe.wait_ge(y_out, t + (1 + f * NT))
                e = expert_of(t)
                for j in range(FC):
                    w = expert_sets[f][:, bass.DynSlice(e % 2, 1), DC * FF + j * D:DC * FF + (j + 1) * D]
                    last = nc.tensor.matmul(psum[:, 1, 0:D], tile_cols[f][:, j, :], w.rearrange("p a n -> p (a n)"),
                                            start=j == 0, stop=j == FC - 1)
                last.then_inc(tiles_done, 1)

            def experts(f):
                base = f * NT
                if f == 0:
                    await_step(pe, ev1, SPECIAL, "e1")
                    await_step(pe, ev2, SPECIAL - 1, "e1")
                    await_step(pe, zsum, SPECIAL - 1, "z")
                    await_step(pe, relu, SPECIAL - 1, f"f{FC - 1}")
                    await_step(pe, fr_out, SPECIAL - 1, "s")
                    await_step(pe, comb, SPECIAL - 2, "x")
                    await_step(pe, route, 0, "tab1")
                    tile_in(f, 0)
                    up(f, 0, expert_of(0))
                with pe.Fori(3 if f else 1, NT) as t:
                    e = expert_of(t)
                    tile_in(f, t)
                    turn_hidden(f, t - 1)
                    up(f, t, e)
                    down(f, t - 1)
                turn_hidden(f, NT - 1)
                down(f, NT - 1)
                pe.wait_ge(y_out, NT + 1 + base)
                pe.wait_ge(hidt_ready, NT + base)

            turns(pe, turn, catch_up)
            experts(1)

        @block.vector
        def _(dve):
            def log_of_sigmoid():
                x_, (s_, s2, p, t) = vec[:, COL["log_a"]:COL["log_a"] + DC], [b_[:] for b_ in la]
                done = [0]

                def step(ins):
                    ins.then_inc(log_steps, 1)
                    done[0] += 1
                    dve.wait_ge(log_steps, done[0])

                dve.wait_ge(consts_loaded, 16)
                step(nc.vector.scalar_tensor_tensor(t, x_, -1.0, x_, ALU.mult, ALU.min))
                dve.wait_ge(exp_made, 1)
                step(nc.vector.tensor_scalar(t, s_, 2.0, None, ALU.add))
                step(nc.vector.reciprocal(t, t))
                step(nc.vector.tensor_tensor(s_, s_, t, ALU.mult))
                step(nc.vector.tensor_tensor(s2, s_, s_, ALU.mult))
                step(nc.vector.tensor_scalar(p, s2, 1.0 / LOG_TERMS[0], None, ALU.mult))
                for n in LOG_TERMS[1:]:
                    step(nc.vector.scalar_tensor_tensor(p, p, 1.0 / n, s2, ALU.add, ALU.mult))
                step(nc.vector.scalar_tensor_tensor(p, p, 1.0, s_, ALU.add, ALU.mult))
                step(nc.vector.tensor_scalar(t, x_, 0.0, 8.0, ALU.min, ALU.mult))
                step(nc.vector.scalar_tensor_tensor(log_a8[:], p, -16.0, t, ALU.mult, ALU.add))
                assert done[0] == LOG_STEPS

            for buf in (xn1, xn2, alpha, beta):
                nc.vector.memset(buf[:, :, 0:1], 0.0).then_inc(cols_made, 1)
            nc.vector.memset(top[:, :, 0:1], -1e30).then_inc(cols_made, 1)
            dve.wait_ge(vec_made, 2)
            log_of_sigmoid()

            def norm_stats(src, n, st, b, chunks):
                for c in range(chunks):
                    nc.vector.bn_stats(stats[n][:, c, :], src[:, c, :]).then_inc(st.sem, 1)
                await_apart(dve, st.sem, st.count(b, f"st{chunks - 1}"))
                for c in range(chunks):
                    nc.vector.bn_aggr(moments[n][:, c, :], stats[n][:, c, :]).then_inc(st.sem, 1)
                await_step(dve, st, b, f"ag{chunks - 1}")
                nc.vector.tensor_scalar(negmean[n][:, 0:chunks], moments[n][:, 0:chunks, 0], -1.0, None, ALU.mult)\
                    .then_inc(st.sem, 1)
                nc.vector.tensor_scalar(varis[n][:, 0:chunks], moments[n][:, 0:chunks, 1], EPS, None, ALU.add)\
                    .then_inc(st.sem, 1)

            def mix(src, st, b, outs):
                nc.vector.tensor_tensor(diff, src[:, :, 1:T + 1], src[:, :, 0:T], ALU.subtract).then_inc(st.sem, 1)
                await_step(dve, st, b, "d")
                for dst, m in outs:
                    mixed_part(src, st, dst, m)

            def mixed_part(src, st, dst, m):
                for c in range(DC):
                    nc.vector.scalar_tensor_tensor(dst[:, c, :], diff[:, c, :], col(m, c), src[:, c, 0:T],
                                                   ALU.mult, ALU.add).then_inc(st.sem, 1)

            def split(src, parts, st, b, name):
                await_step(dve, st, b, name)
                nc.vector.tensor_copy(parts[0][:, :, :], src).then_inc(st.sem, 1)
                await_step(dve, st, b, "hi")
                nc.vector.tensor_tensor(parts[1][:, :, :], src, parts[0][:, :, :].bitcast(F32), ALU.subtract).then_inc(st.sem, 1)

            def mix_first(b):
                await_step(dve, ev1, b, "e1")
                await_step(dve, kvr, b - 1, "r1")
                await_step(dve, wkv, b - 1, "out")
                mix(xn1, mix1, b, ((xk, "mix_k"), (xv, "mix_v"), (xr, "mix_r")))

            def mix_second(b):
                await_step(dve, ev2, b, "e1")
                await_step(dve, fr, b - 1, "f")
                mix(xn2, mix2, b, ((xfk_whole, "fmix_k"),))
                split(xfk_whole, xfk, mix2, b, "k1")
                mixed_part(xn2, mix2, xfr, "fmix_r")

            def weights_of(b):
                was = top[:, :, 0:T]
                for c in range(DC):
                    await_step(dve, kvr_out, b, f"k{c}")
                    nc.vector.tensor_tensor_scan(top[:, c, 1:T + 1], decay[:, c:c + 1].to_broadcast([P, T]), kc[:, c, :],
                                                 -1e30, ALU.add, ALU.max).then_inc(wkv.sem, 1)
                for c in range(DC):
                    await_step(dve, wkv, b, f"m{c}")
                    nc.vector.scalar_tensor_tensor(g[:, c, :], kc[:, c, :], col("first", c), was[:, c, :],
                                                   ALU.add, ALU.subtract).then_inc(wkv.sem, 1)
                await_step(dve, wkv, b, "q1")
                nc.vector.tensor_scalar(g[:], g[:], LOGIT_CAP, None, ALU.min).then_inc(wkv.sem, 1)
                for c in range(DC):
                    nc.vector.scalar_tensor_tensor(dec[:, 0, c, :], was[:, c, :], decay[:, c:c + 1], top[:, c, 1:T + 1],
                                                   ALU.add, ALU.subtract).then_inc(wkv.sem, 1)
                nc.vector.tensor_tensor(dec[:, 1], kc[:], top[:, :, 1:T + 1], ALU.subtract).then_inc(wkv.sem, 1)

            def sums(b):
                await_step(dve, wkv_act, b, "dec")
                for c in range(DC):
                    nc.vector.tensor_tensor_scan(beta[:, c, 1:T + 1], dec[:, 0, c, :], dec[:, 1, c, :], 0.0,
                                                 ALU.mult, ALU.add).then_inc(wkv.sem, 1)
                await_step(dve, wkv, b, "b1")
                await_step(dve, kvr_out, b, "v1")
                nc.vector.tensor_tensor(dv, dec[:, 1], vc[:], ALU.mult).then_inc(wkv.sem, 1)
                await_step(dve, wkv, b, "dv")
                for c in range(DC):
                    nc.vector.tensor_tensor_scan(alpha[:, c, 1:T + 1], dec[:, 0, c, :], dv[:, c, :], 0.0,
                                                 ALU.mult, ALU.add).then_inc(wkv.sem, 1)

            def quotient(b):
                await_step(dve, wkv, b, "a1")
                await_step(dve, wkv_gv, b, "gv")
                nc.vector.tensor_tensor(num, alpha[:, :, 0:T], gv[:], ALU.add).then_inc(wkv.sem, 1)
                nc.vector.tensor_tensor(den[:], beta[:, :, 0:T], g[:], ALU.add).then_inc(wkv.sem, 1)

            def gated(b):
                await_step(dve, wkv_act, b, "inv")
                await_step(dve, kvr_out, b, "r1")
                nc.vector.tensor_tensor(den[:], den[:], sr[:], ALU.mult).then_inc(wkv.sem, 1)
                await_step(dve, wkv, b, "gate")
                nc.vector.tensor_tensor(mixed[:], den[:], num, ALU.mult).then_inc(wkv.sem, 1)

            def convolve(s):
                await_step(dve, ev3, s, "c1")
                for j in (2, 1, 0):
                    for c in range(DC):
                        if j < 2:
                            await_step(dve, conv, s, f"c{j + 1}{c}")
                        nc.vector.scalar_tensor_tensor(cv[:, c, :], xc[:, c, j:j + T], col(f"conv{j}", c), cv[:, c, :],
                                                       ALU.mult, ALU.add).then_inc(conv.sem, 1)
                await_step(dve, gin, s - 1, "b")
                await_step(dve, rproj, s - 1, "o")
                split(cv, cv_parts, conv, s, "c01")

            def scales(s):
                await_step(dve, gates_out, s, "a1")
                nc.vector.scalar_tensor_tensor(om[:], aa[:], -1.0, aa[:], ALU.mult, ALU.mult).then_inc(rec.sem, 1)
                await_step(dve, rec, s, "na")
                nc.vector.tensor_scalar(om[:], om[:], 1.0, TINY, ALU.add, ALU.max).then_inc(rec.sem, 1)

            def recur(s):
                await_step(dve, gates_out, s, "sc")
                await_step(dve, gin, s, "b")
                await_step(dve, rproj, s - 1, "o")
                for c in range(DC):
                    nc.vector.tensor_tensor_scan(hs[:, c, :], aa[:, c, :], ig[:, c, :], 0.0, ALU.mult, ALU.add)\
                        .then_inc(rec.sem, 1)

            def route_first():
                dve.wait_ge(idx_loaded, 16)
                nc.vector.tensor_copy(rank, asg_i).then_inc(route.sem, 1)
                await_step(dve, route, 0, "idx")
                nc.vector.tensor_scalar(onehot, rank, expert_id, None, ALU.is_equal).then_inc(route.sem, 1)
                await_step(dve, route, 0, "one")
                nc.vector.tensor_tensor_scan(rank, ones_e[:, 0:1].to_broadcast([E, NASG]), onehot, 0.0,
                                             ALU.mult, ALU.add).then_inc(route.sem, 1)
                await_step(dve, route, 0, "rank")
                nc.vector.tensor_scalar(ntiles_i[:, 0:1], rank[:, NASG - 1:NASG], float(P - 1), None, ALU.add)\
                    .then_inc(route.sem, 1)
                await_step(dve, route, 0, "n")
                nc.vector.tensor_scalar(ntiles_i[:, 1:2], ntiles_i[:, 0:1], P.bit_length() - 1, None,
                                        ALU.logical_shift_right).then_inc(route.sem, 1)
                await_step(dve, route, 0, "nf")
                nc.vector.tensor_copy(ntiles, ntiles_i[:, 1:2]).then_inc(route.sem, 1)

            def route_second():
                await_step(dve, route_pe, 0, "ends")
                nc.vector.tensor_scalar(starts, psum[0:E, 0, 0:1], float(P), -1.0, ALU.mult, ALU.add).then_inc(route.sem, 1)
                nc.vector.tensor_copy(ends, psum[0:E, 0, 1:2]).then_inc(route.sem, 1)
                nc.vector.tensor_copy(table[0:1, NT:NT + E], psum[0:1, 0, 2:2 + E]).then_inc(route.sem, 1)
                await_step(dve, route, 0, "end")
                nc.vector.scalar_tensor_tensor(rank, rank, starts, onehot, ALU.add, ALU.mult).then_inc(route.sem, 1)
                nc.vector.tensor_scalar(past, tile_no, ends, None, ALU.is_ge).then_inc(route.sem, 1)
                await_step(dve, route_pe, 0, "experts")
                nc.vector.tensor_scalar(table[0:1, 0:NT], psum[0:1, 0, 40:40 + NT], float(E - 1), None, ALU.min)\
                    .then_inc(route.sem, 1)
                nc.vector.tensor_copy(slot_i[:], psum[:, 0, 16:16 + NCH * TOPK]).then_inc(route.sem, 1)

            def gated_values(b, half):
                await_step(dve, fr_out, b, "s")
                await_step(dve, fv, b, ("a", "v")[half])
                part = slice(half * TC // 2, (half + 1) * TC // 2)
                nc.vector.tensor_tensor(sf[:, part, :], rows4[:, part, :], sf[:, part, :], ALU.mult).then_inc(comb.sem, 1)

            def combine(b):
                await_step(dve, comb, b, "g")
                await_step(dve, keep_xz, b, "xz")
                if not isinstance(b, int) or b > NB:
                    await_step(dve, keep_x2, b - 1, "x2b")
                    await_step(dve, hat3, b - 1, f"h{TC - 1}")
                nc.vector.tensor_tensor(rows_of(b), sf[:], xz[:], ALU.add).then_inc(comb.sem, 1)

            def third_stats(b):
                if isinstance(b, int) and b < NB:
                    await_step(dve, merged, 0, f"q{TC * (b + 1) - 1}")
                else:
                    await_step(dve, comb, b, "x")
                await_step(dve, hat3, b - 1, f"h{TC - 1}")
                norm_stats(rows_of(b), 2, ln3, b, TC)

            def finish(b):
                await_step(dve, sumsq, b, f"s{TC - 1}")
                nc.vector.tensor_scalar(msq[:], ssq[:], 1.0 / D, EPS_RMS, ALU.mult, ALU.add).then_inc(fin.sem, 1)
                await_step(dve, fin_pow, b, "p")
                await_step(dve, res, b - 1, "o")
                if not isinstance(b, int) or b > NB:
                    dve.wait_ge(out_stored, (b - NB) * 16)
                for c in range(TC):
                    nc.vector.scalar_tensor_tensor(fo[:, c, :], rows4[:, c, :], rms[:, c:c + 1], gamma[:],
                                                   ALU.mult, ALU.mult).then_inc(fin.sem, 1)

            def turn(i):
                now, next_, channel, recurs = (has(i, 0, 0, B - 1), has(i, 1, 0, B - 1), has(i, -1, 0, B - 1),
                                               has(i, -2, NB, B - 1))
                if at(i, SPECIAL):
                    experts_norm(0)
                if channel:
                    mix_second(i - 1)
                if at(i, SPECIAL):
                    experts_rows(0)
                if now:
                    weights_of(i)
                if at(i, SPECIAL + 2):
                    finish(NB)
                if recurs:
                    if at(i, B + 1):
                        tile_columns(1, 1)
                    convolve(i - 2)
                if at(i, B - 1):
                    experts_norm(1)
                if at(i, B):
                    experts_rows(1)
                    tile_columns(1, 0)
                if at(i, B + 1):
                    hidden_columns(1, 1)
                    tile_columns(1, 2)
                if at(i, 0):
                    stats_in(1)
                if now:
                    sums(i)
                if next_ and not at(i, 0):
                    stats_in(i + 1)
                if at(i, -1):
                    route_first()
                if at(i, 1):
                    route_second()
                if at(i, SPECIAL):
                    tile_columns(0, 0)
                if now:
                    quotient(i)
                    gated(i)
                if at(i, SPECIAL):
                    experts(0)
                if recurs:
                    scales(i - 2)
                if next_:
                    mix_first(i + 1)
                if at(i, SPECIAL):
                    merge(0, 0)
                    third_stats(0)
                elif channel:
                    gated_values(i - 1, 0)
                if recurs:
                    recur(i - 2)
                if now:
                    residual_mid(i)
                if at(i, SPECIAL):
                    gated_values(i - 1, 0)
                    gated_values(i - 1, 1)
                    combine(i - 1)
                    merge(0, 1)
                    convolve(0)
                    third_stats(1)
                    mix_second(i)
                elif channel:
                    gated_values(i - 1, 1)
                    combine(i - 1)
                if has(i, -1, NB, B - 1) and not at(i, SPECIAL):
                    third_stats(i - 1)
                if at(i, B):
                    hidden_columns(1, 0)
                if recurs:
                    finish(i - 2)

            def catch_up(i):
                weights_of(i)
                scales(0)
                sums(i)
                recur(0)
                convolve(1)
                stats_in(i + 1)
                quotient(i)
                finish(0)
                gated(i)
                third_stats(2)
                mix_first(i + 1)
                scales(1)
                residual_mid(i)
                recur(1)
                gated_values(i - 1, 0)
                gated_values(i - 1, 1)
                convolve(2)
                finish(1)
                scales(2)
                combine(i - 1)
                third_stats(i - 1)
                recur(2)

            def stats_in(b):
                dve.wait_ge(x_loaded, (b + 1) * 16)
                await_step(dve, keep_y, b - 1, "xb")
                norm_stats(x_in, 0, ln1, b, TC)
                await_step(dve, ln1, b, "v0")
                nc.vector.tensor_scalar(varis[0][:, TC:2 * TC], moments[0][:, 0:TC, 1], 1.0 + EPS, EPS * EPS,
                                        ALU.mult, ALU.add).then_inc(ln1.sem, 1)

            def residual_mid(b):
                await_step(dve, proj, b, "o")
                await_step(dve, keep_y, b, "xb")
                nc.vector.tensor_tensor(z[:], fr4, y[:], ALU.add).then_inc(zsum.sem, 1)
                await_step(dve, zsum, b, "z")
                await_step(dve, hat2, b - 1, f"h{TC - 1}")
                norm_stats(z, 1, ln2, b, TC)

            def experts_norm(f):
                if f:
                    await_step(dve, res, 1, "o")
                else:
                    await_step(dve, comb, NB - 1, "x")
                norm_stats(xf, 3, lnf, f, NCH)

            def experts_rows(f):
                if f:
                    await_step(dve, mix2, B - 1, "r1")
                dve.wait_ge(experts_rstd, f + 1)
                for c in range(NCH):
                    nc.vector.tensor_scalar(xfn[f][:, c, :], xf[:, c, :], negmean[3][:, c:c + 1], rstd[3][:, c:c + 1],
                                            ALU.add, ALU.mult).then_inc(experts_hat.sem, 1)

            def tile_columns(f, t):
                base = f * NT
                dve.wait_ge(xs_t, t + (1 + base))
                if f or not isinstance(t, int):
                    dve.wait_ge(up_done, t + base)
                nc.vector.tensor_copy(xst[:].rearrange("p a n -> p (a n)"), psum[:, 0, 0:D]).then_inc(xst_ready, 1)

            def hidden_columns(f, t):
                base = f * NT
                dve.wait_ge(hid_t, t + (1 + base))
                dve.wait_ge(tiles_done, t + (1 + base))
                nc.vector.tensor_copy(tile_cols[f].rearrange("p j n -> p (j n)"), psum[:, 4:6, :].rearrange("p a t -> p (a t)"))\
                    .then_inc(hidt_ready, 1)

            def experts(f):
                base = f * NT
                with dve.Fori(3 if f else 1, NT) as t:
                    tile_columns(f, t)
                    hidden_columns(f, t - 1)
                hidden_columns(f, NT - 1)
                dve.wait_ge(tiles_done, NT + 1 + base)
                if f == 0:
                    nc.vector.memset(xc[:, :, 0:3], 0.0).then_inc(cols_made, 1)

            def merge(f, b):
                for c in range(TC * b, TC * (b + 1)):
                    nc.vector.tensor_tensor(xf[:, c, :], xf[:, c, :], bias[:], ALU.add).then_inc(merged.sem, 1)
                    dve.wait_ge(picks[c], 16 * TOPK * (f + 1))
                    for k, name in enumerate(("b", "p")):
                        await_step(dve, merged, f, f"{name}{c}")
                        nc.vector.scalar_tensor_tensor(xf[:, c, :], picked[:, c, k, :], choice_w[:, c, k:k + 1], xf[:, c, :],
                                                       ALU.mult, ALU.add).then_inc(merged.sem, 1)

            turns(dve, turn, catch_up)
            experts(1)
            for b in range(NB):
                merge(1, b)


def kernel(**inputs):
    import numpy as np
    import concourse.bacc as bacc
    from concourse.bass_utils import run_bass_kernel_spmd

    def given(name):
        return np.asarray(inputs[name])

    a, b = "L0_attn_a_", "L0_attn_b_"
    conv_w = given(b + "conv_w")
    vectors = [given(a + "ln1_w"), given(a + "ln1_b"), given(a + "ln2_w"), given(a + "ln2_b"),
               given(a + "time_decay"), given(a + "time_first"), given(a + "time_mix_k").reshape(-1),
               given(a + "time_mix_v").reshape(-1), given(a + "time_mix_r").reshape(-1),
               given(a + "f_time_mix_k").reshape(-1), given(a + "f_time_mix_r").reshape(-1),
               given(b + "conv_b"), given(b + "b_r"), given(b + "b_i"), given(b + "log_a")]
    vectors += [conv_w[:, 0, j] for j in range(4)]
    packed = np.concatenate([v.reshape(2, 128).T for v in vectors], axis=1)
    arrays = {
        "x": given(a + "x"), "vecs": packed, "bias": given("L0_ffn_bias"), "gamma": given(b + "gamma"),
        "w_key": given(a + "w_key"), "w_value": given(a + "w_value"), "w_recept": given(a + "w_recept"),
        "w_output": given(a + "w_output"), "f_w_key": given(a + "f_w_key"), "f_w_recept": given(a + "f_w_recept"),
        "f_w_value": given(a + "f_w_value"), "w_r_t": given(b + "W_r").T, "w_i_t": given(b + "W_i").T,
        "w_out_t": given(b + "W_out").T, "expert_weights": given("L0_ffn_expert_weights"),
        "expert_indices": given("L0_ffn_expert_indices"), "w1": given("L0_ffn_w1"), "w2": given("L0_ffn_w2"),
    }
    arrays = {name: np.ascontiguousarray(v) for name, v in arrays.items()}
    nc = bacc.Bacc("TRN2", target_bir_lowering=False, num_devices=1)
    args = [nc.dram_tensor("in_" + name, v.shape, mybir.dt.from_np(v.dtype), kind="ExternalInput").ap()
            for name, v in arrays.items()]
    out = nc.dram_tensor("out", (B, T, D), F32, kind="ExternalOutput").ap()
    hybrid_kernel(nc, *args, out)
    r = run_bass_kernel_spmd(nc, [{"in_" + name: v for name, v in arrays.items()}], core_ids=[0])
    return r.results[0]["out"]
```
